# Optimizing a Trainium2 kernel written in Bass

```python
import numpy as np
import jax
import jax.numpy as jnp

def _softmax(x, axis=-1):
    return jax.nn.softmax(x, axis=axis)

def _gelu(x):
    return jax.nn.gelu(x, approximate=True)

def _silu(x):
    return jax.nn.silu(x)

def _sigmoid(x):
    return jax.nn.sigmoid(x)

def _layernorm(x, axis=-1, eps=1e-05):
    m = jnp.mean(x, axis=axis, keepdims=True)
    v = jnp.var(x, axis=axis, keepdims=True)
    return (x - m) / jnp.sqrt(v + eps)

def _scatter_add(tgt, idx, src, axis=0):
    return tgt.at[idx].add(src)

def _segment_sum(src, seg, n):
    return jax.ops.segment_sum(src, seg, n)
kernel_name = 'mk_gps_d1_gnn_r8_c65fff'

def setup_inputs(seed: int=0):
    np.random.seed(seed)
    _w = jnp.asarray

    def _rec_inputs():
        import jax
        import jax.numpy as jnp
        _gk = jax.random.key(seed)
        x = -0.0001126 + 1 * jax.random.normal(jax.random.fold_in(_gk, 1), (1250, 768), jnp.float32)
        src = jax.random.randint(jax.random.fold_in(_gk, 2), (20000,), 0, 1250, jnp.int32)
        dst = jax.random.randint(jax.random.fold_in(_gk, 3), (20000,), 0, 1250, jnp.int32)
        _o = jnp.argsort(dst, stable=True)
        src = src[_o]
        dst = dst[_o]
        edge_weight1 = -0.00472126 + 0.997171 * jax.random.normal(jax.random.fold_in(_gk, 13), (20000, 1), jnp.float32)
        return (x, src, dst, edge_weight1)
    x, src, dst, edge_weight1 = _rec_inputs()

    def _L0_gnn_setup():
        import jax, jax.numpy as jnp
        import numpy as np
        N, E, D, H, C = (1250, 12500, 768, 4, 192)
        NEG_SLOPE = 0.2

        def gat_conv(x, src, dst, W, a_src, a_dst, b):
            h = (x @ W).reshape(N, H, C)
            as_n = (h * a_src).sum(-1)
            ad_n = (h * a_dst).sum(-1)
            e = jax.nn.leaky_relu(as_n[src] + ad_n[dst], NEG_SLOPE)
            m = jax.ops.segment_max(e, dst, num_segments=N)
            p = jnp.exp(e - m[dst])
            s = jax.ops.segment_sum(p, dst, num_segments=N)
            alpha = p / (s[dst] + 1e-16)
            out = jax.ops.segment_sum(alpha[:, :, None] * h[src], dst, num_segments=N)
            return out.reshape(N, H * C) + b
        key = jax.random.key(seed)
        ks = jax.random.split(key, 16)
        w = lambda k, shape: jax.random.normal(k, shape, dtype=jnp.float32) * 0.02
        inp = {}
        inp['x'] = jax.random.normal(ks[0], (N, D), dtype=jnp.float32)
        inp['edge_index'] = jax.random.randint(ks[1], (2, E), 0, N, dtype=jnp.int32)
        inp['batch'] = jnp.zeros((N,), dtype=jnp.int32)
        inp['edge_attr'] = jax.random.normal(ks[2], (E, 1), dtype=jnp.float32)
        inp['W_ah'] = w(ks[3], (D, D))
        inp['b_ah'] = jnp.zeros((D,), jnp.float32)
        for i in range(3):
            inp[f'W{i}'] = w(ks[4 + 3 * i], (D, H * C))
            inp[f'a_src{i}'] = w(ks[5 + 3 * i], (H, C))
            inp[f'a_dst{i}'] = w(ks[6 + 3 * i], (H, C))
            inp[f'b{i}'] = jnp.zeros((H * C,), jnp.float32)
        inp['W_out'] = w(ks[13], (3 * D, D))
        inp['b_out'] = jnp.zeros((D,), jnp.float32)
        return inp
    _L0_gnn_all = _L0_gnn_setup()
    _L0_gnn_in = {k: v for k, v in _L0_gnn_all.items() if k in ('W_ah', 'b_ah', 'W0', 'a_src0', 'a_dst0', 'b0', 'W1', 'a_src1', 'a_dst1', 'b1', 'W2', 'a_src2', 'a_dst2', 'b2', 'W_out', 'b_out')}
    del _L0_gnn_all

    def _L0_mix_setup():
        import jax, jax.numpy as jnp
        import numpy as np
        DIM = 768
        HEADS = 12
        DH = DIM // HEADS
        M = 256
        EPS = 0.0001

        def softmax_kernel(data, proj, is_query):
            data_normalizer = data.shape[-1] ** (-0.25)
            ratio = proj.shape[0] ** (-0.5)
            data_dash = jnp.einsum('bhsd,md->bhsm', data_normalizer * data, proj)
            diag = 0.5 * data_normalizer ** 2 * jnp.sum(data * data, axis=-1, keepdims=True)
            if is_query:
                stab = jnp.max(data_dash, axis=-1, keepdims=True)
            else:
                stab = jnp.max(data_dash, axis=(-2, -1), keepdims=True)
            stab = jax.lax.stop_gradient(stab)
            return ratio * (jnp.exp(data_dash - diag - stab) + EPS)
        key = jax.random.key(seed)
        kx, kq, kk, kv, ko, kp = jax.random.split(key, 6)
        B, S = (8, 512)
        w_scale = DIM ** (-0.5)
        return {'x': jax.random.normal(kx, (B, S, DIM), jnp.float32), 'Wq': jax.random.normal(kq, (DIM, DIM), jnp.float32) * w_scale, 'Wk': jax.random.normal(kk, (DIM, DIM), jnp.float32) * w_scale, 'Wv': jax.random.normal(kv, (DIM, DIM), jnp.float32) * w_scale, 'Wo': jax.random.normal(ko, (DIM, DIM), jnp.float32) * w_scale, 'proj': jax.random.normal(kp, (M, DH), jnp.float32)}
    _L0_mix_all = _L0_mix_setup()
    _L0_mix_in = {k: v for k, v in _L0_mix_all.items() if k in ('Wq', 'Wk', 'Wv', 'Wo', 'proj')}
    del _L0_mix_all

    def _L0_ffn_setup():
        import jax, jax.numpy as jnp
        import numpy as np
        import math
        B, S, D = (8, 1024, 768)
        H, DH = (12, 64)
        DFF = 384
        N_NEURONS, N_BASIS, RANK, K = (96, 32, 64, 8)

        def _ln(x, g, b, eps=1e-05):
            m = x.mean(-1, keepdims=True)
            v = ((x - m) ** 2).mean(-1, keepdims=True)
            return (x - m) * jax.lax.rsqrt(v + eps) * g + b
        key = jax.random.key(seed)
        ks = jax.random.split(key, 20)
        sc = lambda i, shape, s=0.02: jax.random.normal(ks[i], shape, jnp.float32) * s
        return {'x': jax.random.normal(ks[0], (B, S, D), jnp.float32), 'q_w': sc(1, (D, D)), 'q_b': jnp.zeros((D,), jnp.float32), 'k_w': sc(2, (D, D)), 'k_b': jnp.zeros((D,), jnp.float32), 'ao_w': sc(3, (D, D)), 'ao_b': jnp.zeros((D,), jnp.float32), 'recipe': jax.random.normal(ks[4], (N_NEURONS, N_BASIS), jnp.float32) * 0.5, 'ctx_pat': jax.random.normal(ks[5], (N_NEURONS, H), jnp.float32) * 0.5, 'basis_emb': sc(6, (N_BASIS, D), 0.05), 'basis_A': sc(7, (N_BASIS, D, RANK), 0.05), 'vout_w': sc(8, (RANK, D)), 'vout_b': jnp.zeros((D,), jnp.float32), 'up_w': sc(9, (D, DFF)), 'up_b': jnp.zeros((DFF,), jnp.float32), 'down_w': sc(10, (DFF, D)), 'down_b': jnp.zeros((D,), jnp.float32), 'n1_g': jnp.ones((D,), jnp.float32), 'n1_b': jnp.zeros((D,), jnp.float32), 'n2_g': jnp.ones((D,), jnp.float32), 'n2_b': jnp.zeros((D,), jnp.float32)}
    _L0_ffn_all = _L0_ffn_setup()
    _L0_ffn_in = {k: v for k, v in _L0_ffn_all.items() if k in ('q_w', 'q_b', 'k_w', 'k_b', 'ao_w', 'ao_b', 'recipe', 'ctx_pat', 'basis_emb', 'basis_A', 'vout_w', 'vout_b', 'up_w', 'up_b', 'down_w', 'down_b', 'n1_g', 'n1_b', 'n2_g', 'n2_b')}
    del _L0_ffn_all
    return {'x': x, 'src': src, 'dst': dst, 'edge_weight1': edge_weight1, 'L0_gnn_W_ah': _L0_gnn_in['W_ah'], 'L0_gnn_b_ah': _L0_gnn_in['b_ah'], 'L0_gnn_W0': _L0_gnn_in['W0'], 'L0_gnn_a_src0': _L0_gnn_in['a_src0'], 'L0_gnn_a_dst0': _L0_gnn_in['a_dst0'], 'L0_gnn_b0': _L0_gnn_in['b0'], 'L0_gnn_W1': _L0_gnn_in['W1'], 'L0_gnn_a_src1': _L0_gnn_in['a_src1'], 'L0_gnn_a_dst1': _L0_gnn_in['a_dst1'], 'L0_gnn_b1': _L0_gnn_in['b1'], 'L0_gnn_W2': _L0_gnn_in['W2'], 'L0_gnn_a_src2': _L0_gnn_in['a_src2'], 'L0_gnn_a_dst2': _L0_gnn_in['a_dst2'], 'L0_gnn_b2': _L0_gnn_in['b2'], 'L0_gnn_W_out': _L0_gnn_in['W_out'], 'L0_gnn_b_out': _L0_gnn_in['b_out'], 'L0_mix_Wq': _L0_mix_in['Wq'], 'L0_mix_Wk': _L0_mix_in['Wk'], 'L0_mix_Wv': _L0_mix_in['Wv'], 'L0_mix_Wo': _L0_mix_in['Wo'], 'L0_mix_proj': _L0_mix_in['proj'], 'L0_ffn_q_w': _L0_ffn_in['q_w'], 'L0_ffn_q_b': _L0_ffn_in['q_b'], 'L0_ffn_k_w': _L0_ffn_in['k_w'], 'L0_ffn_k_b': _L0_ffn_in['k_b'], 'L0_ffn_ao_w': _L0_ffn_in['ao_w'], 'L0_ffn_ao_b': _L0_ffn_in['ao_b'], 'L0_ffn_recipe': _L0_ffn_in['recipe'], 'L0_ffn_ctx_pat': _L0_ffn_in['ctx_pat'], 'L0_ffn_basis_emb': _L0_ffn_in['basis_emb'], 'L0_ffn_basis_A': _L0_ffn_in['basis_A'], 'L0_ffn_vout_w': _L0_ffn_in['vout_w'], 'L0_ffn_vout_b': _L0_ffn_in['vout_b'], 'L0_ffn_up_w': _L0_ffn_in['up_w'], 'L0_ffn_up_b': _L0_ffn_in['up_b'], 'L0_ffn_down_w': _L0_ffn_in['down_w'], 'L0_ffn_down_b': _L0_ffn_in['down_b'], 'L0_ffn_n1_g': _L0_ffn_in['n1_g'], 'L0_ffn_n1_b': _L0_ffn_in['n1_b'], 'L0_ffn_n2_g': _L0_ffn_in['n2_g'], 'L0_ffn_n2_b': _L0_ffn_in['n2_b']}

def reference(x, src, dst, edge_weight1, L0_gnn_W_ah, L0_gnn_b_ah, L0_gnn_W0, L0_gnn_a_src0, L0_gnn_a_dst0, L0_gnn_b0, L0_gnn_W1, L0_gnn_a_src1, L0_gnn_a_dst1, L0_gnn_b1, L0_gnn_W2, L0_gnn_a_src2, L0_gnn_a_dst2, L0_gnn_b2, L0_gnn_W_out, L0_gnn_b_out, L0_mix_Wq, L0_mix_Wk, L0_mix_Wv, L0_mix_Wo, L0_mix_proj, L0_ffn_q_w, L0_ffn_q_b, L0_ffn_k_w, L0_ffn_k_b, L0_ffn_ao_w, L0_ffn_ao_b, L0_ffn_recipe, L0_ffn_ctx_pat, L0_ffn_basis_emb, L0_ffn_basis_A, L0_ffn_vout_w, L0_ffn_vout_b, L0_ffn_up_w, L0_ffn_up_b, L0_ffn_down_w, L0_ffn_down_b, L0_ffn_n1_g, L0_ffn_n1_b, L0_ffn_n2_g, L0_ffn_n2_b):
    import jax
    import jax.numpy as jnp

    def _L0_gnn_ref(x, edge_index, batch, edge_attr, W_ah, b_ah, W0, a_src0, a_dst0, b0, W1, a_src1, a_dst1, b1, W2, a_src2, a_dst2, b2, W_out, b_out):
        import jax, jax.numpy as jnp
        import numpy as np
        N, E, D, H, C = (1250, 12500, 768, 4, 192)
        NEG_SLOPE = 0.2

        def gat_conv(x, src, dst, W, a_src, a_dst, b):
            h = (x @ W).reshape(N, H, C)
            as_n = (h * a_src).sum(-1)
            ad_n = (h * a_dst).sum(-1)
            e = jax.nn.leaky_relu(as_n[src] + ad_n[dst], NEG_SLOPE)
            m = jax.ops.segment_max(e, dst, num_segments=N)
            p = jnp.exp(e - m[dst])
            s = jax.ops.segment_sum(p, dst, num_segments=N)
            alpha = p / (s[dst] + 1e-16)
            out = jax.ops.segment_sum(alpha[:, :, None] * h[src], dst, num_segments=N)
            return out.reshape(N, H * C) + b
        loops = jnp.arange(N, dtype=edge_index.dtype)
        src = jnp.concatenate([edge_index[0], loops])
        dst = jnp.concatenate([edge_index[1], loops])
        x1 = jax.nn.relu(x @ W_ah + b_ah)
        xs = [jax.nn.relu(gat_conv(x1, src, dst, W, a_s, a_d, b)) for W, a_s, a_d, b in ((W0, a_src0, a_dst0, b0), (W1, a_src1, a_dst1, b1), (W2, a_src2, a_dst2, b2))]
        node_emb = jnp.concatenate(xs, axis=1)
        return jax.nn.relu(node_emb @ W_out + b_out)

    def _L0_mix_ref(x, Wq, Wk, Wv, Wo, proj):
        import jax, jax.numpy as jnp
        import numpy as np
        DIM = 768
        HEADS = 12
        DH = DIM // HEADS
        M = 256
        EPS = 0.0001

        def softmax_kernel(data, proj, is_query):
            data_normalizer = data.shape[-1] ** (-0.25)
            ratio = proj.shape[0] ** (-0.5)
            data_dash = jnp.einsum('bhsd,md->bhsm', data_normalizer * data, proj)
            diag = 0.5 * data_normalizer ** 2 * jnp.sum(data * data, axis=-1, keepdims=True)
            if is_query:
                stab = jnp.max(data_dash, axis=-1, keepdims=True)
            else:
                stab = jnp.max(data_dash, axis=(-2, -1), keepdims=True)
            stab = jax.lax.stop_gradient(stab)
            return ratio * (jnp.exp(data_dash - diag - stab) + EPS)
        B, S, _ = x.shape

        def split_heads(t):
            return t.reshape(B, S, HEADS, DH).transpose(0, 2, 1, 3)
        q = split_heads(x @ Wq)
        k = split_heads(x @ Wk)
        v = split_heads(x @ Wv)
        qp = softmax_kernel(q, proj, is_query=True)
        kp = softmax_kernel(k, proj, is_query=False)
        k_sum = jnp.sum(kp, axis=2)
        d_inv = 1.0 / jnp.einsum('bhsm,bhm->bhs', qp, k_sum)
        ctx = jnp.einsum('bhsm,bhsd->bhmd', kp, v)
        out = jnp.einsum('bhsm,bhmd,bhs->bhsd', qp, ctx, d_inv)
        out = out.transpose(0, 2, 1, 3).reshape(B, S, DIM)
        return out @ Wo

    def _L0_ffn_ref(x, q_w, q_b, k_w, k_b, ao_w, ao_b, recipe, ctx_pat, basis_emb, basis_A, vout_w, vout_b, up_w, up_b, down_w, down_b, n1_g, n1_b, n2_g, n2_b):
        import jax, jax.numpy as jnp
        import numpy as np
        import math
        B, S, D = (8, 1024, 768)
        H, DH = (12, 64)
        DFF = 384
        N_NEURONS, N_BASIS, RANK, K = (96, 32, 64, 8)

        def _ln(x, g, b, eps=1e-05):
            m = x.mean(-1, keepdims=True)
            v = ((x - m) ** 2).mean(-1, keepdims=True)
            return (x - m) * jax.lax.rsqrt(v + eps) * g + b
        b, s, d = x.shape
        normed = _ln(x, n1_g, n1_b)
        Q = (normed @ q_w + q_b).reshape(b, s, H, DH).transpose(0, 2, 1, 3)
        Kt = (normed @ k_w + k_b).reshape(b, s, H, DH).transpose(0, 2, 1, 3)
        attn = jax.nn.softmax(jnp.einsum('bhsd,bhtd->bhst', Q, Kt) / math.sqrt(DH), axis=-1)
        recipe_norm = jax.nn.softmax(recipe, axis=-1)
        neuron_emb = recipe_norm @ basis_emb
        semantic = normed @ neuron_emb.T
        attn_summary = attn.mean(-1).transpose(0, 2, 1)
        context = attn_summary @ ctx_pat.T
        final = semantic * jax.nn.sigmoid(context)
        topk_scores, neuron_idx = jax.lax.top_k(final, K)
        w = jax.nn.softmax(topk_scores, axis=-1)
        sel = recipe_norm[neuron_idx]
        token_recipe = (sel * w[..., None]).sum(2)
        proj = jnp.einsum('bsd,ndr->bsnr', normed, basis_A)
        v_sem = jnp.einsum('bsn,bsnr->bsr', token_recipe, proj)
        V = (v_sem @ vout_w + vout_b).reshape(b, s, H, DH).transpose(0, 2, 1, 3)
        attn_out = jnp.einsum('bhst,bhtd->bhsd', attn, V).transpose(0, 2, 1, 3).reshape(b, s, d)
        x = x + (attn_out @ ao_w + ao_b)
        normed2 = _ln(x, n2_g, n2_b)
        ffn = jax.nn.gelu(normed2 @ up_w + up_b, approximate=False) @ down_w + down_b
        return x + ffn
    edge_index = jnp.stack([src, dst])
    batch0 = jnp.zeros((1250,), jnp.int32)
    xn = _layernorm(x, axis=-1)
    x = x + _L0_gnn_ref(xn, edge_index, batch0, edge_weight1, L0_gnn_W_ah, L0_gnn_b_ah, L0_gnn_W0, L0_gnn_a_src0, L0_gnn_a_dst0, L0_gnn_b0, L0_gnn_W1, L0_gnn_a_src1, L0_gnn_a_dst1, L0_gnn_b1, L0_gnn_W2, L0_gnn_a_src2, L0_gnn_a_dst2, L0_gnn_b2, L0_gnn_W_out, L0_gnn_b_out) + _L0_mix_ref(xn[None], L0_mix_Wq, L0_mix_Wk, L0_mix_Wv, L0_mix_Wo, L0_mix_proj)[0]
    x = x + _L0_ffn_ref(_layernorm(x, axis=-1)[None], L0_ffn_q_w, L0_ffn_q_b, L0_ffn_k_w, L0_ffn_k_b, L0_ffn_ao_w, L0_ffn_ao_b, L0_ffn_recipe, L0_ffn_ctx_pat, L0_ffn_basis_emb, L0_ffn_basis_A, L0_ffn_vout_w, L0_ffn_vout_b, L0_ffn_up_w, L0_ffn_up_b, L0_ffn_down_w, L0_ffn_down_b, L0_ffn_n1_g, L0_ffn_n1_b, L0_ffn_n2_g, L0_ffn_n2_b)[0]
    return x

_drawn_inputs = setup_inputs


def setup_inputs(seed=0):
    import zlib

    import numpy as np

    out = dict(_drawn_inputs(seed))
    spreads = {'L0_gnn_b_ah': (0.0, 0.658),
     'L0_gnn_b0': (0.0, 0.32),
     'L0_gnn_b1': (0.0, 0.341),
     'L0_gnn_b2': (0.0, 0.331),
     'L0_gnn_b_out': (0.0, 0.1),
     'L0_ffn_q_b': (0.0, 0.8),
     'L0_ffn_k_b': (0.0, 2.0),
     'L0_ffn_ao_b': (0.0, 0.8),
     'L0_ffn_vout_b': (0.0, 1.439),
     'L0_ffn_up_b': (0.0, 2.0),
     'L0_ffn_down_b': (0.0, 0.8),
     'L0_ffn_n1_g': (1.0, 0.6),
     'L0_ffn_n1_b': (0.0, 0.8),
     'L0_ffn_n2_g': (1.0, 0.6),
     'L0_ffn_n2_b': (0.0, 2.0)}
    factors = {'L0_gnn_W_ah': 2.899,
     'L0_gnn_a_src0': 8.0,
     'L0_gnn_a_dst0': 8.0,
     'L0_gnn_a_src1': 8.0,
     'L0_gnn_a_dst1': 8.0,
     'L0_gnn_a_src2': 8.0,
     'L0_gnn_a_dst2': 8.0,
     'L0_mix_Wq': 8.0,
     'L0_mix_Wk': 8.0,
     'L0_mix_proj': 8.0,
     'L0_ffn_q_w': 8.0,
     'L0_ffn_k_w': 8.0,
     'L0_ffn_recipe': 8.0,
     'L0_ffn_ctx_pat': 8.0,
     'L0_ffn_basis_emb': 8.0,
     'L0_ffn_basis_A': 8.0,
     'L0_ffn_vout_w': 8.0}
    for name, (base, spread) in spreads.items():
        noise = np.random.default_rng([zlib.crc32(name.encode()), seed]).standard_normal(out[name].shape)
        drawn = base * np.exp(spread * noise) if base else spread * noise
        out[name] = jnp.asarray(drawn.astype(out[name].dtype))
    for name, factor in factors.items():
        out[name] = (out[name] * factor).astype(out[name].dtype)
    return out
```

```python
from contextlib import ExitStack

import concourse.bass as bass
from concourse import mybir

F32 = mybir.dt.float32
I32 = mybir.dt.int32
U32 = mybir.dt.uint32
BF16 = mybir.dt.bfloat16
ALU = mybir.AluOpType
ACT = mybir.ActivationFunctionType
AX = mybir.AxisListType

N, D = 1250, 768
T, NT = 125, 10
KT = D // 128
HALF = D // 2
E = 20000
EB = E // T
EG = EB // 4
GH, GC, GL = 4, 192, 3
GI = GL * GH
MH, DH = 12, 64
MP = MH // 2
M = 256
NB, RANK, NN = 32, 64, 96
FF = 384
FJ = FF // 128
LN_EPS = 1e-5
MIX_EPS = 1e-4
NEG = -1e30
CHUNKS = [(0, 512), (512, 512), (1024, 226)]
CELLS = N * N


class Tally:

    def __init__(self, eng, sem):
        self.eng, self.sem, self.n, self.i, self.per, self.start = eng, sem, 0, None, 0, 0

    def mark(self, ins):
        ins.then_inc(self.sem, 1)
        self.n += 1

    def settle(self):
        self.eng.wait_ge(self.sem, self.n if self.i is None else self.i * self.per + self.n)

    def step(self, ins):
        self.mark(ins)
        self.settle()

    def enter(self, i, per):
        self.i, self.per, self.start = i, per, self.n

    def leave(self, times):
        assert self.n - self.start == self.per, (self.n - self.start, self.per)
        self.n, self.i = self.start + self.per * times, None


class Env:
    pass


def weight_view(w):
    return w.rearrange("(k p) n -> p k n", p=128)


def node_view(x):
    return x.rearrange("(t p) d -> p t d", p=T)


def norm_stats(v, tally, src, stats, mv, veps):
    for t in range(NT):
        for c in range(2):
            tally.mark(v.bn_stats(stats[:, t, 6 * c:6 * c + 6], src[:, t, c * HALF:(c + 1) * HALF]))
    tally.settle()
    for t in range(NT):
        tally.mark(v.bn_aggr(mv[:, t, :], stats[:, t, :]))
    tally.settle()
    return v.tensor_scalar(veps[:, :], mv[:, :, 1], LN_EPS, None, ALU.add)


def newton_rstd(v, tally, rstd, std, veps, tmp):
    tally.step(v.reciprocal(rstd, std))
    tally.step(v.tensor_tensor(tmp, rstd, rstd, ALU.mult))
    tally.step(v.tensor_tensor(tmp, tmp, veps, ALU.mult))
    tally.step(v.tensor_scalar(tmp, tmp, -0.5, 1.5, ALU.mult, ALU.add))
    tally.step(v.tensor_tensor(rstd, rstd, tmp, ALU.mult))


def front(nc, g):
    with ExitStack() as ctx:
        sb = lambda n, s, d=F32: ctx.enter_context(nc.sbuf_tensor(n, s, d))
        ps = lambda n, s: ctx.enter_context(nc.psum_tensor(n, s, F32))
        sem = g.sem
        x = sb("fr_x", [T, NT, D])
        wv = sb("fr_wv", [128, KT, D])
        stage = sb("fr_stage", [128, 2, KT, T])
        stats, mv = sb("fr_stats", [T, NT, 12]), sb("fr_mv", [T, NT, 2])
        veps, std, rstd = (sb(f"fr_{n}", [T, NT]) for n in ("veps", "std", "rstd"))
        tmp = sb("fr_tmp", [T, NT])
        zeros = sb("fr_zeros", [T, 2 * N])
        srci, dsti = sb("fr_src", [T, EB], I32), sb("fr_dst", [T, EB], I32)
        key, tot = sb("fr_key", [T, EB + 4]), sb("fr_tot", [T, EB])
        xn = sb("fr_xn", [T, 2, D])
        ones = sb("fr_ones", [T, T])
        before = sb("fr_before", [T, T])
        spare = sb("fr_spare", [T, 1])
        sparei = sb("fr_sparei", [T, 1], I32)
        diag = sb("fr_diag", [T, 2, 4, T])
        junk = sb("fr_junk", [T, 2, 4, T])
        first, idxf = sb("fr_first", [T, EB]), sb("fr_idxf", [T, EB])
        tr = ps("fr_tr", [128, 2, 2, 512])
        vps = ps("fr_vps", [128, 2, 512])
        kps = ps("fr_kps", [128, 2, 512])
        x_in, e_in, wv_in = sem("fr_x_in"), sem("fr_e_in"), sem("fr_wv_in")
        zeroed, setup, spare_ok = sem("fr_zeroed"), sem("fr_setup"), sem("fr_spare_ok")
        dve, pool = sem("fr_dve"), sem("fr_pool")
        var_ok, std_ok, xn_ok = sem("fr_var"), sem("fr_std"), sem("fr_xn_ok")
        tr_ok, st_ok, xnT_ok, v_ok, v_out = (sem(f"fr_{n}") for n in ("tr_ok", "st_ok", "xnT_ok", "v_ok", "v_out"))
        diag_ok, row_ok, row_used = sem("fr_diag_ok"), sem("fr_row_ok"), sem("fr_row_used")

        with nc.Block() as block:
            @block.sync
            def _(sp):
                sp.dma_start(x[:], node_view(g.x)).then_inc(x_in, 16)
                sp.dma_start(srci[:], g.src.rearrange("(p b) -> p b", p=T)).then_inc(e_in, 16)
                sp.dma_start(dsti[:], g.dst.rearrange("(p b) -> p b", p=T)).then_inc(e_in, 16)
                sp.dma_start(wv[:], weight_view(g.mix_Wv)).then_inc(wv_in, 16)
                sp.wait_ge(zeroed, 1)
                cells = g.table[0:CELLS].rearrange("(q p r) o -> q p (r o)", p=T, r=2 * N)
                for q in range(NT // 2):
                    sp.dma_start(cells[q], zeros[:]).then_inc(g.table_sem, 16)
                sp.dma_start(g.table[CELLS:CELLS + T], zeros[:, 0:1]).then_inc(g.table_sem, 16)
                sp.wait_ge(g.table_sem, g.TABLE_ZERO)

            @block.gpsimd
            def _(e):
                seq = Tally(e, pool)
                seq.step(e.memset(g.ident[:], 0.0))
                seq.step(e.affine_select(out=g.ident[:], in_=g.ident[:], compare_op=ALU.not_equal, fill=1.0,
                                         base=0, pattern=[[-1, 128]], channel_multiplier=1))
                e.memset(zeros[:], 0.0).then_inc(zeroed, 1)
                e.memset(ones[:], 1.0).then_inc(setup, 1)
                seq.step(e.memset(before[:], float(1 + 2 * T)))
                e.affine_select(out=before[:], in_=before[:], compare_op=ALU.is_gt, fill=1.0,
                                base=0, pattern=[[-1, T]], channel_multiplier=1).then_inc(setup, 1)
                e.memset(g.v[:], 1.0).then_inc(setup, 1)
                e.iota(sparei[:], pattern=[[0, 1]], base=CELLS, channel_multiplier=1).then_inc(spare_ok, 1)
                with e.Fori(0, NT // 2) as i:
                    for par in range(2):
                        e.wait_ge(st_ok, i * 2 + par + 1)
                        e.tensor_copy(g.xnT[:, :, bass.ds((i * 2 + par) * T, T)], stage[:, par]).then_inc(xnT_ok, 1)

            @block.vector
            def _(e):
                seq = Tally(e, dve)
                e.wait_ge(x_in, 16)
                norm_stats(e, seq, x, stats, mv, veps).then_inc(var_ok, 1)
                e.wait_ge(e_in, 32)
                seq.mark(e.memset(key[:, EB:EB + 4], 0.0))
                seq.mark(e.scalar_tensor_tensor(out=key[:, 0:EB], in0=srci[:], scalar=float(N), in1=dsti[:],
                                                op0=ALU.mult, op1=ALU.add))
                e.wait_ge(std_ok, 1)
                newton_rstd(e, seq, rstd[:], std[:], veps[:], tmp[:])
                e.wait_ge(setup, 2)

                def spread(n, slot):
                    e.tensor_tensor(diag[:, slot], g.ident[0:T, 0:T].unsqueeze(1).to_broadcast([T, 4, T]),
                                    key[:, bass.ds(n * 4, 4)].unsqueeze(2).to_broadcast([T, 4, T]),
                                    ALU.mult).then_inc(diag_ok, 1)

                spread(0, 0)
                with e.Fori(0, NT // 2) as i:
                    for par in range(2):
                        n = i * 2 + par
                        e.wait_ge(tr_ok, n)
                        e.tensor_scalar(xn[:, par], x[:, n, :], mv[:, n, 0:1], rstd[:, bass.ds(n, 1)],
                                        ALU.subtract, ALU.mult).then_inc(xn_ok, 1)
                        for q in range(4):
                            grp = n * 4 + q
                            e.wait_ge(row_ok, grp)
                            spread(grp + 1, (q + 1) % 2)
                            e.wait_ge(row_ok, grp + 1)
                            e.wait_ge(row_used, grp)
                            for j in range(4):
                                ins = e.scalar_tensor_tensor(
                                    out=junk[:, q % 2, j], in0=kps[0:T, q % 2, j * T:(j + 1) * T],
                                    scalar=key[:, bass.ds(grp * 4 + j, 1)], in1=before[:], op0=ALU.is_equal,
                                    op1=ALU.mult, accum_out=tot[:, bass.ds(grp * 4 + j, 1)])
                            ins.then_inc(row_used, 1)
                e.wait_ge(row_used, EG + 1)
                e.wait_ge(spare_ok, 1)
                seq.mark(e.tensor_copy(spare[:], sparei[:]))
                seq.step(e.tensor_scalar(first[:], tot[:], float(2 * T), None, ALU.is_lt))
                seq.mark(e.tensor_tensor(g.edge_add[:], tot[:], first[:], ALU.mult))
                seq.step(e.scalar_tensor_tensor(out=idxf[:], in0=key[:, 0:EB], scalar=spare[:], in1=first[:],
                                                op0=ALU.subtract, op1=ALU.mult))
                seq.step(e.tensor_scalar(g.edge_cell[:], idxf[:], spare[:], None, ALU.add))

            @block.scalar
            def _(e):
                e.wait_ge(var_ok, 1)
                e.activation(std[:], veps[:], ACT.Sqrt).then_inc(std_ok, 1)
                e.wait_ge(setup, 3)
                with e.Fori(0, NT // 2) as i:
                    for par in range(2):
                        n = i * 2 + par
                        e.wait_ge(tr_ok, n + 1)
                        e.wait_ge(xnT_ok, n)
                        e.activation(stage[:, par].rearrange("p (c k) t -> p c (k t)", c=2),
                                     tr[:, par, :, 0:3 * T], ACT.Copy).then_inc(st_ok, 1)
                        e.wait_ge(v_ok, n + 1)
                        e.activation(g.v[:, n, :].rearrange("p (c h d) -> p c h d", c=2, h=MP)[:, :, :, 0:DH],
                                     vps[0:T, :, 0:HALF].rearrange("p c (h d) -> p c h d", h=MP),
                                     ACT.Copy).then_inc(v_out, 1)

            @block.tensor
            def _(e):
                e.wait_ge(setup, 3)
                e.wait_ge(wv_in, 16)
                e.sem_inc(row_used, 1)
                with e.Fori(0, NT // 2) as i:
                    for par in range(2):
                        n = i * 2 + par
                        e.wait_ge(xn_ok, n + 1)
                        for k in range(KT):
                            ins = e.transpose(tr[:, par, k // 3, (k % 3) * T:(k % 3 + 1) * T],
                                              xn[:, par, k * 128:(k + 1) * 128], g.ident[0:T, 0:T])
                        ins.then_inc(tr_ok, 1)
                        for q in range(4):
                            grp = n * 4 + q
                            e.wait_ge(diag_ok, grp + 1)
                            e.wait_ge(row_used, grp)
                            e.matmul(kps[0:T, q % 2, 0:4 * T], ones[:], diag[:, q % 2].rearrange("p j f -> p (j f)"),
                                     start=True, stop=True).then_inc(row_ok, 1)
                        e.wait_ge(st_ok, n + 1)
                        e.wait_ge(v_out, n)
                        for c in range(2):
                            for k in range(KT):
                                ins = e.matmul(vps[0:T, c, 0:HALF], stage[:, par, k], wv[:, k, c * HALF:(c + 1) * HALF],
                                               start=(k == 0), stop=(k == KT - 1))
                        ins.then_inc(v_ok, 1)


def scatter_counts(e, g, blocks):
    for b in blocks:
        if b > 0:
            e.wait_ge(g.scattered, 16 * b)
        e.indirect_dma_start(out=g.table, out_offset=bass.IndirectOffsetOnAxis(
            ap=g.edge_cell[:, b:b + 1].bitcast(U32), axis=0), in_=g.edge_add[:, b:b + 1], in_offset=None,
            compute_op=ALU.add, bounds_check=CELLS + T - 1).then_inc(g.scattered, 16)
    e.wait_ge(g.scattered, 16 * (blocks[-1] + 1))


def mix(nc, g, blocks):
    NORM = DH ** -0.25
    RATIO = M ** -0.5
    W2 = 2 * (DH + 1)
    with ExitStack() as ctx:
        sb = lambda n, s, d=F32: ctx.enter_context(nc.sbuf_tensor("mx_" + n, s, d))
        ps = lambda n, s: ctx.enter_context(nc.psum_tensor("mx_" + n, s, F32))
        sem = lambda n: g.sem("mx_" + n)
        wk, wq = sb("wk", [128, KT, 128]), sb("wq", [128, KT, 128])
        wo = sb("wo", [128, KT, D])
        proj2 = sb("proj2", [128, 2, 2, DH])
        feat = sb("feat", [128, 2 * M])
        halves = sb("halves", [128, 128])
        ones2 = sb("ones2", [2, T])
        kT, qT, sq = sb("kT", [128, N]), sb("qT", [128, N]), sb("sq", [128, N])
        dk, dq = sb("dk", [T, NT, 2]), sb("dq", [T, NT, 2])
        kf = sb("kf", [T, NT, 2 * M])
        kmax, gmax, gdiag, kbias = sb("kmax", [T, 2]), sb("gmax", [2, 1]), sb("gdiag", [2, 2]), sb("kbias", [T, NT, 2])
        cx = sb("cx", [128, 2, 2 * W2])
        qm, nb, rc = sb("qm", [T, 2, 2]), sb("nb", [T, 2, 2]), sb("rc", [T, 2, 2])
        qf = sb("qf", [T, 3, 2 * M])
        qfT = sb("qfT", [128, 2, 4, T])
        mo = sb("mo", [T, NT, D])
        stage = sb("stage", [128, 2, KT, T])
        res = sb("res", [T, 2, D])
        LQ, DD, TT, CO = ps("LQ", [128, 3 * 512]), ps("DD", [128, 2, 512]), ps("TT", [128, 2, 512]), ps("CO", [128, 512])
        wk_in, wq_in, wo_in, pr_in = sem("wk_in"), sem("wq_in"), sem("wo_in"), sem("pr_in")
        pset, ptr, pdone = sem("pset"), sem("ptr"), sem("pdone")
        klin, qlin, lin_out = sem("klin"), sem("qlin"), sem("lin_out")
        kdg, qdg, d_out = sem("kdg"), sem("qdg"), sem("d_out")
        kdd, kf_ok, kmax_ok, kmT, gd_ok, kmB, kb_ok = (sem(n) for n in ("kdd", "kf_ok", "kmax_ok", "kmT", "gd_ok", "kmB", "kb_ok"))
        ke_ok, kp_ok, cx_ok, cx_out = sem("ke_ok"), sem("kp_ok"), sem("cx_ok"), sem("cx_out")
        qdd, nb_ok, qe_ok, qp_ok, qtr, qfT_ok, out_ok, mo_ok = (
            sem(n) for n in ("qdd", "nb_ok", "qe_ok", "qp_ok", "qtr", "qfT_ok", "out_ok", "mo_ok"))
        otr, ost, omm, ores = (sem(n) for n in ("otr", "ost", "omm", "ores"))
        sent = [sem("sent0"), sem("sent1")]
        dve = sem("dve")
        tile = lambda t: slice(t * T, (t + 1) * T)

        with nc.Block() as block:
            @block.sync
            def _(sp):
                for c in range(2):
                    for d in range(2):
                        sp.dma_start(proj2[:, c, d], g.mix_proj[c * 128:(c + 1) * 128, :]).then_inc(pr_in, 16)
                for w, dram, into, used in ((wk, g.mix_Wk, wk_in, None), (wq, g.mix_Wq, wq_in, None)):
                    sp.dma_start(w[:], weight_view(dram)[:, :, 0:128]).then_inc(into, 16)
                sp.dma_start(wo[:], weight_view(g.mix_Wo)).then_inc(wo_in, 16)
                with sp.Fori(1, MP) as m:
                    sp.wait_ge(klin, m)
                    sp.dma_start(wk[:], weight_view(g.mix_Wk)[:, :, bass.ds(m * 128, 128)]).then_inc(wk_in, 16)
                    sp.wait_ge(qlin, m)
                    sp.dma_start(wq[:], weight_view(g.mix_Wq)[:, :, bass.ds(m * 128, 128)]).then_inc(wq_in, 16)
                for t in range(NT):
                    sp.wait_ge(ores, t + 1)
                    sp.dma_start(g.mix_out[tile(t), :], res[:, t % 2]).then_inc(sent[t % 2], 16)
                for s in sent:
                    sp.wait_ge(s, 16 * NT // 2)

            @block.gpsimd
            def _(e):
                e.memset(feat[:], 0.0).then_inc(pset, 1)
                e.memset(ones2[:], 1.0).then_inc(pset, 1)
                e.memset(halves[:], 0.0).then_inc(pset, 1)
                e.wait_ge(pset, 3)
                e.memset(halves[0:DH, 0:DH], 0.5).then_inc(pset, 1)
                e.memset(halves[DH:128, DH:128], 0.5).then_inc(pset, 1)
                e.wait_ge(pset, 5)
                scatter_counts(e, g, blocks)

            @block.tensor
            def _(e):
                e.wait_ge(pr_in, 64)
                for c in range(2):
                    ins = e.transpose(CO[:, c * 128:(c + 1) * 128], proj2[:, c].rearrange("p a b -> p (a b)"), g.ident[:])
                ins.then_inc(ptr, 1)
                e.wait_ge(pdone, 2)
                e.wait_ge(pset, 5)

                def linear(w):
                    for a, n in CHUNKS:
                        for k in range(KT):
                            ins = e.matmul(LQ[:, a:a + n], w[:, k], g.xnT[:, k, a:a + n], start=(k == 0), stop=(k == KT - 1))
                    return ins

                def norms(j, bank):
                    for c in range(2):
                        ins = e.matmul(DD[0:T, bank, c * 128:(c + 1) * 128], sq[:, tile(2 * j + c)], halves[:],
                                       start=True, stop=True)
                    return ins

                with e.Fori(0, MP) as m:
                    e.wait_ge(wk_in, m * 16 + 16)
                    e.wait_ge(lin_out, m * 2)
                    linear(wk).then_inc(klin, 1)
                    e.wait_ge(lin_out, m * 2 + 1)
                    for j in range(5):
                        e.wait_ge(qe_ok, m * NT) if j < 2 else e.wait_ge(d_out, m * 10 + j - 1)
                        norms(j, j % 2).then_inc(kdg, 1)
                    for t in range(NT):
                        e.wait_ge(d_out, m * 10 + 4 + t) if t < 2 else e.wait_ge(kf_ok, m * NT + t - 1)
                        e.matmul(DD[0:T, (t + 1) % 2, :], kT[:, tile(t)], feat[:], start=True, stop=True).then_inc(kdd, 1)
                    e.wait_ge(wq_in, m * 16 + 16)
                    linear(wq).then_inc(qlin, 1)
                    e.wait_ge(kmax_ok, m + 1)
                    e.wait_ge(mo_ok, m * NT)
                    e.transpose(CO[0:2, 0:T], kmax[:], g.ident[0:T, 0:T]).then_inc(kmT, 1)
                    e.wait_ge(gd_ok, m + 1)
                    e.matmul(CO[0:T, 0:2], ones2[:], gdiag[:], start=True, stop=True).then_inc(kmB, 1)
                    e.wait_ge(lin_out, m * 2 + 2)
                    for j in range(5):
                        e.wait_ge(kf_ok, m * NT + 9 + j) if j < 2 else e.wait_ge(d_out, m * 10 + 5 + j - 1)
                        norms(j, (j + 1) % 2).then_inc(qdg, 1)
                    for h in range(2):
                        e.wait_ge(qfT_ok, m * NT)
                        for c in range(2):
                            for t in range(NT):
                                if h == 0 and c == 0 and t % 5 == 0:
                                    e.wait_ge(kp_ok, m * 2 + t // 5 + 1)
                                ins = e.matmul(TT[:, h, c * W2:(c + 1) * W2], kf[:, t, h * M + c * 128:h * M + (c + 1) * 128],
                                               g.v[:, t, bass.ds(m * W2, W2)], start=(t == 0), stop=(t == NT - 1))
                        ins.then_inc(cx_ok, 1)
                    for s in range(NT + 3):
                        if s < NT:
                            e.wait_ge(d_out, m * 10 + 9 + s) if s < 2 else e.wait_ge(qe_ok, m * NT + s - 1)
                            e.matmul(DD[0:T, s % 2, :], qT[:, tile(s)], feat[:], start=True, stop=True).then_inc(qdd, 1)
                        t = s - 2
                        if 0 <= t < NT:
                            e.wait_ge(qp_ok, m * NT + t + 1)
                            e.wait_ge(cx_out, m * 2 + 2) if t < 2 else e.wait_ge(qfT_ok, m * NT + t - 1)
                            for c in range(4):
                                ins = e.transpose(TT[:, t % 2, c * T:(c + 1) * T], qf[:, t % 3, c * 128:(c + 1) * 128],
                                                  g.ident[0:T, 0:T])
                            ins.then_inc(qtr, 1)
                        t = s - 3
                        if t >= 0:
                            e.wait_ge(qfT_ok, m * NT + t + 1)
                            e.wait_ge(mo_ok, m * NT + t)
                            for h in range(2):
                                for c in range(2):
                                    ins = e.matmul(CO[0:T, h * W2:(h + 1) * W2], qfT[:, t % 2, 2 * h + c],
                                                   cx[:, h, c * W2:(c + 1) * W2], start=(c == 0), stop=(c == 1))
                            ins.then_inc(out_ok, 1)
                e.wait_ge(wo_in, 16)
                e.wait_ge(mo_ok, MP * NT)
                e.wait_ge(qfT_ok, MP * NT)
                for t in range(NT + 1):
                    if t < NT:
                        e.wait_ge(ost, t)
                        for k in range(KT):
                            ins = e.transpose(LQ[:, k // 3 * 512 + k % 3 * T:k // 3 * 512 + (k % 3 + 1) * T],
                                              mo[:, t, k * 128:(k + 1) * 128], g.ident[0:T, 0:T])
                        ins.then_inc(otr, 1)
                    if t > 0:
                        u = t - 1
                        bank = (DD, TT)[u % 2]
                        e.wait_ge(ost, u + 1)
                        if u >= 2:
                            e.wait_ge(ores, u - 1)
                        for c in range(2):
                            for k in range(KT):
                                ins = e.matmul(bank[0:T, c, 0:HALF], stage[:, u % 2, k], wo[:, k, c * HALF:(c + 1) * HALF],
                                               start=(k == 0), stop=(k == KT - 1))
                        ins.then_inc(omm, 1)

            @block.scalar
            def _(e):
                with e.Fori(0, MP) as m:
                    for which, ready, dst in ((0, klin, kT), (1, qlin, qT)):
                        e.wait_ge(ready, m + 1)
                        e.activation(dst[:], LQ[:, 0:N], ACT.Copy, scale=NORM)
                        e.activation(sq[:], LQ[:, 0:N], ACT.Square, scale=NORM).then_inc(lin_out, 1)
                        if which == 0:
                            for t in range(NT):
                                e.wait_ge(kdd, m * NT + t + 1)
                                e.activation(kf[:, t], DD[0:T, (t + 1) % 2, :], ACT.Copy).then_inc(kf_ok, 1)
                    e.wait_ge(kb_ok, m + 1)
                    for t in range(NT):
                        for h in range(2):
                            ins = e.activation(kf[:, t, h * M:(h + 1) * M], kf[:, t, h * M:(h + 1) * M], ACT.Exp,
                                               bias=kbias[:, t, h:h + 1])
                        if t % 5 == 4:
                            ins.then_inc(ke_ok, 1)
                    for s in range(NT + 2):
                        if s < NT:
                            e.wait_ge(nb_ok, m * NT + s + 1)
                            e.wait_ge(qtr, m * NT + max(s - 2, 0))
                            for h in range(2):
                                ins = e.activation(qf[:, s % 3, h * M:(h + 1) * M], DD[0:T, s % 2, h * M:(h + 1) * M],
                                                   ACT.Exp, bias=nb[:, s % 2, h:h + 1])
                            ins.then_inc(qe_ok, 1)
                        t = s - 2
                        if t >= 0:
                            e.wait_ge(qtr, m * NT + t + 1)
                            e.wait_ge(out_ok, m * NT + max(t - 1, 0))
                            e.activation(qfT[:, t % 2].rearrange("p c t -> p (c t)"), TT[:, t % 2, 0:4 * T],
                                         ACT.Copy).then_inc(qfT_ok, 1)
                for t in range(NT):
                    e.wait_ge(otr, t + 1)
                    if t >= 2:
                        e.wait_ge(omm, t - 1)
                    e.activation(stage[:, t % 2].rearrange("p (c k) t -> p c (k t)", c=2),
                                 LQ[:, 0:1024].rearrange("p (c n) -> p c n", c=2)[:, :, 0:3 * T], ACT.Copy).then_inc(ost, 1)

            @block.vector
            def _(e):
                seq = Tally(e, dve)
                e.wait_ge(ptr, 1)
                e.wait_ge(pset, 5)
                for d in range(2):
                    e.tensor_copy(feat[d * DH:(d + 1) * DH, d * M:(d + 1) * M],
                                  CO[d * DH:(d + 1) * DH, 0:M]).then_inc(pdone, 1)
                diag_of = lambda bank: DD[0:T, bank, 0:256].rearrange("p (t h r) -> p t h r", t=2, h=2)[:, :, :, 0]
                with e.Fori(0, MP) as m:
                    seq.enter(m, 1 + 2 * NT)
                    for j in range(5):
                        e.wait_ge(kdg, m * 5 + j + 1)
                        e.tensor_copy(dk[:, 2 * j:2 * j + 2, :], diag_of(j % 2)).then_inc(d_out, 1)
                    e.wait_ge(kf_ok, m * NT + NT)
                    e.tensor_reduce(kmax[:], kf[:].rearrange("p t (h m) -> p h t m", h=2), AX.XY, ALU.max).then_inc(kmax_ok, 1)
                    e.wait_ge(kmT, m + 1)
                    seq.step(e.tensor_reduce(gmax[:], CO[0:2, 0:T], AX.X, ALU.max))
                    e.tensor_scalar(gdiag[:], g.ident[0:2, 0:2], gmax[:, 0:1], None, ALU.mult).then_inc(gd_ok, 1)
                    e.wait_ge(kmB, m + 1)
                    e.wait_ge(d_out, m * 10 + 5)
                    e.scalar_tensor_tensor(out=kbias[:], in0=dk[:], scalar=-1.0,
                                           in1=CO[0:T, 0:2].unsqueeze(1).to_broadcast([T, NT, 2]),
                                           op0=ALU.mult, op1=ALU.subtract).then_inc(kb_ok, 1)
                    for j in range(5):
                        e.wait_ge(qdg, m * 5 + j + 1)
                        e.tensor_copy(dq[:, 2 * j:2 * j + 2, :], diag_of((j + 1) % 2)).then_inc(d_out, 1)
                    for c in range(2):
                        e.wait_ge(ke_ok, m * 2 + c + 1)
                        e.tensor_scalar(kf[:, 5 * c:5 * c + 5], kf[:, 5 * c:5 * c + 5], MIX_EPS, RATIO,
                                        ALU.add, ALU.mult).then_inc(kp_ok, 1)
                    for h in range(2):
                        e.wait_ge(cx_ok, m * 2 + h + 1)
                        e.tensor_copy(cx[:, h], TT[:, h, 0:2 * W2]).then_inc(cx_out, 1)
                    e.wait_ge(d_out, m * 10 + 10)
                    for s in range(NT + 3):
                        if s < NT:
                            e.wait_ge(qdd, m * NT + s + 1)
                            seq.step(e.tensor_reduce(qm[:, s % 2], DD[0:T, s % 2, :].rearrange("p (h m) -> p h m", h=2),
                                                     AX.X, ALU.max))
                            e.scalar_tensor_tensor(out=nb[:, s % 2], in0=qm[:, s % 2], scalar=-1.0, in1=dq[:, s],
                                                   op0=ALU.mult, op1=ALU.subtract).then_inc(nb_ok, 1)
                        t = s - 1
                        if 0 <= t < NT:
                            e.wait_ge(qe_ok, m * NT + t + 1)
                            e.tensor_scalar(qf[:, t % 3], qf[:, t % 3], MIX_EPS, RATIO, ALU.add, ALU.mult).then_inc(qp_ok, 1)
                        t = s - 3
                        if t >= 0:
                            e.wait_ge(out_ok, m * NT + t + 1)
                            heads = CO[0:T, 0:2 * 3 * (DH + 1)].rearrange("p (h c) -> p h c", h=2)
                            seq.step(e.reciprocal(rc[:, t % 2], heads[:, :, DH]))
                            e.tensor_tensor(mo[:, t, bass.ds(m * 128, 128)].rearrange("p (h c) -> p h c", h=2),
                                            heads[:, :, 0:DH], rc[:, t % 2].unsqueeze(2).to_broadcast([T, 2, DH]),
                                            ALU.mult).then_inc(mo_ok, 1)
                    seq.leave(MP)
                for t in range(NT):
                    e.wait_ge(omm, t + 1)
                    if t >= 2:
                        e.wait_ge(sent[t % 2], 16 * (t // 2))
                    e.tensor_copy(res[:, t % 2].rearrange("p (c n) -> p c n", c=2),
                                  (DD, TT)[t % 2][0:T, :, 0:HALF]).then_inc(ores, 1)


def lift(nc, g):
    with ExitStack() as ctx:
        sb = lambda n, s, d=F32: ctx.enter_context(nc.sbuf_tensor("li_" + n, s, d))
        ps = lambda n, s: ctx.enter_context(nc.psum_tensor("li_" + n, s, F32))
        sem = lambda n: g.sem("li_" + n)
        tile = lambda t: slice(t * T, (t + 1) * T)
        wa = sb("wa", [128, 2, KT, 128])
        bah = sb("bah", [128, KT])
        x1T = sb("x1T", [128, KT, N])
        w = sb("w", [128, 2, KT, D])
        arow = sb("arow", [128, 2, D])
        prod = sb("prod", [128, KT // 2, D])
        watt = sb("watt", [128, KT, 2 * GI])
        rows = sb("rows", [2 * GI, N])
        cnt = sb("cnt", [T, 2, N])
        maskT = sb("maskT", [T, NT, N], BF16)
        srow = sb("srow", [T, 2, N])
        junk = sb("junk", [T, N])
        top, topd = sb("top", [T, 2, NT]), sb("topd", [T, NT, GI])
        m1, m2, uv = sb("m1", [T, NT, GI]), sb("m2", [T, NT, GI]), sb("uv", [T, NT, 2 * GI])
        xs = sb("xs", [128, 2, KT, T])
        ho = sb("ho", [T, 2, D])
        A, B, C = ps("A", [128, 3 * 512]), ps("B", [128, 3 * 512]), ps("C", [128, 2, 512])
        wa_in = [sem("wa_in0"), sem("wa_in1")]
        w_in = [sem("w_in0"), sem("w_in1")]
        ar_in = [sem("ar_in0"), sem("ar_in1")]
        cnt_in = [sem("cnt_in0"), sem("cnt_in1")]
        srow_in = [sem("srow_in0"), sem("srow_in1")]
        ho_sent = [sem("ho_sent0"), sem("ho_sent1")]
        b_in, rows_sent, uv_sent = sem("b_in"), sem("rows_sent"), sem("uv_sent")
        x1_mm, x1_ok, watt_ok, rows_mm, rows_ok = (sem(n) for n in ("x1_mm", "x1_ok", "watt_ok", "rows_mm", "rows_ok"))
        loop_ok, mt_mm, mt_ok, col_mm, col_ok = (sem(n) for n in ("loop_ok", "mt_mm", "mt_ok", "col_mm", "col_ok"))
        seg_ok, uv_ok, uvt_mm, uvt_ok = (sem(n) for n in ("seg_ok", "uv_ok", "uvt_mm", "uvt_ok"))
        xs_ok, h_mm, h_out, dve = (sem(n) for n in ("xs_ok", "h_mm", "h_out", "dve"))
        ORDER = (2, 1, 0)
        W = (g.gnn_W0, g.gnn_W1, g.gnn_W2)
        AV = ((g.gnn_a_src0, g.gnn_a_src1, g.gnn_a_src2), (g.gnn_a_dst0, g.gnn_a_dst1, g.gnn_a_dst2))

        with nc.Block() as block:
            @block.sync
            def _(sp):
                sp.dma_start(bah[:], g.gnn_b_ah.rearrange("(k p) -> p k", p=128), allow_slow_non_contiguous=True).then_inc(b_in, 16)
                for p in range(2):
                    sp.dma_start(wa[:, p], weight_view(g.gnn_W_ah)[:, :, p * 128:(p + 1) * 128]).then_inc(wa_in[p], 16)
                for i in range(2):
                    sp.dma_start(w[:, i], weight_view(W[i])).then_inc(w_in[i], 16)
                for i in range(GL):
                    for c in range(2):
                        if i > 0:
                            sp.wait_ge(watt_ok, 4 * i + 2 * c - 2)
                        sp.dma_start(arow[:, c], AV[c][i].rearrange("h c -> (h c)").partition_broadcast(128)).then_inc(ar_in[c], 16)
                    if i == 1:
                        sp.wait_ge(watt_ok, 4)
                        sp.dma_start(w[:, 0], weight_view(W[2])).then_inc(w_in[0], 16)
                for k in range(2, KT):
                    sp.wait_ge(x1_mm, k - 1)
                    sp.dma_start(wa[:, k % 2], weight_view(g.gnn_W_ah)[:, :, k * 128:(k + 1) * 128]).then_inc(wa_in[k % 2], 16)
                for s in range(NT):
                    if s >= 2:
                        sp.wait_ge(mt_mm, s - 1)
                    sp.dma_start(cnt[:, s % 2], g.table[s * T * N:(s + 1) * T * N].rearrange("(p n) o -> p (n o)", p=T)
                                 ).then_inc(cnt_in[s % 2], 16)
                sp.wait_ge(rows_ok, 1)
                sp.dma_start(g.rows, rows[:]).then_inc(rows_sent, 16)
                sp.wait_ge(rows_sent, 16)
                with sp.Fori(0, GI // 2) as i:
                    for p in range(2):
                        sp.wait_ge(seg_ok, i * 2 + p)
                        sp.dma_start(srow[:, p], g.rows[bass.ds(i * 2 + p, 1), :].rearrange("a n -> (a n)").partition_broadcast(T)
                                     ).then_inc(srow_in[p], 16)
                sp.wait_ge(uvt_ok, 1)
                sp.dma_start(g.uv, rows[:]).then_inc(uv_sent, 16)
                sp.wait_ge(uv_sent, 16)

            @block.gpsimd
            def _(e):
                e.wait_ge(x1_ok, KT)
                for l in range(GL):
                    with e.Fori(0, NT // 2) as i:
                        for p in range(2):
                            e.wait_ge(h_mm, i * 2 + (p + l * NT))
                            e.tensor_copy(xs[:, p], x1T[:, :, bass.ds((i * 2 + p) * T, T)]).then_inc(xs_ok, 1)

            @block.tensor
            def _(e):
                for k in range(KT):
                    e.wait_ge(wa_in[k % 2], 16 * (k // 2 + 1))
                    if k >= 2:
                        e.wait_ge(x1_ok, k - 1)
                    bank = (A, B)[k % 2]
                    for a, n in CHUNKS:
                        for kk in range(KT):
                            ins = e.matmul(bank[:, a:a + n], wa[:, k % 2, kk], g.xnT[:, kk, a:a + n],
                                           start=(kk == 0), stop=(kk == KT - 1))
                    ins.then_inc(x1_mm, 1)
                e.wait_ge(watt_ok, 4 * GL)
                e.wait_ge(x1_ok, KT)
                for a, n in CHUNKS:
                    for k in range(KT):
                        ins = e.matmul(A[0:2 * GI, a:a + n], watt[:, k], x1T[:, k, a:a + n], start=(k == 0), stop=(k == KT - 1))
                ins.then_inc(rows_mm, 1)
                for s in range(NT):
                    bank = (B, A)[s % 2]
                    e.wait_ge(loop_ok, s + 1)
                    if s == 1:
                        e.wait_ge(rows_ok, 1)
                    if s >= 2:
                        e.wait_ge(mt_ok, s - 1)
                    for d in range(NT):
                        ins = e.transpose(bank[0:T, d // 4 * 512 + d % 4 * T:d // 4 * 512 + (d % 4 + 1) * T],
                                          cnt[:, s % 2, tile(d)], g.ident[0:T, 0:T])
                    ins.then_inc(mt_mm, 1)
                for t in range(NT):
                    ins = e.transpose(C[0:T, 0, t * 2 * GI:(t + 1) * 2 * GI], rows[:, tile(t)], g.ident[0:2 * GI, 0:2 * GI])
                ins.then_inc(col_mm, 1)
                e.wait_ge(mt_ok, NT)
                e.sem_inc(h_mm, 1)
                for l, layer in enumerate(ORDER):
                    e.wait_ge(w_in[l % 2], 48 if l == 2 else (32, 16)[l])
                    with e.Fori(0, NT // 2) as i:
                        for p in range(2):
                            n = i * 2 + (p + l * NT)
                            bank = (A, B)[p]
                            e.wait_ge(xs_ok, n + 1)
                            e.wait_ge(h_out, n)
                            for c in range(2):
                                for k in range(KT):
                                    ins = e.matmul(bank[0:T, c * 512:c * 512 + HALF], xs[:, p, k],
                                                   w[:, (0, 1, 0)[l], k, c * HALF:(c + 1) * HALF],
                                                   start=(k == 0), stop=(k == KT - 1))
                            ins.then_inc(h_mm, 1)
                e.wait_ge(uv_ok, 1)
                e.wait_ge(h_out, GL * NT + 1)
                for t in range(NT):
                    ins = e.transpose(A[0:2 * GI, t // 4 * 512 + t % 4 * T:t // 4 * 512 + (t % 4 + 1) * T], uv[:, t],
                                      g.ident[0:T, 0:T])
                ins.then_inc(uvt_mm, 1)

            @block.scalar
            def _(e):
                e.wait_ge(b_in, 16)
                for k in range(KT):
                    e.wait_ge(x1_mm, k + 1)
                    e.activation(x1T[:, k], (A, B)[k % 2][:, 0:N], ACT.Relu, bias=bah[:, k:k + 1]).then_inc(x1_ok, 1)
                e.wait_ge(rows_mm, 1)
                e.activation(rows[:], A[0:2 * GI, 0:N], ACT.Copy).then_inc(rows_ok, 1)
                e.sem_inc(h_out, 1)
                for l, layer in enumerate(ORDER):
                    with e.Fori(0, NT // 2) as i:
                        for p in range(2):
                            n = i * 2 + (p + l * NT)
                            e.wait_ge(h_mm, n + 2)
                            e.wait_ge(ho_sent[p], i * 16 + l * 16 * NT // 2)
                            e.activation(ho[:, p].rearrange("p (c n) -> p c n", c=2),
                                         (A, B)[p][0:T, 0:1024].rearrange("p (c n) -> p c n", c=2)[:, :, 0:HALF],
                                         ACT.Copy).then_inc(h_out, 1)
                            e.wait_ge(h_out, n + 2)
                            e.dma_start(g.h[layer * GH:(layer + 1) * GH, bass.ds((i * 2 + p) * T, T), :].rearrange("h p c -> p h c"),
                                        ho[:, p].rearrange("p (h c) -> p h c", h=GH)).then_inc(ho_sent[p], 16)
                    if l == 0:
                        e.wait_ge(h_mm, NT + 1)
                        e.dma_start(w[:, 0], weight_view(W[0])).then_inc(w_in[0], 16)
                for s in ho_sent:
                    e.wait_ge(s, 16 * GL * NT // 2)
                e.wait_ge(uvt_mm, 1)
                for b, (t0, t1) in enumerate(((0, 4), (4, 8), (8, 10))):
                    ins = e.activation(rows[:, t0 * T:t1 * T], A[0:2 * GI, b * 512:b * 512 + (t1 - t0) * T], ACT.Copy)
                ins.then_inc(uvt_ok, 1)

            @block.vector
            def _(e):
                seq = Tally(e, dve)
                for i in range(GL):
                    e.wait_ge(w_in[i % 2], 32 if i == 2 else 16)
                    for c in range(2):
                        e.wait_ge(ar_in[c], 16 * (i + 1))
                        for hf in range(2):
                            ks = slice(hf * KT // 2, (hf + 1) * KT // 2)
                            seq.step(e.tensor_tensor(prod[:], w[:, i % 2, ks], arow[:, c].unsqueeze(1).to_broadcast([128, KT // 2, D]),
                                                     ALU.mult))
                            ins = e.tensor_reduce(watt[:, ks, c * GI + i * GH:c * GI + (i + 1) * GH],
                                                  prod[:].rearrange("p k (h c) -> p k h c", h=GH), AX.X, ALU.add)
                            ins.then_inc(watt_ok, 1)
                            e.wait_ge(watt_ok, 4 * i + 2 * c + hf + 1)
                for s in range(NT + 1):
                    if s < NT:
                        e.wait_ge(cnt_in[s % 2], 16 * (s // 2 + 1))
                        e.tensor_tensor(cnt[:, s % 2, tile(s)], cnt[:, s % 2, tile(s)], g.ident[0:T, 0:T], ALU.add).then_inc(loop_ok, 1)
                    if s > 0:
                        bank = (B, A)[(s - 1) % 2]
                        e.wait_ge(mt_mm, s)
                        for b, (d0, d1) in enumerate(((0, 4), (4, 8), (8, 10))):
                            ins = e.tensor_scalar(maskT[:, d0:d1, tile(s - 1)],
                                                  bank[0:T, b * 512:b * 512 + (d1 - d0) * T].rearrange("p (d s) -> p d s", s=T),
                                                  0.0, NEG, ALU.is_equal, ALU.mult)
                        ins.then_inc(mt_ok, 1)
                e.wait_ge(col_mm, 1)
                seq.step(e.tensor_copy(g.asad[:].rearrange("p t c -> p (t c)"), C[0:T, 0, 0:NT * 2 * GI]))
                e.wait_ge(mt_ok, NT)
                e.sem_inc(seg_ok, 1)
                for i in range(GI):
                    e.wait_ge(srow_in[i % 2], 16 * (i // 2 + 1))
                    for d in range(NT):
                        seq.step(e.tensor_tensor_reduce(junk[:], srow[:, i % 2], maskT[:, d], 1.0, NEG, ALU.add, ALU.max,
                                                        top[:, i % 2, d:d + 1]))
                    e.tensor_copy(topd[:, :, i:i + 1], top[:, i % 2].unsqueeze(2)).then_inc(seg_ok, 1)
                e.wait_ge(seg_ok, GI + 1)
                s_term, d_term = g.asad[:, :, 0:GI], g.asad[:, :, GI:2 * GI]
                seq.mark(e.tensor_scalar(g.as02[:], s_term, 0.2, None, ALU.mult))
                seq.step(e.tensor_tensor(m1[:], topd[:], d_term, ALU.add))
                seq.step(e.tensor_scalar(m2[:], m1[:], 0.2, None, ALU.mult))
                seq.step(e.tensor_tensor(m1[:], m1[:], m2[:], ALU.max))
                seq.mark(e.tensor_tensor(uv[:, :, 0:GI], d_term, m1[:], ALU.subtract))
                seq.settle()
                e.scalar_tensor_tensor(out=uv[:, :, GI:2 * GI], in0=d_term, scalar=0.2, in1=m1[:], op0=ALU.mult,
                                       op1=ALU.subtract).then_inc(uv_ok, 1)


def graph(nc, g):
    RING = 4
    HC = GC + 1
    with ExitStack() as ctx:
        sb = lambda n, s, d=F32: ctx.enter_context(nc.sbuf_tensor("gr_" + n, s, d))
        ps = lambda n, s: ctx.enter_context(nc.psum_tensor("gr_" + n, s, F32))
        sem = lambda n: g.sem("gr_" + n)
        tile = lambda t: slice(t * T, (t + 1) * T)
        cnt = sb("cnt", [T, NT, N])
        ub, vb = sb("ub", [T, 2, N]), sb("vb", [T, 2, N])
        h = sb("h", [T, 2, NT, HC])
        ring = sb("ring", [T, RING, N])
        bias = sb("bias", [T, GI * GC])
        node = sb("node", [T, 2, NT, GC])
        den, rec = sb("den", [T, 2, NT]), sb("rec", [T, 2, NT])
        acc = ps("acc", [128, 5, 512])
        cnt_in, b_in = sem("cnt_in"), sem("b_in")
        uv_in = [sem("uv_in0"), sem("uv_in1")]
        h_in = [sem("h_in0"), sem("h_in1")]
        sent = [sem("sent0"), sem("sent1")]
        ones_ok, loop_ok = sem("ones_ok"), sem("loop_ok")
        a_ok, t_ok, e_ok, p_ok, mm, acc_out, node_ok, dve = (
            sem(n) for n in ("a_ok", "t_ok", "e_ok", "p_ok", "mm", "acc_out", "node_ok", "dve"))

        with nc.Block() as block:
            @block.sync
            def _(sp):
                def fetch(n, p):
                    sp.dma_start(ub[:, p], g.uv[bass.ds(n, 1), :].rearrange("a n -> (a n)").partition_broadcast(T)).then_inc(uv_in[p], 16)
                    sp.dma_start(vb[:, p], g.uv[bass.ds(n + GI, 1), :].rearrange("a n -> (a n)").partition_broadcast(T)).then_inc(uv_in[p], 16)
                    sp.dma_start(h[:, p, :, 0:GC], g.h[bass.ds(n, 1)].rearrange("a (t p) c -> p (a t) c", p=T)).then_inc(h_in[p], 16)

                fetch(0, 0)
                sp.dma_start(cnt[:], g.table[0:CELLS].rearrange("(t p n) o -> p t (n o)", p=T, n=N)).then_inc(cnt_in, 16)
                for i, b in enumerate((g.gnn_b0, g.gnn_b1, g.gnn_b2)):
                    sp.dma_start(bias[:, i * D:(i + 1) * D], b.partition_broadcast(T)).then_inc(b_in, 16)
                fetch(1, 1)
                with sp.Fori(0, GI // 2 - 1) as i:
                    for p in range(2):
                        sp.wait_ge(mm, (i * 2 + (p + 1)) * NT)
                        fetch(i * 2 + p + 2, p)

            @block.gpsimd
            def _(e):
                e.memset(h[:, :, :, GC:HC], 1.0).then_inc(ones_ok, 1)
                nodes = g.node.rearrange("(t p) (i c) -> p t i c", p=T, c=GC)
                with e.Fori(0, GI // 2) as i:
                    for p in range(2):
                        e.wait_ge(node_ok, i * 2 + p + 1)
                        e.dma_start(nodes[:, :, bass.ds(i * 2 + p, 1), :].rearrange("p t i c -> p t (i c)"), node[:, p]).then_inc(sent[p], 16)
                for s in sent:
                    e.wait_ge(s, 16 * GI // 2)

            @block.scalar
            def _(e):
                with e.Fori(0, GI // 2) as i:
                    for j in range(2 * NT + 2):
                        if j < 2 * NT:
                            p, s = j // NT, j % NT
                            if s == 0:
                                e.wait_ge(uv_in[p], i * 32 + 32)
                            e.wait_ge(mm, i * 2 * NT + max(j - RING + 1, 0))
                            e.activation(ring[:, j % RING], ub[:, p], ACT.Identity,
                                         bias=g.asad[:, s, bass.ds(i * 2 + p, 1)]).then_inc(a_ok, 1)
                        k = j - 1
                        if 0 <= k < 2 * NT:
                            e.wait_ge(t_ok, i * 2 * NT + k + 1)
                            e.activation(ring[:, k % RING], ring[:, k % RING], ACT.Exp).then_inc(e_ok, 1)
                        if j == NT + 1 or j == 2 * NT + 1:
                            p = j // NT - 1
                            e.wait_ge(acc_out, (i * 2 + p + 1) * 5)
                            e.activation(node[:, p], node[:, p], ACT.Relu).then_inc(node_ok, 1)

            @block.vector
            def _(e):
                seq = Tally(e, dve)
                e.wait_ge(cnt_in, 16)
                for s in range(NT):
                    e.tensor_tensor(cnt[:, s, tile(s)], cnt[:, s, tile(s)], g.ident[0:T, 0:T], ALU.add).then_inc(loop_ok, 1)
                e.wait_ge(loop_ok, NT)
                e.wait_ge(b_in, 48)
                with e.Fori(0, GI // 2) as i:
                    seq.enter(i, 2 * 10)
                    for j in range(2 * NT + 1):
                        if j < 2 * NT:
                            p, s = j // NT, j % NT
                            e.wait_ge(a_ok, i * 2 * NT + j + 1)
                            e.scalar_tensor_tensor(out=ring[:, j % RING], in0=vb[:, p], scalar=g.as02[:, s, bass.ds(i * 2 + p, 1)],
                                                   in1=ring[:, j % RING], op0=ALU.add, op1=ALU.max).then_inc(t_ok, 1)
                        k = j - 1
                        if k >= 0:
                            e.wait_ge(e_ok, i * 2 * NT + k + 1)
                            e.scalar_tensor_tensor(out=ring[:, k % RING], in0=ring[:, k % RING], scalar=1.0, in1=cnt[:, k % NT],
                                                   op0=ALU.min, op1=ALU.mult).then_inc(p_ok, 1)
                        if j == NT or j == 2 * NT:
                            p = j // NT - 1
                            e.wait_ge(mm, i * 2 * NT + j)
                            e.wait_ge(sent[p], i * 16)
                            for b in range(5):
                                two = acc[0:T, b].rearrange("p (d c) -> p d c", d=2)
                                seq.step(e.tensor_scalar(den[:, p, 2 * b:2 * b + 2], two[:, :, GC], 1e-16, None, ALU.add))
                                seq.step(e.reciprocal(rec[:, p, 2 * b:2 * b + 2], den[:, p, 2 * b:2 * b + 2]))
                                for d in range(2):
                                    ins = e.scalar_tensor_tensor(
                                        out=node[:, p, 2 * b + d], in0=two[:, d, 0:GC], scalar=rec[:, p, 2 * b + d:2 * b + d + 1],
                                        in1=bias[:, bass.ds((i * 2 + p) * GC, GC)], op0=ALU.mult, op1=ALU.add)
                                ins.then_inc(acc_out, 1)
                    seq.leave(GI // 2)

            @block.tensor
            def _(e):
                e.wait_ge(ones_ok, 1)
                with e.Fori(0, GI // 2) as i:
                    for j in range(2 * NT):
                        p, s = j // NT, j % NT
                        e.wait_ge(p_ok, i * 2 * NT + j + 1)
                        if s == 0:
                            e.wait_ge(h_in[p], i * 16 + 16)
                        for d in range(NT):
                            if s == 0 and d == 0:
                                e.wait_ge(acc_out, (i * 2 + p) * 5)
                            ins = e.matmul(acc[0:T, d // 2, d % 2 * 256:d % 2 * 256 + HC], ring[:, j % RING, tile(d)],
                                           h[:, p, s], start=(s == 0 and d % 2 == 0), stop=(s == NT - 1 and d % 2 == 1),
                                           skip_group_check=True)
                        ins.then_inc(mm, 1)


def join(nc, g):
    KO = GL * KT
    with ExitStack() as ctx:
        sb = lambda n, s, d=F32: ctx.enter_context(nc.sbuf_tensor("jo_" + n, s, d))
        ps = lambda n, s: ctx.enter_context(nc.psum_tensor("jo_" + n, s, F32))
        sem = lambda n: g.sem("jo_" + n)
        w = sb("w", [128, KO, D])
        node = sb("node", [T, 2, GL * D])
        xt, mt = sb("xt", [T, 2, D]), sb("mt", [T, 2, D])
        bias = sb("bias", [T, D])
        stage = sb("stage", [128, 2, KO, T])
        tmp = sb("tmp", [T, 2, D])
        TR, O = ps("TR", [128, 2, 2, 512]), ps("O", [128, 2, 2, 512])
        w_in, b_in = sem("w_in"), sem("b_in")
        in_, sent = [sem("in0"), sem("in1")], [sem("sent0"), sem("sent1")]
        tr_mm, st_ok, mm, xm_ok, pre_ok, x_ok = (sem(n) for n in ("tr_mm", "st_ok", "mm", "xm_ok", "pre_ok", "x_ok"))

        with nc.Block() as block:
            @block.sync
            def _(sp):
                def fetch(n, p):
                    rows = bass.ds(n * T, T)
                    sp.dma_start(node[:, p], g.node[rows, :]).then_inc(in_[p], 16)
                    sp.dma_start(xt[:, p], g.x[rows, :]).then_inc(in_[p], 16)
                    sp.dma_start(mt[:, p], g.mix_out[rows, :]).then_inc(in_[p], 16)

                fetch(0, 0)
                for c in range(3):
                    sp.dma_start(w[:, c * KT:(c + 1) * KT], weight_view(g.gnn_W_out)[:, c * KT:(c + 1) * KT]).then_inc(w_in, 16)
                sp.dma_start(bias[:], g.gnn_b_out.partition_broadcast(T)).then_inc(b_in, 16)
                fetch(1, 1)
                with sp.Fori(0, NT // 2 - 1) as i:
                    for p in range(2):
                        sp.wait_ge(x_ok, i * 2 + p + 1)
                        sp.dma_start(g.xj[bass.ds((i * 2 + p) * T, T), :], g.y[:, i * 2 + p, :]).then_inc(sent[p], 16)
                        fetch(i * 2 + p + 2, p)
                for n in range(NT - 2, NT):
                    sp.wait_ge(x_ok, n + 1)
                    sp.dma_start(g.xj[n * T:(n + 1) * T, :], g.y[:, n]).then_inc(sent[n % 2], 16)
                for s in sent:
                    sp.wait_ge(s, 16 * NT // 2)

            @block.tensor
            def _(e):
                e.wait_ge(w_in, 48)
                with e.Fori(0, NT // 2) as i:
                    for p in range(2):
                        e.wait_ge(in_[p], i * 48 + 48)
                        for c in range(3):
                            u = 3 * p + c
                            e.wait_ge(st_ok, i * 6 + max(u - 1, 0))
                            for k in range(KT):
                                kk = c * KT + k
                                ins = e.transpose(TR[:, u % 2, k // 3, k % 3 * T:(k % 3 + 1) * T],
                                                  node[:, p, kk * 128:(kk + 1) * 128], g.ident[0:T, 0:T])
                            ins.then_inc(tr_mm, 1)
                        e.wait_ge(pre_ok, i * 2)
                        for hf in range(2):
                            for k in range(KO):
                                if hf == 0 and k % KT == 0:
                                    e.wait_ge(st_ok, i * 6 + 3 * p + k // KT + 1)
                                ins = e.matmul(O[0:T, p, hf, 0:HALF], stage[:, p, k], w[:, k, hf * HALF:(hf + 1) * HALF],
                                               start=(k == 0), stop=(k == KO - 1))
                        ins.then_inc(mm, 1)

            @block.scalar
            def _(e):
                with e.Fori(0, NT // 2) as i:
                    for p in range(2):
                        for c in range(3):
                            u = 3 * p + c
                            e.wait_ge(tr_mm, i * 6 + u + 1)
                            e.wait_ge(mm, i * 2)
                            e.activation(stage[:, p, c * KT:(c + 1) * KT].rearrange("p (b k) t -> p b (k t)", b=2),
                                         TR[:, u % 2, :, 0:3 * T], ACT.Copy).then_inc(st_ok, 1)

            @block.vector
            def _(e):
                e.wait_ge(b_in, 16)
                with e.Fori(0, NT // 2) as i:
                    for p in range(2):
                        n = i * 2 + p
                        e.wait_ge(in_[p], i * 48 + 48)
                        e.tensor_tensor(xt[:, p], xt[:, p], mt[:, p], ALU.add).then_inc(xm_ok, 1)
                        e.wait_ge(mm, n + 1)
                        e.wait_ge(x_ok, n)
                        e.tensor_tensor(tmp[:, p].rearrange("p (c n) -> p c n", c=2), O[0:T, p, :, 0:HALF],
                                        bias[:].rearrange("p (c n) -> p c n", c=2), ALU.add).then_inc(pre_ok, 1)
                        e.wait_ge(pre_ok, n + 1)
                        e.wait_ge(xm_ok, n + 1)
                        e.scalar_tensor_tensor(out=g.y[:, n, :], in0=tmp[:, p], scalar=0.0, in1=xt[:, p],
                                               op0=ALU.max, op1=ALU.add).then_inc(x_ok, 1)


def route(nc, g):
    NG = 4
    NPB = NB // NG
    with ExitStack() as ctx:
        sb = lambda n, s, d=F32: ctx.enter_context(nc.sbuf_tensor("ro_" + n, s, d))
        ps = lambda n, s: ctx.enter_context(nc.psum_tensor("ro_" + n, s, F32))
        sem = lambda n: g.sem("ro_" + n)
        stats, mv, mv2 = sb("stats", [T, NT, 12]), sb("mv", [T, NT, 2]), sb("mv2", [T, NT, 2])
        veps, std, rstd, tmp = (sb(n, [T, NT]) for n in ("veps", "std", "rstd", "tmp"))
        gain, shift = sb("gain", [128, KT]), sb("shift", [128, KT])
        recipe, rmax, rsum, rrec = sb("recipe", [NN, NB]), sb("rmax", [NN, 1]), sb("rsum", [NN, 1]), sb("rrec", [NN, 1])
        pat, gate, gated = sb("pat", [NN, MH]), sb("gate", [NN, 1]), sb("gated", [NN, NN])
        ones = sb("ones", [NN, T])
        gateB = sb("gateB", [T, NN])
        bemb = sb("bemb", [NB, D])
        recT = sb("recT", [NB, NN])
        nemb = sb("nemb", [128, KT, NN])
        basis = sb("basis", [128, KT, NB, RANK])
        vw, vb = sb("vw", [RANK, D]), sb("vb", [T, D])
        z = sb("z", [T, 2, D])
        stage = sb("stage", [128, 2, KT, T])
        fin, rep, ex, sel = (sb(n, [T, NN]) for n in ("fin", "rep", "ex", "sel"))
        top, ntop, ssum, srec = sb("top", [T, 8]), sb("ntop", [T, 1]), sb("ssum", [T, 1]), sb("srec", [T, 1])
        selT = sb("selT", [NN, T])
        mixw = sb("mixw", [T, NB])
        pw = sb("pw", [T, NB, RANK])
        vs = sb("vs", [T, 128])
        vsT = sb("vsT", [RANK, T])
        TR, PR, S1, S2 = ps("TR", [128, 2, 512]), ps("PR", [128, NG, 512]), ps("S1", [128, 512]), ps("S2", [128, 512])
        gs_in, small_in, bas_in, vw_in = sem("gs_in"), sem("small_in"), sem("bas_in"), sem("vw_in")
        var_ok, std_ok, ones_ok, dve, act = sem("var_ok"), sem("std_ok"), sem("ones_ok"), sem("dve"), sem("act")
        rmax_ok, rexp_ok, rec_ok, pat_ok, pexp_ok, gd_ok = (sem(n) for n in ("rmax_ok", "rexp_ok", "rec_ok", "pat_ok", "pexp_ok", "gd_ok"))
        recT_mm, recT_ok, nemb_mm, gateB_mm, setup = (sem(n) for n in ("recT_mm", "recT_ok", "nemb_mm", "gateB_mm", "setup"))
        z_ok, tr_mm, st_ok, nT_ok, sem_mm, pr_mm = (sem(n) for n in ("z_ok", "tr_mm", "st_ok", "nT_ok", "sem_mm", "pr_mm"))
        fin_ok = sem("fin_ok")
        top_ok, ex_ok, sel_ok, selT_mm, selT_ok, mixw_mm, mixw_ok, pw_ok, vs_ok, vsT_mm, vsT_ok, v_mm, v_ok = (
            sem(n) for n in ("top_ok", "ex_ok", "sel_ok", "selT_mm", "selT_ok", "mixw_mm", "mixw_ok", "pw_ok", "vs_ok", "vsT_mm",
                             "vsT_ok", "v_mm", "v_ok"))

        with nc.Block() as block:
            @block.sync
            def _(sp):
                sp.dma_start(recipe[:], g.ffn_recipe).then_inc(small_in, 16)
                sp.dma_start(pat[:], g.ffn_ctx_pat).then_inc(small_in, 16)
                sp.dma_start(bemb[:], g.ffn_basis_emb).then_inc(small_in, 16)
                for dst, v in ((gain, g.ffn_n1_g), (shift, g.ffn_n1_b)):
                    sp.dma_start(dst[:], v.rearrange("(k p) -> p k", p=128), allow_slow_non_contiguous=True).then_inc(gs_in, 16)
                for k in range(KT):
                    sp.dma_start(basis[:, k], g.ffn_basis_A[:, k * 128:(k + 1) * 128, :].rearrange("n p r -> p n r")).then_inc(bas_in, 16)
                sp.dma_start(vw[:], g.ffn_vout_w).then_inc(vw_in, 16)
                sp.dma_start(vb[:], g.ffn_vout_b.partition_broadcast(T)).then_inc(vw_in, 16)

            @block.gpsimd
            def _(e):
                e.memset(ones[:], 1.0).then_inc(ones_ok, 1)
                e.memset(g.v[:], 1.0).then_inc(ones_ok, 1)
                e.memset(vs[:], 0.0).then_inc(ones_ok, 1)
                with e.Fori(0, NT // 2) as i:
                    for p in range(2):
                        e.wait_ge(st_ok, (i * 2 + p + 1) * KT)
                        e.tensor_copy(g.nT[:, :, bass.ds((i * 2 + p) * T, T)], stage[:, p]).then_inc(nT_ok, 1)

            @block.vector
            def _(e):
                seq = Tally(e, dve)
                e.wait_ge(small_in, 48)
                e.tensor_reduce(rmax[:], recipe[:], AX.X, ALU.max, negate=True).then_inc(rmax_ok, 1)
                seq.step(e.tensor_reduce(gate[:], pat[:], AX.X, ALU.add))
                e.tensor_scalar(gate[:], gate[:], -1.0 / N, None, ALU.mult).then_inc(pat_ok, 1)
                e.wait_ge(pexp_ok, 1)
                seq.step(e.tensor_scalar(gate[:], gate[:], 1.0, None, ALU.add))
                seq.step(e.reciprocal(gate[:], gate[:]))
                e.tensor_scalar(gated[:], g.ident[0:NN, 0:NN], gate[:], None, ALU.mult).then_inc(gd_ok, 1)
                e.wait_ge(rexp_ok, 1)
                seq.step(e.reciprocal(rrec[:], rsum[:]))
                e.tensor_scalar(recipe[:], recipe[:], rrec[:], None, ALU.mult).then_inc(rec_ok, 1)
                e.wait_ge(recT_mm, 1)
                e.tensor_copy(recT[:], S1[0:NB, 0:NN]).then_inc(recT_ok, 1)
                e.wait_ge(nemb_mm, 1)
                e.tensor_copy(nemb[:, 0:3], TR[:, 0, 0:3 * NN].rearrange("p (k n) -> p k n", k=3)).then_inc(setup, 1)
                e.tensor_copy(nemb[:, 3:6], TR[:, 1, 0:3 * NN].rearrange("p (k n) -> p k n", k=3)).then_inc(setup, 1)
                e.wait_ge(gateB_mm, 1)
                e.tensor_copy(gateB[:], S2[0:T, 0:NN]).then_inc(setup, 1)
                norm_stats(e, seq, g.y, stats, mv, veps).then_inc(var_ok, 1)
                e.wait_ge(std_ok, 1)
                newton_rstd(e, seq, rstd[:], std[:], veps[:], tmp[:])
                for t in range(NT):
                    seq.mark(e.tensor_scalar(g.y[:, t], g.y[:, t], mv[:, t, 0:1], rstd[:, t:t + 1], ALU.subtract, ALU.mult))
                seq.settle()
                norm_stats(e, seq, g.y, stats, mv2, veps).then_inc(var_ok, 1)
                e.wait_ge(std_ok, 2)
                newton_rstd(e, seq, rstd[:], std[:], veps[:], tmp[:])
                e.wait_ge(setup, 3)
                e.wait_ge(vw_in, 32)
                e.wait_ge(ones_ok, 3)
                with e.Fori(0, NT // 2) as i:
                    seq.enter(i, 12)
                    for p in range(2):
                        n = i * 2 + p
                        e.wait_ge(tr_mm, n)
                        e.tensor_scalar(z[:, p], g.y[:, n, :], mv2[:, n, 0:1], rstd[:, bass.ds(n, 1)],
                                        ALU.subtract, ALU.mult).then_inc(z_ok, 1)
                        e.wait_ge(sem_mm, n + 1)
                        seq.step(e.tensor_tensor(fin[:], S1[0:T, 0:NN], gateB[:], ALU.mult))
                        e.sem_inc(fin_ok, 1)
                        seq.step(e.max(top[:], fin[:]))
                        e.tensor_scalar(ntop[:], top[:, 0:1], -1.0, None, ALU.mult).then_inc(top_ok, 1)
                        seq.step(e.match_replace(rep[:], top[:], fin[:], NEG))
                        e.wait_ge(ex_ok, n + 1)
                        seq.step(e.scalar_tensor_tensor(out=sel[:], in0=rep[:], scalar=NEG, in1=ex[:], op0=ALU.is_equal,
                                                        op1=ALU.mult, accum_out=ssum[:]))
                        seq.step(e.reciprocal(srec[:], ssum[:]))
                        e.tensor_scalar(sel[:], sel[:], srec[:], None, ALU.mult).then_inc(sel_ok, 1)
                        e.wait_ge(mixw_mm, n + 1)
                        e.tensor_copy(mixw[:], S1[0:T, 128:128 + NB]).then_inc(mixw_ok, 1)
                        e.wait_ge(mixw_ok, n + 1)
                        for c in range(NG):
                            e.wait_ge(pr_mm, n * NG + c + 1)
                            e.tensor_tensor(pw[:, c * NPB:(c + 1) * NPB], PR[0:T, c].rearrange("p (n r) -> p n r", r=RANK),
                                            mixw[:, c * NPB:(c + 1) * NPB].unsqueeze(2).to_broadcast([T, NPB, RANK]),
                                            ALU.mult).then_inc(pw_ok, 1)
                        e.wait_ge(pw_ok, (n + 1) * NG)
                        seq.step(e.tensor_reduce(vs[:, 0:RANK], pw[:].rearrange("p n r -> p r n"), AX.X, ALU.add))
                        e.sem_inc(vs_ok, 1)
                        e.wait_ge(v_mm, n + 1)
                        e.tensor_tensor(g.v[:, n, :].rearrange("p (c h d) -> p c h d", c=2, h=MP)[:, :, :, 0:DH],
                                        TR[0:T, :, 0:HALF].rearrange("p c (h d) -> p c h d", h=MP),
                                        vb[:].rearrange("p (c h d) -> p c h d", c=2, h=MP), ALU.add).then_inc(v_ok, 1)
                    seq.leave(NT // 2)

            @block.scalar
            def _(e):
                e.wait_ge(rmax_ok, 1)
                e.activation(recipe[:], recipe[:], ACT.Exp, bias=rmax[:], accum_out=rsum[:]).then_inc(rexp_ok, 1)
                e.wait_ge(pat_ok, 1)
                e.activation(gate[:], gate[:], ACT.Exp).then_inc(pexp_ok, 1)
                for i in range(2):
                    e.wait_ge(var_ok, i + 1)
                    e.activation(std[:], veps[:], ACT.Sqrt).then_inc(std_ok, 1)
                e.wait_ge(gs_in, 32)
                with e.Fori(0, NT // 2) as i:
                    for p in range(2):
                        n = i * 2 + p
                        e.wait_ge(tr_mm, n + 1)
                        e.wait_ge(nT_ok, n)
                        for k in range(KT):
                            e.activation(stage[:, p, k], TR[:, k // 3, k % 3 * T:(k % 3 + 1) * T], ACT.Identity,
                                         bias=shift[:, k:k + 1], scale=gain[:, k:k + 1]).then_inc(st_ok, 1)
                        e.wait_ge(top_ok, n + 1)
                        e.activation(ex[:], fin[:], ACT.Exp, bias=ntop[:]).then_inc(ex_ok, 1)
                        e.wait_ge(selT_mm, n + 1)
                        e.activation(selT[:], S2[0:NN, 0:T], ACT.Copy).then_inc(selT_ok, 1)
                        e.wait_ge(vsT_mm, n + 1)
                        e.activation(vsT[:], S2[0:RANK, 128:128 + T], ACT.Copy).then_inc(vsT_ok, 1)

            @block.tensor
            def _(e):
                e.wait_ge(rec_ok, 1)
                e.transpose(S1[0:NB, 0:NN], recipe[:], g.ident[0:NN, 0:NN]).then_inc(recT_mm, 1)
                e.wait_ge(recT_ok, 1)
                for k in range(KT):
                    ins = e.matmul(TR[:, k // 3, k % 3 * NN:(k % 3 + 1) * NN], bemb[:, k * 128:(k + 1) * 128], recT[:],
                                   start=True, stop=True)
                ins.then_inc(nemb_mm, 1)
                e.wait_ge(gd_ok, 1)
                e.wait_ge(ones_ok, 3)
                e.matmul(S2[0:T, 0:NN], ones[:], gated[:], start=True, stop=True).then_inc(gateB_mm, 1)
                e.wait_ge(setup, 3)
                e.wait_ge(bas_in, 16 * KT)
                e.wait_ge(vw_in, 32)
                with e.Fori(0, NT // 2) as i:
                    for p in range(2):
                        n = i * 2 + p
                        e.wait_ge(z_ok, n + 1)
                        e.wait_ge(v_ok, n)
                        for k in range(KT):
                            ins = e.transpose(TR[:, k // 3, k % 3 * T:(k % 3 + 1) * T], z[:, p, k * 128:(k + 1) * 128],
                                              g.ident[0:T, 0:T])
                        ins.then_inc(tr_mm, 1)
                        e.wait_ge(st_ok, (n + 1) * KT)
                        for k in range(KT):
                            ins = e.matmul(S1[0:T, 0:NN], stage[:, p, k], nemb[:, k], start=(k == 0), stop=(k == KT - 1))
                        ins.then_inc(sem_mm, 1)
                        for c in range(NG):
                            e.wait_ge(pw_ok, n * NG)
                            for k in range(KT):
                                ins = e.matmul(PR[0:T, c], stage[:, p, k], basis[:, k, c * NPB:(c + 1) * NPB].rearrange("p n r -> p (n r)"),
                                               start=(k == 0), stop=(k == KT - 1))
                            ins.then_inc(pr_mm, 1)
                        e.wait_ge(sel_ok, n + 1)
                        e.transpose(S2[0:NN, 0:T], sel[:], g.ident[0:T, 0:T]).then_inc(selT_mm, 1)
                        e.wait_ge(selT_ok, n + 1)
                        e.matmul(S1[0:T, 128:128 + NB], selT[:], recipe[:], start=True, stop=True).then_inc(mixw_mm, 1)
                        e.wait_ge(vs_ok, n + 1)
                        e.transpose(S2[:, 128:128 + T], vs[:], g.ident[0:T, 0:T]).then_inc(vsT_mm, 1)
                        e.wait_ge(vsT_ok, n + 1)
                        for c in range(2):
                            ins = e.matmul(TR[0:T, c, 0:HALF], vsT[:], vw[:, c * HALF:(c + 1) * HALF], start=True, stop=True)
                        ins.then_inc(v_mm, 1)


def attend(nc, g):
    STEPS = 2 * NT
    W2 = 2 * (DH + 1)
    NA = 500
    with ExitStack() as ctx:
        sb = lambda n, s, d=F32: ctx.enter_context(nc.sbuf_tensor("at_" + n, s, d))
        ps = lambda n, s: ctx.enter_context(nc.psum_tensor("at_" + n, s, F32))
        sem = lambda n: g.sem("at_" + n)
        qw, kw = sb("qw", [128, KT, 128]), sb("kw", [128, KT, 128])
        qb, kb = sb("qb", [128, KT]), sb("kb", [128, KT])
        qz = sb("qz", [128, 2, N])
        kT = sb("kT", [128, N])
        nmax, rc = sb("nmax", [T, 2]), sb("rc", [T, 2])
        A = sb("A", [T, 2, N])
        AT = sb("AT", [T, 2, N])
        S, O = ps("S", [128, 2, 3 * 512]), ps("O", [128, 2, 512])
        b_in, qw_in, kw_in, zero = sem("b_in"), sem("qw_in"), sem("kw_in"), sem("zero")
        q_mm, k_mm, q_out, k_out = sem("q_mm"), sem("k_mm"), sem("q_out"), sem("k_out")
        s_mm, max_ok, exp_ok, tt_mm, at_v, at_a, av_mm, rc_ok, ao_ok = (
            sem(n) for n in ("s_mm", "max_ok", "exp_ok", "tt_mm", "at_v", "at_a", "av_mm", "rc_ok", "ao_ok"))

        def over_pairs(e, pair):
            with e.Fori(0, MP - 1) as m:
                pair(m, False)
            pair(MP - 1, True)

        with nc.Block() as block:
            @block.sync
            def _(sp):
                sp.dma_start(qw[:], weight_view(g.ffn_q_w)[:, :, 0:128]).then_inc(qw_in, 16)
                sp.dma_start(kw[:], weight_view(g.ffn_k_w)[:, :, 0:128]).then_inc(kw_in, 16)
                for dst, v in ((qb, g.ffn_q_b), (kb, g.ffn_k_b)):
                    sp.dma_start(dst[:], v.rearrange("(k p) -> p k", p=128), allow_slow_non_contiguous=True).then_inc(b_in, 16)
                with sp.Fori(1, MP) as m:
                    sp.wait_ge(q_mm, m)
                    sp.dma_start(qw[:], weight_view(g.ffn_q_w)[:, :, bass.ds(m * 128, 128)]).then_inc(qw_in, 16)
                    sp.wait_ge(k_mm, m)
                    sp.dma_start(kw[:], weight_view(g.ffn_k_w)[:, :, bass.ds(m * 128, 128)]).then_inc(kw_in, 16)

            @block.gpsimd
            def _(e):
                e.memset(qz[DH:128, 0, :], 0.0).then_inc(zero, 1)
                e.memset(qz[0:DH, 1, :], 0.0).then_inc(zero, 1)

            @block.tensor
            def _(e):
                def linear(w, slot):
                    for a, n in CHUNKS:
                        for k in range(KT):
                            ins = e.matmul(S[:, slot, a:a + n], w[:, k], g.nT[:, k, a:a + n], start=(k == 0), stop=(k == KT - 1))
                    return ins

                def scores(u):
                    for a, n in CHUNKS:
                        ins = e.matmul(S[0:T, u % 2, a:a + n], qz[:, u // NT, u % NT * T:(u % NT + 1) * T], kT[:, a:a + n],
                                       start=True, stop=True)
                    ins.then_inc(s_mm, 1)

                def values(m, u):
                    e.wait_ge(at_v, m * STEPS + u + 1)
                    e.wait_ge(at_a, m * STEPS + u + 1)
                    e.wait_ge(ao_ok, m * STEPS + max(u - 1, 0))
                    for t in range(NT):
                        ins = e.matmul(O[0:T, u % 2, 0:W2], AT[:, u % 2, t * T:(t + 1) * T], g.v[:, t, bass.ds(m * W2, W2)],
                                       start=(t == 0), stop=(t == NT - 1))
                    ins.then_inc(av_mm, 1)

                def pair(m, last):
                    e.wait_ge(q_out, 2 * m + 2)
                    e.wait_ge(k_out, m + 1)
                    scores(0)
                    scores(1)
                    for u in range(STEPS):
                        e.wait_ge(exp_ok, m * STEPS + u + 1)
                        for t in range(NT):
                            a = t // 4 * 512 + t % 4 * T
                            ins = e.transpose(S[0:T, u % 2, a:a + T], A[:, u % 2, t * T:(t + 1) * T], g.ident[0:T, 0:T])
                        ins.then_inc(tt_mm, 1)
                        if u > 0:
                            values(m, u - 1)
                        if not last or u + 2 < STEPS:
                            e.wait_ge(at_v, m * STEPS + u + 1)
                            e.wait_ge(at_a, m * STEPS + u + 1)
                        if u + 2 < STEPS:
                            scores(u + 2)
                        elif not last:
                            w, into, done = ((qw, qw_in, q_mm), (kw, kw_in, k_mm))[u + 2 - STEPS]
                            e.wait_ge(into, (m + 2) * 16)
                            linear(w, u % 2).then_inc(done, 1)
                    values(m, STEPS - 1)

                e.wait_ge(zero, 2)
                e.wait_ge(qw_in, 16)
                linear(qw, 0).then_inc(q_mm, 1)
                e.wait_ge(kw_in, 16)
                linear(kw, 1).then_inc(k_mm, 1)
                over_pairs(e, pair)

            @block.scalar
            def _(e):
                def keys(m):
                    e.wait_ge(k_mm, m + 1)
                    e.activation(kT[:], S[:, 1, 0:N], ACT.Identity, bias=kb[:, bass.ds(m, 1)]).then_inc(k_out, 1)

                def pair(m, last):
                    for s in range(STEPS + 1):
                        u = s - 1
                        if u >= 0:
                            e.wait_ge(tt_mm, m * STEPS + u + 1)
                            e.wait_ge(av_mm, m * STEPS + max(u - 1, 0))
                            e.activation(AT[:, u % 2, 0:NA], S[0:T, u % 2, 0:NA], ACT.Copy)
                            e.activation(AT[:, u % 2, 2 * NA:N], S[0:T, u % 2, 1024:1024 + N - 2 * NA], ACT.Copy).then_inc(at_a, 1)
                        if s < STEPS:
                            e.wait_ge(max_ok, m * STEPS + s + 1)
                            e.wait_ge(tt_mm, m * STEPS + max(s - 1, 0))
                            e.activation(A[:, s % 2], S[0:T, s % 2, 0:N], ACT.Exp, bias=nmax[:, s % 2:s % 2 + 1]).then_inc(exp_ok, 1)
                    if not last:
                        keys(m + 1)

                e.wait_ge(b_in, 32)
                keys(0)
                over_pairs(e, pair)

            @block.vector
            def _(e):
                def queries(m):
                    e.wait_ge(q_mm, m + 1)
                    for h in range(2):
                        rows = slice(h * DH, (h + 1) * DH)
                        e.tensor_scalar(qz[rows, h, :], S[rows, 0, 0:N], qb[rows, bass.ds(m, 1)], DH ** -0.5,
                                        ALU.add, ALU.mult).then_inc(q_out, 1)

                def pair(m, last):
                    for s in range(STEPS + 2):
                        if s < STEPS:
                            e.wait_ge(s_mm, m * STEPS + s + 1)
                            e.tensor_reduce(nmax[:, s % 2:s % 2 + 1], S[0:T, s % 2, 0:N], AX.X, ALU.max,
                                            negate=True).then_inc(max_ok, 1)
                        u = s - 1
                        if 0 <= u < STEPS:
                            e.wait_ge(tt_mm, m * STEPS + u + 1)
                            e.wait_ge(av_mm, m * STEPS + max(u - 1, 0))
                            e.tensor_copy(AT[:, u % 2, NA:2 * NA], S[0:T, u % 2, 512:512 + NA]).then_inc(at_v, 1)
                        if s == STEPS and not last:
                            queries(m + 1)
                        u = s - 2
                        if u >= 0:
                            e.wait_ge(av_mm, m * STEPS + u + 1)
                            c = u // NT * (DH + 1)
                            e.reciprocal(rc[:, u % 2:u % 2 + 1], O[0:T, u % 2, c + DH:c + DH + 1]).then_inc(rc_ok, 1)
                            e.wait_ge(rc_ok, m * STEPS + u + 1)
                            e.tensor_scalar(g.ao[:, u % NT, bass.ds(m * 128 + u // NT * DH, DH)], O[0:T, u % 2, c:c + DH],
                                            rc[:, u % 2:u % 2 + 1], None, ALU.mult).then_inc(ao_ok, 1)

                e.wait_ge(b_in, 32)
                queries(0)
                over_pairs(e, pair)


def tail(nc, g):
    with ExitStack() as ctx:
        sb = lambda n, s, d=F32: ctx.enter_context(nc.sbuf_tensor("ta_" + n, s, d))
        ps = lambda n, s: ctx.enter_context(nc.psum_tensor("ta_" + n, s, F32))
        sem = lambda n: g.sem("ta_" + n)
        wo, wu, wd = sb("wo", [128, KT, D]), sb("wu", [128, KT, FF]), sb("wd", [128, FJ, D])
        bo, bd = sb("bo", [T, D]), sb("bd", [T, D])
        gain, shift, bu = sb("gain", [128, KT]), sb("shift", [128, KT]), sb("bu", [128, FJ])
        stats, mv = sb("stats", [T, NT, 12]), sb("mv", [T, NT, 2])
        veps, std, rstd, tmp = (sb(n, [T, NT]) for n in ("veps", "std", "rstd", "tmp"))
        stage = sb("stage", [128, 2, KT, T])
        z, xt, res = sb("z", [T, 2, D]), sb("xt", [T, 2, D]), sb("res", [T, 2, D])
        uT = sb("uT", [128, 2, FJ, T])
        TR, O = ps("TR", [128, 2, 2, 512]), ps("O", [128, 2, 2, 512])
        wo_in, w_in, b_in = sem("wo_in"), sem("w_in"), sem("b_in")
        in_, sent = [sem("in0"), sem("in1")], [sem("sent0"), sem("sent1")]
        tr_mm, st_ok, mm, add_ok, x2_ok, dve, var_ok, std_ok = (
            sem(n) for n in ("tr_mm", "st_ok", "mm", "add_ok", "x2_ok", "dve", "var_ok", "std_ok"))
        z_ok, zt_mm, zs_ok, up_mm, u_ok, dn_mm, xt_ok, res_ok = (
            sem(n) for n in ("z_ok", "zt_mm", "zs_ok", "up_mm", "u_ok", "dn_mm", "xt_ok", "res_ok"))
        split = lambda x: x.rearrange("p (c n) -> p c n", c=2)

        with nc.Block() as block:
            @block.sync
            def _(sp):
                sp.dma_start(wo[:], weight_view(g.ffn_ao_w)).then_inc(wo_in, 16)
                sp.dma_start(bo[:], g.ffn_ao_b.partition_broadcast(T)).then_inc(b_in, 16)
                sp.dma_start(bd[:], g.ffn_down_b.partition_broadcast(T)).then_inc(b_in, 16)
                for dst, v in ((gain, g.ffn_n2_g), (shift, g.ffn_n2_b), (bu, g.ffn_up_b)):
                    sp.dma_start(dst[:], v.rearrange("(k p) -> p k", p=128), allow_slow_non_contiguous=True).then_inc(b_in, 16)
                sp.dma_start(wu[:], weight_view(g.ffn_up_w)).then_inc(w_in, 16)
                sp.dma_start(wd[:], weight_view(g.ffn_down_w)).then_inc(w_in, 16)
                for p in range(2):
                    sp.dma_start(xt[:, p], g.xj[p * T:(p + 1) * T, :]).then_inc(in_[p], 16)
                with sp.Fori(0, NT // 2 - 1) as i:
                    for p in range(2):
                        n = i * 2 + p
                        sp.wait_ge(res_ok, n + 1)
                        sp.dma_start(g.out[bass.ds(n * T, T), :], res[:, p]).then_inc(sent[p], 16)
                        sp.dma_start(xt[:, p], g.xj[bass.ds((n + 2) * T, T), :]).then_inc(in_[p], 16)
                for n in range(NT - 2, NT):
                    sp.wait_ge(res_ok, n + 1)
                    sp.dma_start(g.out[n * T:(n + 1) * T, :], res[:, n % 2]).then_inc(sent[n % 2], 16)
                for s in sent:
                    sp.wait_ge(s, 16 * NT // 2)

            @block.tensor
            def _(e):
                e.wait_ge(wo_in, 16)
                for n in range(NT):
                    p = n % 2
                    if n > 0:
                        e.wait_ge(st_ok, n)
                    for k in range(KT):
                        ins = e.transpose(TR[:, p, k // 3, k % 3 * T:(k % 3 + 1) * T],
                                          g.ao[:, n, k * 128:(k + 1) * 128], g.ident[0:T, 0:T])
                    ins.then_inc(tr_mm, 1)
                    e.wait_ge(st_ok, n + 1)
                    if n >= 2:
                        e.wait_ge(add_ok, n - 1)
                    for c in range(2):
                        for k in range(KT):
                            ins = e.matmul(O[0:T, p, c, 0:HALF], stage[:, p, k], wo[:, k, c * HALF:(c + 1) * HALF],
                                           start=(k == 0), stop=(k == KT - 1))
                    ins.then_inc(mm, 1)
                e.wait_ge(w_in, 32)
                e.wait_ge(add_ok, NT)
                with e.Fori(0, NT // 2) as i:
                    for p in range(2):
                        n = i * 2 + p
                        e.wait_ge(z_ok, n + 1)
                        e.wait_ge(zs_ok, n)
                        for k in range(KT):
                            ins = e.transpose(TR[:, 0, k // 3, k % 3 * T:(k % 3 + 1) * T], z[:, p, k * 128:(k + 1) * 128],
                                              g.ident[0:T, 0:T])
                        ins.then_inc(zt_mm, 1)
                        e.wait_ge(zs_ok, n + 1)
                        e.wait_ge(u_ok, n)
                        for j in range(FJ):
                            for k in range(KT):
                                ins = e.matmul(TR[:, 1, p, j * T:(j + 1) * T], wu[:, k, j * 128:(j + 1) * 128], stage[:, p, k],
                                               start=(k == 0), stop=(k == KT - 1))
                        ins.then_inc(up_mm, 1)
                        e.wait_ge(u_ok, n + 1)
                        e.wait_ge(res_ok, i * 2)
                        for c in range(2):
                            for j in range(FJ):
                                ins = e.matmul(O[0:T, p, c, 0:HALF], uT[:, p, j], wd[:, j, c * HALF:(c + 1) * HALF],
                                               start=(j == 0), stop=(j == FJ - 1))
                        ins.then_inc(dn_mm, 1)

            @block.scalar
            def _(e):
                with e.Fori(0, NT // 2) as i:
                    for p in range(2):
                        n = i * 2 + p
                        e.wait_ge(tr_mm, n + 1)
                        e.wait_ge(mm, i * 2)
                        e.activation(stage[:, p].rearrange("p (c k) t -> p c (k t)", c=2), TR[:, p, :, 0:3 * T],
                                     ACT.Copy).then_inc(st_ok, 1)
                e.wait_ge(var_ok, 1)
                e.activation(std[:], veps[:], ACT.Sqrt).then_inc(std_ok, 1)
                e.wait_ge(b_in, 80)
                e.wait_ge(mm, NT)
                with e.Fori(0, NT // 2) as i:
                    for p in range(2):
                        n = i * 2 + p
                        e.wait_ge(zt_mm, n + 1)
                        for k in range(KT):
                            ins = e.activation(stage[:, p, k], TR[:, 0, k // 3, k % 3 * T:(k % 3 + 1) * T], ACT.Identity,
                                               bias=shift[:, k:k + 1], scale=gain[:, k:k + 1])
                        ins.then_inc(zs_ok, 1)
                        e.wait_ge(up_mm, n + 1)
                        e.wait_ge(dn_mm, i * 2)
                        for j in range(FJ):
                            ins = e.activation(uT[:, p, j], TR[:, 1, p, j * T:(j + 1) * T], ACT.Gelu, bias=bu[:, j:j + 1])
                        ins.then_inc(u_ok, 1)

            @block.vector
            def _(e):
                seq = Tally(e, dve)
                e.wait_ge(b_in, 80)
                with e.Fori(0, NT // 2) as i:
                    for p in range(2):
                        n = i * 2 + p
                        e.wait_ge(mm, n + 1)
                        e.tensor_tensor(split(z[:, p]), O[0:T, p, :, 0:HALF], split(bo[:]), ALU.add).then_inc(add_ok, 1)
                        e.wait_ge(add_ok, n + 1)
                        e.tensor_tensor(g.y[:, n, :], g.y[:, n, :], z[:, p], ALU.add).then_inc(x2_ok, 1)
                e.wait_ge(x2_ok, NT)
                norm_stats(e, seq, g.y, stats, mv, veps).then_inc(var_ok, 1)
                e.wait_ge(std_ok, 1)
                newton_rstd(e, seq, rstd[:], std[:], veps[:], tmp[:])
                with e.Fori(0, NT // 2) as i:
                    for p in range(2):
                        n = i * 2 + p
                        e.wait_ge(zt_mm, n)
                        e.tensor_scalar(z[:, p], g.y[:, n, :], mv[:, n, 0:1], rstd[:, bass.ds(n, 1)],
                                        ALU.subtract, ALU.mult).then_inc(z_ok, 1)
                        e.wait_ge(in_[p], i * 16 + 16)
                        e.tensor_tensor(xt[:, p], xt[:, p], g.y[:, n, :], ALU.add).then_inc(xt_ok, 1)
                        e.wait_ge(xt_ok, 2 * n + 1)
                        e.tensor_tensor(xt[:, p], xt[:, p], bd[:], ALU.add).then_inc(xt_ok, 1)
                        e.wait_ge(dn_mm, n + 1)
                        e.wait_ge(xt_ok, 2 * n + 2)
                        e.wait_ge(sent[p], i * 16)
                        e.tensor_tensor(split(res[:, p]), O[0:T, p, :, 0:HALF], split(xt[:, p]), ALU.add).then_inc(res_ok, 1)


def graph_transformer_layer(
    nc: bass.Bass,
    x: bass.AP,
    src: bass.AP,
    dst: bass.AP,
    gnn_W_ah: bass.AP,
    gnn_b_ah: bass.AP,
    gnn_W0: bass.AP,
    gnn_a_src0: bass.AP,
    gnn_a_dst0: bass.AP,
    gnn_b0: bass.AP,
    gnn_W1: bass.AP,
    gnn_a_src1: bass.AP,
    gnn_a_dst1: bass.AP,
    gnn_b1: bass.AP,
    gnn_W2: bass.AP,
    gnn_a_src2: bass.AP,
    gnn_a_dst2: bass.AP,
    gnn_b2: bass.AP,
    gnn_W_out: bass.AP,
    gnn_b_out: bass.AP,
    mix_Wq: bass.AP,
    mix_Wk: bass.AP,
    mix_Wv: bass.AP,
    mix_Wo: bass.AP,
    mix_proj: bass.AP,
    ffn_q_w: bass.AP,
    ffn_q_b: bass.AP,
    ffn_k_w: bass.AP,
    ffn_k_b: bass.AP,
    ffn_ao_w: bass.AP,
    ffn_ao_b: bass.AP,
    ffn_recipe: bass.AP,
    ffn_ctx_pat: bass.AP,
    ffn_basis_emb: bass.AP,
    ffn_basis_A: bass.AP,
    ffn_vout_w: bass.AP,
    ffn_vout_b: bass.AP,
    ffn_up_w: bass.AP,
    ffn_up_b: bass.AP,
    ffn_down_w: bass.AP,
    ffn_down_b: bass.AP,
    ffn_n1_g: bass.AP,
    ffn_n1_b: bass.AP,
    ffn_n2_g: bass.AP,
    ffn_n2_b: bass.AP,
    out: bass.AP,
):
    g = Env()
    g.x = x
    g.src = src
    g.dst = dst
    g.gnn_W_ah = gnn_W_ah
    g.gnn_b_ah = gnn_b_ah
    g.gnn_W0 = gnn_W0
    g.gnn_a_src0 = gnn_a_src0
    g.gnn_a_dst0 = gnn_a_dst0
    g.gnn_b0 = gnn_b0
    g.gnn_W1 = gnn_W1
    g.gnn_a_src1 = gnn_a_src1
    g.gnn_a_dst1 = gnn_a_dst1
    g.gnn_b1 = gnn_b1
    g.gnn_W2 = gnn_W2
    g.gnn_a_src2 = gnn_a_src2
    g.gnn_a_dst2 = gnn_a_dst2
    g.gnn_b2 = gnn_b2
    g.gnn_W_out = gnn_W_out
    g.gnn_b_out = gnn_b_out
    g.mix_Wq = mix_Wq
    g.mix_Wk = mix_Wk
    g.mix_Wv = mix_Wv
    g.mix_Wo = mix_Wo
    g.mix_proj = mix_proj
    g.ffn_q_w = ffn_q_w
    g.ffn_q_b = ffn_q_b
    g.ffn_k_w = ffn_k_w
    g.ffn_k_b = ffn_k_b
    g.ffn_ao_w = ffn_ao_w
    g.ffn_ao_b = ffn_ao_b
    g.ffn_recipe = ffn_recipe
    g.ffn_ctx_pat = ffn_ctx_pat
    g.ffn_basis_emb = ffn_basis_emb
    g.ffn_basis_A = ffn_basis_A
    g.ffn_vout_w = ffn_vout_w
    g.ffn_vout_b = ffn_vout_b
    g.ffn_up_w = ffn_up_w
    g.ffn_up_b = ffn_up_b
    g.ffn_down_w = ffn_down_w
    g.ffn_down_b = ffn_down_b
    g.ffn_n1_g = ffn_n1_g
    g.ffn_n1_b = ffn_n1_b
    g.ffn_n2_g = ffn_n2_g
    g.ffn_n2_b = ffn_n2_b
    g.out = out
    g.TABLE_ZERO = 16 * (NT // 2 + 1)
    scratch = lambda n, s: nc.dram_tensor(n, s, F32, kind="Internal").ap()
    g.table = scratch("edge_table", (CELLS + T, 1))
    g.mix_out = scratch("mixer_out", (N, D))
    g.rows, g.uv = scratch("score_rows", (2 * GI, N)), scratch("score_uv", (2 * GI, N))
    g.h = scratch("gnn_h", (GI, N, GC))
    g.node = scratch("gnn_nodes", (N, GL * D))
    g.xj = scratch("residual", (N, D))
    g.sem = lambda n: nc.alloc_semaphore(name=n)
    keep = lambda scope, n, s, d=F32: scope.enter_context(nc.sbuf_tensor(n, s, d))
    with ExitStack() as whole:
        g.ident = keep(whole, "ident", [128, 128])
        with nc.cleanup_on_exit(), ExitStack() as gnn:
            g.table_sem, g.scattered = g.sem("table_zeroed"), g.sem("scattered")
            g.asad, g.as02 = keep(gnn, "asad", [T, NT, 2 * GI]), keep(gnn, "as02", [T, NT, GI])
            with ExitStack() as first:
                g.edge_add, g.edge_cell = keep(first, "edge_add", [T, EB]), keep(first, "edge_cell", [T, EB], I32)
                g.xnT = keep(first, "xnT", [128, KT, N])
                with ExitStack() as values:
                    g.v = keep(values, "mix_v", [T, NT, MH * (DH + 1)])
                    front(nc, g)
                    mix(nc, g, range(EB))
                lift(nc, g)
            graph(nc, g)
        with nc.cleanup_on_exit(), ExitStack() as ffn:
            g.y = keep(ffn, "y", [T, NT, D])
            join(nc, g)
            with ExitStack() as late:
                g.ao = keep(late, "ao", [T, NT, D])
                with ExitStack() as attention:
                    g.v = keep(attention, "ffn_v", [T, NT, MH * (DH + 1)])
                    g.nT = keep(attention, "normedT", [128, KT, N])
                    route(nc, g)
                    attend(nc, g)
                tail(nc, g)


_INS = ['x', 'src', 'dst', 'L0_gnn_W_ah', 'L0_gnn_b_ah', 'L0_gnn_W0', 'L0_gnn_a_src0', 'L0_gnn_a_dst0', 'L0_gnn_b0', 'L0_gnn_W1', 'L0_gnn_a_src1', 'L0_gnn_a_dst1', 'L0_gnn_b1', 'L0_gnn_W2', 'L0_gnn_a_src2', 'L0_gnn_a_dst2', 'L0_gnn_b2', 'L0_gnn_W_out', 'L0_gnn_b_out', 'L0_mix_Wq', 'L0_mix_Wk', 'L0_mix_Wv', 'L0_mix_Wo', 'L0_mix_proj', 'L0_ffn_q_w', 'L0_ffn_q_b', 'L0_ffn_k_w', 'L0_ffn_k_b', 'L0_ffn_ao_w', 'L0_ffn_ao_b', 'L0_ffn_recipe', 'L0_ffn_ctx_pat', 'L0_ffn_basis_emb', 'L0_ffn_basis_A', 'L0_ffn_vout_w', 'L0_ffn_vout_b', 'L0_ffn_up_w', 'L0_ffn_up_b', 'L0_ffn_down_w', 'L0_ffn_down_b', 'L0_ffn_n1_g', 'L0_ffn_n1_b', 'L0_ffn_n2_g', 'L0_ffn_n2_b']


def kernel(**inputs):
    import numpy as _np
    import concourse.bacc as _bacc
    from concourse import mybir as _mybir
    from concourse.bass_utils import run_bass_kernel_spmd as _run

    nc = _bacc.Bacc("TRN2", target_bir_lowering=False, num_devices=1)
    arrays, args = {}, []
    for name in _INS:
        a = _np.ascontiguousarray(inputs[name])
        arrays[f"in_{name}_dram"] = a
        args.append(nc.dram_tensor(f"in_{name}_dram", a.shape, _mybir.dt.from_np(a.dtype), kind="ExternalInput").ap())
    args.append(nc.dram_tensor("out_0_dram", (1250, 768), _mybir.dt.float32, kind="ExternalOutput").ap())
    graph_transformer_layer(nc, *args)
    r = _run(nc, [arrays], core_ids=[0])
    return r.results[0]["out_0_dram"]
```

```python
from contextlib import ExitStack

import concourse.bass as bass
from concourse import mybir

F32 = mybir.dt.float32
I32 = mybir.dt.int32
U32 = mybir.dt.uint32
BF16 = mybir.dt.bfloat16
F32R = mybir.dt.float32r
ALU = mybir.AluOpType
ACT = mybir.ActivationFunctionType
AX = mybir.AxisListType

N, D = 1250, 768
T, NT = 125, 10
KT = D // 128
HALF = D // 2
E = 20000
EB = E // T
EG = EB // 4
GH, GC, GL = 4, 192, 3
GI = GL * GH
MH, DH = 12, 64
MP = MH // 2
M = 256
NB, RANK, NN = 32, 64, 96
FF = 384
FJ = FF // 128
LN_EPS = 1e-5
MIX_EPS = 1e-4
NEG = -1e30
CHUNKS = [(0, 512), (512, 512), (1024, 226)]
CELLS = N * N


class Tally:

    def __init__(self, eng, sem):
        self.eng, self.sem, self.n, self.i, self.per, self.start = eng, sem, 0, None, 0, 0

    def mark(self, ins):
        ins.then_inc(self.sem, 1)
        self.n += 1

    def settle(self):
        self.eng.wait_ge(self.sem, self.n if self.i is None else self.i * self.per + self.n)

    def step(self, ins):
        self.mark(ins)
        self.settle()

    def enter(self, i, per):
        self.i, self.per, self.start = i, per, self.n

    def leave(self, times):
        assert self.n - self.start == self.per, (self.n - self.start, self.per)
        self.n, self.i = self.start + self.per * times, None


class Env:
    pass


def shared(nc, sb, first, *later):
    name, shape, dtype = first
    with nc.sbuf_tensor(name, shape, dtype) as old:
        pass
    return [old] + [sb(*x) for x in later]


def weight_view(w):
    return w.rearrange("(k p) n -> p k n", p=128)


def node_view(x):
    return x.rearrange("(t p) d -> p t d", p=T)


def norm_stats(v, tally, src, stats, mv, veps):
    for t in range(NT):
        for c in range(2):
            tally.mark(v.bn_stats(stats[:, t, 6 * c:6 * c + 6], src[:, t, c * HALF:(c + 1) * HALF]))
    tally.settle()
    for t in range(NT):
        tally.mark(v.bn_aggr(mv[:, t, :], stats[:, t, :]))
    tally.settle()
    return v.tensor_scalar(veps[:, :], mv[:, :, 1], LN_EPS, None, ALU.add)


def newton_rstd(v, tally, rstd, std, veps, tmp):
    tally.step(v.reciprocal(rstd, std))
    tally.step(v.tensor_tensor(tmp, rstd, rstd, ALU.mult))
    tally.step(v.tensor_tensor(tmp, tmp, veps, ALU.mult))
    tally.step(v.tensor_scalar(tmp, tmp, -0.5, 1.5, ALU.mult, ALU.add))
    tally.step(v.tensor_tensor(rstd, rstd, tmp, ALU.mult))


def front(nc, g):
    with ExitStack() as ctx:
        sb = lambda n, s, d=F32: ctx.enter_context(nc.sbuf_tensor(n, s, d))
        ps = lambda n, s: ctx.enter_context(nc.psum_tensor(n, s, F32))
        sem = g.sem
        x = sb("fr_x", [T, NT, D])
        wv = sb("fr_wv", [128, KT, D])
        stage = sb("fr_stage", [128, 2, KT, T])
        stats, mv = sb("fr_stats", [T, NT, 12]), sb("fr_mv", [T, NT, 2])
        veps, std, rstd = (sb(f"fr_{n}", [T, NT]) for n in ("veps", "std", "rstd"))
        tmp = sb("fr_tmp", [T, NT])
        zeros = sb("fr_zeros", [T, 2 * N])
        srci, dsti = sb("fr_src", [T, EB], I32), sb("fr_dst", [T, EB], I32)
        key, tot = sb("fr_key", [T, EB + 4]), sb("fr_tot", [T, EB])
        xn = sb("fr_xn", [T, 2, D])
        ones = sb("fr_ones", [T, T])
        before = sb("fr_before", [T, T])
        spare = sb("fr_spare", [T, 1])
        sparei = sb("fr_sparei", [T, 1], I32)
        diag = sb("fr_diag", [T, 2, 4, T])
        junk = sb("fr_junk", [T, 2, 4, T])
        first, idxf = sb("fr_first", [T, EB]), sb("fr_idxf", [T, EB])
        tr = ps("fr_tr", [128, 2, 2, 512])
        vps = ps("fr_vps", [128, 2, 512])
        kps = ps("fr_kps", [128, 2, 512])
        x_in, e_in, wv_in = sem("fr_x_in"), sem("fr_e_in"), sem("fr_wv_in")
        zeroed, setup, spare_ok = sem("fr_zeroed"), sem("fr_setup"), sem("fr_spare_ok")
        dve, pool = sem("fr_dve"), sem("fr_pool")
        var_ok, std_ok, xn_ok = sem("fr_var"), sem("fr_std"), sem("fr_xn_ok")
        tr_ok, st_ok, xnT_ok, v_ok, v_out = (sem(f"fr_{n}") for n in ("tr_ok", "st_ok", "xnT_ok", "v_ok", "v_out"))
        diag_ok, row_ok, row_used = sem("fr_diag_ok"), sem("fr_row_ok"), sem("fr_row_used")

        with nc.Block() as block:
            @block.sync
            def _(sp):
                sp.dma_start(x[:], node_view(g.x)).then_inc(x_in, 16)
                sp.dma_start(srci[:], g.src.rearrange("(p b) -> p b", p=T)).then_inc(e_in, 16)
                sp.dma_start(dsti[:], g.dst.rearrange("(p b) -> p b", p=T)).then_inc(e_in, 16)
                sp.dma_start(wv[:], weight_view(g.mix_Wv)).then_inc(wv_in, 16)
                sp.wait_ge(zeroed, 1)
                cells = g.table[0:CELLS].rearrange("(q p r) o -> q p (r o)", p=T, r=2 * N)
                for q in range(NT // 2):
                    sp.dma_start(cells[q], zeros[:]).then_inc(g.table_sem, 16)
                sp.dma_start(g.table[CELLS:CELLS + T], zeros[:, 0:1]).then_inc(g.table_sem, 16)
                sp.wait_ge(g.table_sem, g.TABLE_ZERO)

            @block.gpsimd
            def _(e):
                seq = Tally(e, pool)
                seq.step(e.memset(g.ident[:], 0.0))
                seq.step(e.affine_select(out=g.ident[:], in_=g.ident[:], compare_op=ALU.not_equal, fill=1.0,
                                         base=0, pattern=[[-1, 128]], channel_multiplier=1))
                e.memset(zeros[:], 0.0).then_inc(zeroed, 1)
                e.memset(ones[:], 1.0).then_inc(setup, 1)
                seq.step(e.memset(before[:], float(1 + 2 * T)))
                e.affine_select(out=before[:], in_=before[:], compare_op=ALU.is_gt, fill=1.0,
                                base=0, pattern=[[-1, T]], channel_multiplier=1).then_inc(setup, 1)
                e.memset(g.v[:], 1.0).then_inc(setup, 1)
                e.iota(sparei[:], pattern=[[0, 1]], base=CELLS, channel_multiplier=1).then_inc(spare_ok, 1)
                with e.Fori(0, NT // 2) as i:
                    for par in range(2):
                        e.wait_ge(st_ok, i * 2 + par + 1)
                        e.tensor_copy(g.xnT[:, :, bass.ds((i * 2 + par) * T, T)], stage[:, par]).then_inc(xnT_ok, 1)

            @block.vector
            def _(e):
                seq = Tally(e, dve)
                e.wait_ge(x_in, 16)
                norm_stats(e, seq, x, stats, mv, veps).then_inc(var_ok, 1)
                e.wait_ge(e_in, 32)
                seq.mark(e.memset(key[:, EB:EB + 4], 0.0))
                seq.mark(e.scalar_tensor_tensor(out=key[:, 0:EB], in0=srci[:], scalar=float(N), in1=dsti[:],
                                                op0=ALU.mult, op1=ALU.add))
                e.wait_ge(std_ok, 1)
                newton_rstd(e, seq, rstd[:], std[:], veps[:], tmp[:])
                e.wait_ge(setup, 2)

                def spread(n, slot):
                    e.tensor_tensor(diag[:, slot], g.ident[0:T, 0:T].unsqueeze(1).to_broadcast([T, 4, T]),
                                    key[:, bass.ds(n * 4, 4)].unsqueeze(2).to_broadcast([T, 4, T]),
                                    ALU.mult).then_inc(diag_ok, 1)

                spread(0, 0)
                with e.Fori(0, NT // 2) as i:
                    for par in range(2):
                        n = i * 2 + par
                        e.wait_ge(tr_ok, n)
                        e.tensor_scalar(xn[:, par], x[:, n, :], mv[:, n, 0:1], rstd[:, bass.ds(n, 1)],
                                        ALU.subtract, ALU.mult).then_inc(xn_ok, 1)
                        for q in range(4):
                            grp = n * 4 + q
                            e.wait_ge(row_ok, grp)
                            spread(grp + 1, (q + 1) % 2)
                            e.wait_ge(row_ok, grp + 1)
                            e.wait_ge(row_used, grp)
                            for j in range(4):
                                ins = e.scalar_tensor_tensor(
                                    out=junk[:, q % 2, j], in0=kps[0:T, q % 2, j * T:(j + 1) * T],
                                    scalar=key[:, bass.ds(grp * 4 + j, 1)], in1=before[:], op0=ALU.is_equal,
                                    op1=ALU.mult, accum_out=tot[:, bass.ds(grp * 4 + j, 1)])
                            ins.then_inc(row_used, 1)
                e.wait_ge(row_used, EG + 1)
                e.wait_ge(spare_ok, 1)
                seq.mark(e.tensor_copy(spare[:], sparei[:]))
                seq.step(e.tensor_scalar(first[:], tot[:], float(2 * T), None, ALU.is_lt))
                seq.mark(e.tensor_tensor(g.edge_add[:], tot[:], first[:], ALU.mult))
                seq.step(e.scalar_tensor_tensor(out=idxf[:], in0=key[:, 0:EB], scalar=spare[:], in1=first[:],
                                                op0=ALU.subtract, op1=ALU.mult))
                seq.step(e.tensor_scalar(g.edge_cell[:], idxf[:], spare[:], None, ALU.add))

            @block.scalar
            def _(e):
                e.wait_ge(var_ok, 1)
                e.activation(std[:], veps[:], ACT.Sqrt).then_inc(std_ok, 1)
                e.wait_ge(setup, 3)
                with e.Fori(0, NT // 2) as i:
                    for par in range(2):
                        n = i * 2 + par
                        e.wait_ge(tr_ok, n + 1)
                        e.wait_ge(xnT_ok, n)
                        e.activation(stage[:, par].rearrange("p (c k) t -> p c (k t)", c=2),
                                     tr[:, par, :, 0:3 * T], ACT.Copy).then_inc(st_ok, 1)
                        e.wait_ge(v_ok, n + 1)
                        e.activation(g.v[:, n, :].rearrange("p (c h d) -> p c h d", c=2, h=MP)[:, :, :, 0:DH],
                                     vps[0:T, :, 0:HALF].rearrange("p c (h d) -> p c h d", h=MP),
                                     ACT.Copy).then_inc(v_out, 1)

            @block.tensor
            def _(e):
                e.wait_ge(setup, 3)
                e.wait_ge(wv_in, 16)
                e.sem_inc(row_used, 1)
                with e.Fori(0, NT // 2) as i:
                    for par in range(2):
                        n = i * 2 + par
                        e.wait_ge(xn_ok, n + 1)
                        for k in range(KT):
                            ins = e.transpose(tr[:, par, k // 3, (k % 3) * T:(k % 3 + 1) * T],
                                              xn[:, par, k * 128:(k + 1) * 128], g.ident[0:T, 0:T])
                        ins.then_inc(tr_ok, 1)
                        for q in range(4):
                            grp = n * 4 + q
                            e.wait_ge(diag_ok, grp + 1)
                            e.wait_ge(row_used, grp)
                            e.matmul(kps[0:T, q % 2, 0:4 * T], ones[:], diag[:, q % 2].rearrange("p j f -> p (j f)"),
                                     start=True, stop=True).then_inc(row_ok, 1)
                        e.wait_ge(st_ok, n + 1)
                        e.wait_ge(v_out, n)
                        for c in range(2):
                            for k in range(KT):
                                ins = e.matmul(vps[0:T, c, 0:HALF], stage[:, par, k], wv[:, k, c * HALF:(c + 1) * HALF],
                                               start=(k == 0), stop=(k == KT - 1))
                        ins.then_inc(v_ok, 1)


def scatter_counts(e, g, blocks):
    for b in blocks:
        if b > 0:
            e.wait_ge(g.scattered, 16 * b)
        e.indirect_dma_start(out=g.table, out_offset=bass.IndirectOffsetOnAxis(
            ap=g.edge_cell[:, b:b + 1].bitcast(U32), axis=0), in_=g.edge_add[:, b:b + 1], in_offset=None,
            compute_op=ALU.add, bounds_check=CELLS + T - 1).then_inc(g.scattered, 16)
    e.wait_ge(g.scattered, 16 * (blocks[-1] + 1))


def mix(nc, g, blocks):
    NORM = DH ** -0.25
    RATIO = M ** -0.5
    W2 = 2 * (DH + 1)
    with ExitStack() as ctx:
        sb = lambda n, s, d=F32: ctx.enter_context(nc.sbuf_tensor("mx_" + n, s, d))
        ps = lambda n, s: ctx.enter_context(nc.psum_tensor("mx_" + n, s, F32))
        sem = lambda n: g.sem("mx_" + n)
        wk, wq = sb("wk", [128, KT, 128]), sb("wq", [128, KT, 128])
        wo, wol = shared(nc, sb, ("mx_wo", [128, KT, D], F32), ("wol", [128, KT, D], F32R))
        proj2 = sb("proj2", [128, 2, 2, DH])
        fraw, fh, fl = sb("fraw", [128, M]), sb("fh", [128, M], F32R), sb("fl", [128, M], F32R)
        halves = sb("halves", [128, 128])
        ones2 = sb("ones2", [2, T])
        lin, sq = sb("lin", [128, N]), sb("sq", [128, N])
        kk, qq = sb("kk", [128, 2, N], F32R), sb("qq", [128, 2, N], F32R)
        head = [slice(0, DH), slice(DH, 128)]
        dk, dq = sb("dk", [T, NT, 2]), sb("dq", [T, NT, 2])
        kf, woh, _ = shared(nc, sb, ("mx_kf", [T, NT, 2 * M], F32), ("woh", [128, KT, D], F32R),
                            ("woh_rest", [128, NT * 2 * M - KT * D], F32))
        khalf = sb("khalf", [T, 2, 2])
        kmax, gmax, gdiag, kbias = sb("kmax", [T, 2]), sb("gmax", [2, 1]), sb("gdiag", [2, 2]), sb("kbias", [T, NT, 2])
        cx = sb("cx", [128, 2, 2 * W2])
        qm, nb, rc = sb("qm", [T, 2, 2]), sb("nb", [T, 2, 2]), sb("rc", [T, 2, 2])
        qf = sb("qf", [T, 3, 2 * M])
        qfT = sb("qfT", [128, 2, 4, T])
        mo = sb("mo", [T, NT, D])
        sh, sl = sb("sh", [128, 2, KT, T], F32R), sb("sl", [128, 2, KT, T], F32R)
        res = sb("res", [T, 2, D])
        LQ, DD, TT, CO = ps("LQ", [128, 3 * 512]), ps("DD", [128, 2, 512]), ps("TT", [128, 2, 512]), ps("CO", [128, 512])
        wk_in, wq_in, wo_in, pr_in = sem("wk_in"), sem("wq_in"), sem("wo_in"), sem("pr_in")
        pset, ptr, pdone, sp_ok = sem("pset"), sem("ptr"), sem("pdone"), sem("sp_ok")
        woh_ok, wol_ok = sem("woh_ok"), sem("wol_ok")
        klin, qlin, lin_out = sem("klin"), sem("qlin"), sem("lin_out")
        kdg, qdg, d_out = sem("kdg"), sem("qdg"), sem("d_out")
        kdd, kf_ok, kmax_ok, kmT, gd_ok, kmB, kb_ok = (sem(n) for n in ("kdd", "kf_ok", "kmax_ok", "kmT", "gd_ok", "kmB", "kb_ok"))
        ke_ok, kp_ok, cx_ok, cx_out = sem("ke_ok"), sem("kp_ok"), sem("cx_ok"), sem("cx_out")
        qdd, nb_ok, qe_ok, qp_ok, qtr, qfT_ok, out_ok, mo_ok = (
            sem(n) for n in ("qdd", "nb_ok", "qe_ok", "qp_ok", "qtr", "qfT_ok", "out_ok", "mo_ok"))
        otr, ost, olo, omm, ores = (sem(n) for n in ("otr", "ost", "olo", "omm", "ores"))
        sent = [sem("sent0"), sem("sent1")]
        kh_ok = sem("kh_ok")
        gmax_ok, qm_ok, rc_ok, lin_ok = sem("gmax_ok"), sem("qm_ok"), sem("rc_ok"), sem("lin_ok")
        tile = lambda t: slice(t * T, (t + 1) * T)

        def over_pairs(e, pair):
            with e.Fori(0, MP - 1) as m:
                pair(m, False)
            pair(MP - 1, True)

        with nc.Block() as block:
            @block.sync
            def _(sp):
                for c in range(2):
                    for d in range(2):
                        sp.dma_start(proj2[:, c, d], g.mix_proj[c * 128:(c + 1) * 128, :]).then_inc(pr_in, 16)
                for w, dram, into, used in ((wk, g.mix_Wk, wk_in, None), (wq, g.mix_Wq, wq_in, None)):
                    sp.dma_start(w[:], weight_view(dram)[:, :, 0:128]).then_inc(into, 16)
                sp.dma_start(wo[:], weight_view(g.mix_Wo)).then_inc(wo_in, 16)
                with sp.Fori(1, MP) as m:
                    sp.wait_ge(klin, m)
                    sp.dma_start(wk[:], weight_view(g.mix_Wk)[:, :, bass.ds(m * 128, 128)]).then_inc(wk_in, 16)
                    sp.wait_ge(qlin, m)
                    sp.dma_start(wq[:], weight_view(g.mix_Wq)[:, :, bass.ds(m * 128, 128)]).then_inc(wq_in, 16)
                for t in range(NT):
                    sp.wait_ge(ores, t + 1)
                    sp.dma_start(g.mix_out[tile(t), :], res[:, t % 2]).then_inc(sent[t % 2], 16)
                for s in sent:
                    sp.wait_ge(s, 16 * NT // 2)

            @block.gpsimd
            def _(e):
                e.memset(ones2[:], 1.0).then_inc(pset, 1)
                e.memset(halves[:], 0.0).then_inc(pset, 1)
                e.wait_ge(pset, 2)
                e.memset(halves[0:DH, 0:DH], 0.5).then_inc(pset, 1)
                e.memset(halves[DH:128, DH:128], 0.5).then_inc(pset, 1)
                e.wait_ge(pset, 4)
                scatter_counts(e, g, blocks)

            @block.tensor
            def _(e):
                e.wait_ge(pr_in, 64)
                for c in range(2):
                    ins = e.transpose(CO[:, c * 128:(c + 1) * 128], proj2[:, c].rearrange("p a b -> p (a b)"), g.ident[:])
                ins.then_inc(ptr, 1)
                e.wait_ge(pdone, 3)
                e.wait_ge(pset, 4)

                def linear(w, steps=range(3 * KT)):
                    for s in steps:
                        (a, n), k = CHUNKS[s // KT], s % KT
                        ins = e.matmul(LQ[:, a:a + n], w[:, k], g.xnT[:, k, a:a + n], start=(k == 0), stop=(k == KT - 1))
                    return ins

                def features(x, t, bank):
                    for h in range(2):
                        for f in (fh, fl):
                            ins = e.matmul(DD[0:T, bank, h * M:(h + 1) * M], x[:, h, tile(t)], f[:], start=(f is fh), stop=(f is fl))
                    return ins

                def norms(j, bank):
                    for c in range(2):
                        ins = e.matmul(DD[0:T, bank, c * 128:(c + 1) * 128], sq[:, tile(2 * j + c)], halves[:],
                                       start=True, stop=True)
                    return ins

                def pair(m, last):
                    e.wait_ge(lin_out, m * 2 + 1)
                    for j in range(5):
                        e.wait_ge(qe_ok, m * NT) if j < 2 else e.wait_ge(d_out, m * 10 + j - 1)
                        norms(j, j % 2).then_inc(kdg, 1)
                    for t in range(NT):
                        e.wait_ge(d_out, m * 10 + 4 + t) if t < 2 else e.wait_ge(kf_ok, m * NT + t - 1)
                        if t == 0:
                            e.wait_ge(sp_ok, m * 8 + 4)
                        features(kk, t, (t + 1) % 2).then_inc(kdd, 1)
                    e.wait_ge(wq_in, m * 16 + 16)
                    linear(wq, range(0, 7))
                    e.wait_ge(kmax_ok, m + 1)
                    e.wait_ge(mo_ok, m * NT)
                    e.transpose(CO[0:2, 0:T], kmax[:], g.ident[0:T, 0:T]).then_inc(kmT, 1)
                    linear(wq, range(7, 9))
                    e.wait_ge(gd_ok, m + 1)
                    e.matmul(CO[0:T, 0:2], ones2[:], gdiag[:], start=True, stop=True).then_inc(kmB, 1)
                    linear(wq, range(9, 18)).then_inc(qlin, 1)
                    for h in range(2):
                        if h == 1:
                            e.wait_ge(lin_out, m * 2 + 2)
                            for j in range(5):
                                e.wait_ge(kf_ok, m * NT + 9 + j) if j < 2 else e.wait_ge(d_out, m * 10 + 5 + j - 1)
                                norms(j, (j + 1) % 2).then_inc(qdg, 1)
                        e.wait_ge(qfT_ok, m * NT)
                        for c in range(2):
                            for t in range(NT):
                                if h == 0 and c == 0 and t % 5 == 0:
                                    e.wait_ge(kp_ok, m * 2 + t // 5 + 1)
                                ins = e.matmul(TT[:, h, c * W2:(c + 1) * W2], kf[:, t, h * M + c * 128:h * M + (c + 1) * 128],
                                               g.v[:, t, bass.ds(m * W2, W2)], start=(t == 0), stop=(t == NT - 1))
                        ins.then_inc(cx_ok, 1)
                    for s in range(NT + 3):
                        if s < NT:
                            e.wait_ge(d_out, m * 10 + 9 + s) if s < 2 else e.wait_ge(qe_ok, m * NT + s - 1)
                            if s == 0:
                                e.wait_ge(sp_ok, m * 8 + 8)
                            features(qq, s, s % 2).then_inc(qdd, 1)
                        t = s - 2
                        if 0 <= t < NT:
                            e.wait_ge(qp_ok, m * NT + t + 1)
                            e.wait_ge(cx_out, m * 2 + 2) if t < 2 else e.wait_ge(qfT_ok, m * NT + t - 1)
                            for c in range(4):
                                ins = e.transpose(TT[:, t % 2, c * T:(c + 1) * T], qf[:, t % 3, c * 128:(c + 1) * 128],
                                                  g.ident[0:T, 0:T])
                            ins.then_inc(qtr, 1)
                        t = s - 3
                        if t >= 0:
                            e.wait_ge(qfT_ok, m * NT + t + 1)
                            e.wait_ge(mo_ok, m * NT + t)
                            for h in range(2):
                                for c in range(2):
                                    ins = e.matmul(CO[0:T, h * W2:(h + 1) * W2], qfT[:, t % 2, 2 * h + c],
                                                   cx[:, h, c * W2:(c + 1) * W2], start=(c == 0), stop=(c == 1))
                            ins.then_inc(out_ok, 1)
                        if not last and s < 9:
                            if s == 0:
                                e.wait_ge(wk_in, m * 16 + 32)
                            ins = linear(wk, range(2 * s, 2 * s + 2))
                            if s == 8:
                                ins.then_inc(klin, 1)

                e.wait_ge(wk_in, 16)
                linear(wk).then_inc(klin, 1)
                over_pairs(e, pair)
                e.wait_ge(wo_in, 16)
                e.wait_ge(mo_ok, MP * NT)
                e.wait_ge(qfT_ok, MP * NT)
                for t in range(NT + 1):
                    if t < NT:
                        if t > 0:
                            e.wait_ge(olo, t)
                        for k in range(KT):
                            ins = e.transpose(LQ[:, k // 3 * 512 + k % 3 * T:k // 3 * 512 + (k % 3 + 1) * T],
                                              mo[:, t, k * 128:(k + 1) * 128], g.ident[0:T, 0:T])
                        ins.then_inc(otr, 1)
                    if t > 0:
                        u = t - 1
                        bank = (DD, TT)[u % 2]
                        e.wait_ge(olo, u + 1)
                        if u >= 2:
                            e.wait_ge(ores, u - 1)
                        for c in range(2):
                            for k in range(KT):
                                if u == 0 and c == 0:
                                    e.wait_ge(wol_ok, k + 1)
                                for x, w in ((sh, woh), (sh, wol), (sl, woh)):
                                    ins = e.matmul(bank[0:T, c, 0:HALF], x[:, u % 2, k], w[:, k, c * HALF:(c + 1) * HALF],
                                                   start=(k == 0 and x is sh and w is woh), stop=(k == KT - 1 and x is sl))
                        ins.then_inc(omm, 1)

            @block.scalar
            def _(e):
                def linear_out(m, which):
                    e.wait_ge((klin, qlin)[which], m + 1)
                    e.wait_ge(sp_ok, m * 8 + which * 4)
                    e.activation(lin[:], LQ[:, 0:N], ACT.Copy, scale=NORM).then_inc(lin_ok, 1)
                    e.activation(sq[:], LQ[:, 0:N], ACT.Square, scale=NORM).then_inc(lin_out, 1)

                def pair(m, last):
                    for t in range(NT):
                        e.wait_ge(kdd, m * NT + t + 1)
                        e.activation(kf[:, t], DD[0:T, (t + 1) % 2, :], ACT.Copy).then_inc(kf_ok, 1)
                    e.wait_ge(kb_ok, m + 1)
                    for t in range(NT):
                        for h in range(2):
                            ins = e.activation(kf[:, t, h * M:(h + 1) * M], kf[:, t, h * M:(h + 1) * M], ACT.Exp,
                                               bias=kbias[:, t, h:h + 1])
                        if t % 5 == 4:
                            ins.then_inc(ke_ok, 1)
                    linear_out(m, 1)
                    for s in range(NT + 2):
                        if s < NT:
                            e.wait_ge(nb_ok, m * NT + s + 1)
                            e.wait_ge(qtr, m * NT + max(s - 2, 0))
                            for h in range(2):
                                ins = e.activation(qf[:, s % 3, h * M:(h + 1) * M], DD[0:T, s % 2, h * M:(h + 1) * M],
                                                   ACT.Exp, bias=nb[:, s % 2, h:h + 1])
                            ins.then_inc(qe_ok, 1)
                        t = s - 2
                        if t >= 0:
                            e.wait_ge(qtr, m * NT + t + 1)
                            e.wait_ge(out_ok, m * NT + max(t - 1, 0))
                            e.activation(qfT[:, t % 2].rearrange("p c t -> p (c t)"), TT[:, t % 2, 0:4 * T],
                                         ACT.Copy).then_inc(qfT_ok, 1)
                        if s == NT - 1 and not last:
                            linear_out(m + 1, 0)

                linear_out(0, 0)
                over_pairs(e, pair)
                e.wait_ge(wo_in, 16)
                e.wait_ge(cx_ok, 2 * MP)
                for k in range(KT):
                    e.activation(woh[:, k], wo[:, k], ACT.Copy).then_inc(woh_ok, 1)
                for t in range(NT):
                    e.wait_ge(otr, t + 1)
                    if t >= 2:
                        e.wait_ge(omm, t - 1)
                    e.activation(sh[:, t % 2].rearrange("p (c k) t -> p c (k t)", c=2),
                                 LQ[:, 0:1024].rearrange("p (c n) -> p c n", c=2)[:, :, 0:3 * T], ACT.Copy).then_inc(ost, 1)

            @block.vector
            def _(e):
                e.wait_ge(ptr, 1)
                e.wait_ge(pset, 4)
                e.tensor_copy(fraw[:], CO[:, 0:M]).then_inc(pdone, 1)
                e.wait_ge(pdone, 1)
                e.tensor_copy(fh[:], fraw[:]).then_inc(pdone, 1)
                e.wait_ge(pdone, 2)
                e.tensor_tensor(fl[:], fraw[:], fh[:].bitcast(F32), ALU.subtract).then_inc(pdone, 1)

                def rescale(m, c):
                    e.wait_ge(ke_ok, m * 2 + c + 1)
                    e.tensor_scalar(kf[:, 5 * c:5 * c + 5], kf[:, 5 * c:5 * c + 5], MIX_EPS, RATIO,
                                    ALU.add, ALU.mult).then_inc(kp_ok, 1)

                def split(dst, m, which):
                    e.wait_ge(lin_ok, m * 2 + which + 1)
                    for h in range(2):
                        e.tensor_copy(dst[head[h], h], lin[head[h]]).then_inc(sp_ok, 1)
                    e.wait_ge(sp_ok, m * 8 + which * 4 + 2)
                    for h in range(2):
                        e.tensor_tensor(dst[head[1 - h], h], lin[head[h]], dst[head[h], h].bitcast(F32), ALU.subtract).then_inc(sp_ok, 1)

                diag_of = lambda bank: DD[0:T, bank, 0:256].rearrange("p (t h r) -> p t h r", t=2, h=2)[:, :, :, 0]
                def pair(m, last):
                    for j in range(5):
                        e.wait_ge(kdg, m * 5 + j + 1)
                        e.tensor_copy(dk[:, 2 * j:2 * j + 2, :], diag_of(j % 2)).then_inc(d_out, 1)
                    for c in range(2):
                        e.wait_ge(kf_ok, m * NT + 5 * c + 5)
                        e.tensor_reduce(khalf[:, c], kf[:, 5 * c:5 * c + 5].rearrange("p t (h m) -> p h t m", h=2), AX.XY,
                                        ALU.max).then_inc(kh_ok, 1)
                    e.wait_ge(kh_ok, m * 2 + 2)
                    e.tensor_tensor(kmax[:], khalf[:, 0], khalf[:, 1], ALU.max).then_inc(kmax_ok, 1)
                    e.wait_ge(kmT, m + 1)
                    e.tensor_reduce(gmax[:], CO[0:2, 0:T], AX.X, ALU.max).then_inc(gmax_ok, 1)
                    e.wait_ge(gmax_ok, m + 1)
                    e.tensor_scalar(gdiag[:], g.ident[0:2, 0:2], gmax[:, 0:1], None, ALU.mult).then_inc(gd_ok, 1)
                    e.wait_ge(kmB, m + 1)
                    e.wait_ge(d_out, m * 10 + 5)
                    e.scalar_tensor_tensor(out=kbias[:], in0=dk[:], scalar=-1.0,
                                           in1=CO[0:T, 0:2].unsqueeze(1).to_broadcast([T, NT, 2]),
                                           op0=ALU.mult, op1=ALU.subtract).then_inc(kb_ok, 1)
                    rescale(m, 0)
                    rescale(m, 1)
                    split(qq, m, 1)
                    for j in range(5):
                        e.wait_ge(qdg, m * 5 + j + 1)
                        e.tensor_copy(dq[:, 2 * j:2 * j + 2, :], diag_of((j + 1) % 2)).then_inc(d_out, 1)
                    for h in range(2):
                        e.wait_ge(cx_ok, m * 2 + h + 1)
                        e.tensor_copy(cx[:, h], TT[:, h, 0:2 * W2]).then_inc(cx_out, 1)
                    e.wait_ge(d_out, m * 10 + 10)
                    for s in range(NT + 3):
                        if s < NT:
                            e.wait_ge(qdd, m * NT + s + 1)
                            e.tensor_reduce(qm[:, s % 2], DD[0:T, s % 2, :].rearrange("p (h m) -> p h m", h=2),
                                            AX.X, ALU.max).then_inc(qm_ok, 1)
                            e.wait_ge(qm_ok, m * NT + s + 1)
                            e.scalar_tensor_tensor(out=nb[:, s % 2], in0=qm[:, s % 2], scalar=-1.0, in1=dq[:, s],
                                                   op0=ALU.mult, op1=ALU.subtract).then_inc(nb_ok, 1)
                        t = s - 1
                        if 0 <= t < NT:
                            e.wait_ge(qe_ok, m * NT + t + 1)
                            e.tensor_scalar(qf[:, t % 3], qf[:, t % 3], MIX_EPS, RATIO, ALU.add, ALU.mult).then_inc(qp_ok, 1)
                        t = s - 3
                        if t >= 0:
                            e.wait_ge(out_ok, m * NT + t + 1)
                            heads = CO[0:T, 0:2 * 3 * (DH + 1)].rearrange("p (h c) -> p h c", h=2)
                            e.reciprocal(rc[:, t % 2], heads[:, :, DH]).then_inc(rc_ok, 1)
                            e.wait_ge(rc_ok, m * NT + t + 1)
                            e.tensor_tensor(mo[:, t, bass.ds(m * 128, 128)].rearrange("p (h c) -> p h c", h=2),
                                            heads[:, :, 0:DH], rc[:, t % 2].unsqueeze(2).to_broadcast([T, 2, DH]),
                                            ALU.mult).then_inc(mo_ok, 1)
                        if s == NT - 1 and not last:
                            split(kk, m + 1, 0)

                split(kk, 0, 0)
                over_pairs(e, pair)
                for k in range(KT):
                    e.wait_ge(woh_ok, k + 1)
                    e.tensor_tensor(wol[:, k], wo[:, k], woh[:, k].bitcast(F32), ALU.subtract).then_inc(wol_ok, 1)

                def low(t):
                    e.wait_ge(ost, t + 1)
                    e.tensor_tensor(sl[:, t % 2].rearrange("p (c k) t -> p c (k t)", c=2),
                                    LQ[:, 0:1024].rearrange("p (c n) -> p c n", c=2)[:, :, 0:3 * T],
                                    sh[:, t % 2].rearrange("p (c k) t -> p c (k t)", c=2).bitcast(F32), ALU.subtract).then_inc(olo, 1)

                low(0)
                for t in range(NT):
                    if t + 1 < NT:
                        low(t + 1)
                    e.wait_ge(omm, t + 1)
                    if t >= 2:
                        e.wait_ge(sent[t % 2], 16 * (t // 2))
                    e.tensor_copy(res[:, t % 2].rearrange("p (c n) -> p c n", c=2),
                                  (DD, TT)[t % 2][0:T, :, 0:HALF]).then_inc(ores, 1)


def lift(nc, g):
    with ExitStack() as ctx:
        sb = lambda n, s, d=F32: ctx.enter_context(nc.sbuf_tensor("li_" + n, s, d))
        ps = lambda n, s: ctx.enter_context(nc.psum_tensor("li_" + n, s, F32))
        sem = lambda n: g.sem("li_" + n)
        tile = lambda t: slice(t * T, (t + 1) * T)
        high_b = sb("high_b", [128, KT, D], F32R)
        xl = sb("xl", [128, 2, KT, T], F32R)
        sb("rest", [128, KT * N - KT * D - 2 * KT * T])
        wa = sb("wa", [128, 2, KT, 128])
        bah = sb("bah", [128, KT])
        x1T = sb("x1T", [128, KT, N])
        w, wlow = shared(nc, sb, ("li_w", [128, 2, KT, D], F32), ("wlow", [128, 2, KT, D], F32R))
        arow = sb("arow", [128, 2, D])
        prod = sb("prod", [128, KT // 2, D])
        watt = sb("watt", [128, KT, 2 * GI])
        rows = sb("rows", [2 * GI, N])
        cnt = sb("cnt", [T, 2, N])
        maskT = sb("maskT", [T, NT, N], BF16)
        srow = cnt
        high_a = sb("high_a", [128, KT, D], F32R)
        HIGH = (high_a, high_b, high_a)
        junk = sb("junk", [T, N])
        top, topd = sb("top", [T, 2, NT]), sb("topd", [T, NT, GI])
        m1, m2, uv = sb("m1", [T, NT, GI]), sb("m2", [T, NT, GI]), sb("uv", [T, NT, 2 * GI])
        xs = sb("xs", [128, 2, KT, T], F32R)
        ho = sb("ho", [T, 2, D])
        A, B, C = ps("A", [128, 3 * 512]), ps("B", [128, 3 * 512]), ps("C", [128, 2, 512])
        wa_in = [sem("wa_in0"), sem("wa_in1")]
        w_in = [sem("w_in0"), sem("w_in1")]
        ar_in = [sem("ar_in0"), sem("ar_in1")]
        cnt_in = [sem("cnt_in0"), sem("cnt_in1")]
        srow_in = [sem("srow_in0"), sem("srow_in1")]
        ho_sent = [sem("ho_sent0"), sem("ho_sent1")]
        b_in, rows_sent, uv_sent = sem("b_in"), sem("rows_sent"), sem("uv_sent")
        x1_mm, x1_ok, watt_ok, rows_mm, rows_ok = (sem(n) for n in ("x1_mm", "x1_ok", "watt_ok", "rows_mm", "rows_ok"))
        loop_ok, mt_mm, mt_ok, col_mm, col_ok = (sem(n) for n in ("loop_ok", "mt_mm", "mt_ok", "col_mm", "col_ok"))
        seg_ok, uv_ok, uvt_mm, uvt_ok = (sem(n) for n in ("seg_ok", "uv_ok", "uvt_mm", "uvt_ok"))
        xs_ok, h_mm, h_out, dve = (sem(n) for n in ("xs_ok", "h_mm", "h_out", "dve"))
        hi_ok, wl_ok, started = sem("hi_ok"), sem("wl_ok"), sem("started")
        ORDER = (2, 1, 0)
        W = (g.gnn_W0, g.gnn_W1, g.gnn_W2)
        AV = ((g.gnn_a_src0, g.gnn_a_src1, g.gnn_a_src2), (g.gnn_a_dst0, g.gnn_a_dst1, g.gnn_a_dst2))

        with nc.Block() as block:
            @block.sync
            def _(sp):
                sp.dma_start(bah[:], g.gnn_b_ah.rearrange("(k p) -> p k", p=128), allow_slow_non_contiguous=True).then_inc(b_in, 16)
                for i in range(2):
                    sp.dma_start(w[:, i], weight_view(W[i])).then_inc(w_in[i], 16)
                for i in range(GL):
                    for c in range(2):
                        if i > 0:
                            sp.wait_ge(watt_ok, 4 * i + 2 * c - 2)
                        sp.dma_start(arow[:, c], AV[c][i].rearrange("h c -> (h c)").partition_broadcast(128)).then_inc(ar_in[c], 16)
                    if i == 1:
                        sp.wait_ge(watt_ok, 4)
                        sp.dma_start(w[:, 0], weight_view(W[2])).then_inc(w_in[0], 16)
                for s in range(NT):
                    if s >= 2:
                        sp.wait_ge(mt_mm, s - 1)
                    sp.dma_start(cnt[:, s % 2], g.table[s * T * N:(s + 1) * T * N].rearrange("(p n) o -> p (n o)", p=T)
                                 ).then_inc(cnt_in[s % 2], 16)
                sp.wait_ge(rows_ok, 1)
                sp.dma_start(g.rows, rows[:]).then_inc(rows_sent, 16)
                sp.wait_ge(rows_sent, 16)
                sp.wait_ge(mt_mm, NT)
                with sp.Fori(0, GI // 2) as i:
                    for p in range(2):
                        sp.wait_ge(seg_ok, i * 2 + p)
                        sp.dma_start(srow[:, p], g.rows[bass.ds(i * 2 + p, 1), :].rearrange("a n -> (a n)").partition_broadcast(T)
                                     ).then_inc(srow_in[p], 16)
                sp.wait_ge(uvt_ok, 1)
                sp.dma_start(g.uv, rows[:]).then_inc(uv_sent, 16)
                sp.wait_ge(uv_sent, 16)

            @block.gpsimd
            def _(e):
                for k in range(KT):
                    if k >= 2:
                        e.wait_ge(x1_mm, k - 1)
                    e.dma_start(wa[:, k % 2], weight_view(g.gnn_W_ah)[:, :, k * 128:(k + 1) * 128]).then_inc(wa_in[k % 2], 16)
                e.wait_ge(x1_ok, KT)
                for l in range(GL):
                    with e.Fori(0, NT // 2) as i:
                        for p in range(2):
                            n = i * 2 + (p + l * NT)
                            cols = bass.ds((i * 2 + p) * T, T)
                            e.wait_ge(h_mm, n)
                            e.tensor_copy(xs[:, p], x1T[:, :, cols]).then_inc(xs_ok, 1)
                            e.wait_ge(xs_ok, 2 * n + 1)
                            e.sem_inc(started, 1)
                            e.tensor_tensor(xl[:, p], x1T[:, :, cols], xs[:, p].bitcast(F32), ALU.subtract).then_inc(xs_ok, 1)

            @block.tensor
            def _(e):
                for k in range(KT):
                    e.wait_ge(wa_in[k % 2], 16 * (k // 2 + 1))
                    if k >= 2:
                        e.wait_ge(x1_ok, k - 1)
                    bank = (A, B)[k % 2]
                    for a, n in CHUNKS:
                        for kk in range(KT):
                            ins = e.matmul(bank[:, a:a + n], wa[:, k % 2, kk], g.xnT[:, kk, a:a + n],
                                           start=(kk == 0), stop=(kk == KT - 1))
                    ins.then_inc(x1_mm, 1)
                e.wait_ge(watt_ok, 4 * GL)
                e.wait_ge(x1_ok, KT)
                for a, n in CHUNKS:
                    for k in range(KT):
                        ins = e.matmul(A[0:2 * GI, a:a + n], watt[:, k], x1T[:, k, a:a + n], start=(k == 0), stop=(k == KT - 1))
                ins.then_inc(rows_mm, 1)
                for s in range(NT):
                    bank = (B, A)[s % 2]
                    e.wait_ge(loop_ok, s + 1)
                    if s == 1:
                        e.wait_ge(rows_ok, 1)
                    if s >= 2:
                        e.wait_ge(mt_ok, s - 1)
                    for d in range(NT):
                        ins = e.transpose(bank[0:T, d // 4 * 512 + d % 4 * T:d // 4 * 512 + (d % 4 + 1) * T],
                                          cnt[:, s % 2, tile(d)], g.ident[0:T, 0:T])
                    ins.then_inc(mt_mm, 1)
                for t in range(NT):
                    ins = e.transpose(C[0:T, 0, t * 2 * GI:(t + 1) * 2 * GI], rows[:, tile(t)], g.ident[0:2 * GI, 0:2 * GI])
                ins.then_inc(col_mm, 1)
                e.wait_ge(mt_ok, NT)
                e.sem_inc(h_mm, 1)
                for l, layer in enumerate(ORDER):
                    e.wait_ge(wl_ok, l + 1)
                    low = wlow[:, l % 2]
                    with e.Fori(0, NT // 2) as i:
                        for p in range(2):
                            n = i * 2 + (p + l * NT)
                            bank = (A, B)[p]
                            e.wait_ge(xs_ok, 2 * n + 2)
                            e.wait_ge(h_out, n)
                            for c in range(2):
                                for k in range(KT):
                                    for x, y in ((xs, HIGH[l]), (xs, low), (xl, HIGH[l])):
                                        ins = e.matmul(bank[0:T, c * 512:c * 512 + HALF], x[:, p, k], y[:, k, c * HALF:(c + 1) * HALF],
                                                       start=(k == 0 and x is xs and y is HIGH[l]), stop=(k == KT - 1 and x is xl))
                            ins.then_inc(h_mm, 1)
                e.wait_ge(uv_ok, 1)
                e.wait_ge(h_out, GL * NT + 1)
                for t in range(NT):
                    ins = e.transpose(A[0:2 * GI, t // 4 * 512 + t % 4 * T:t // 4 * 512 + (t % 4 + 1) * T], uv[:, t],
                                      g.ident[0:T, 0:T])
                ins.then_inc(uvt_mm, 1)

            @block.scalar
            def _(e):
                e.wait_ge(b_in, 16)
                for k in range(KT):
                    e.wait_ge(x1_mm, k + 1)
                    e.activation(x1T[:, k], (A, B)[k % 2][:, 0:N], ACT.Relu, bias=bah[:, k:k + 1]).then_inc(x1_ok, 1)
                e.wait_ge(rows_mm, 1)
                e.activation(rows[:], A[0:2 * GI, 0:N], ACT.Copy).then_inc(rows_ok, 1)
                e.sem_inc(h_out, 1)

                def high(l):
                    e.wait_ge(w_in[l % 2], (32, 16, 48)[l])
                    e.activation(HIGH[l][:], w[:, l % 2], ACT.Copy).then_inc(hi_ok, 1)

                high(0)
                high(1)
                for l, layer, start, end in ((0, 2, 0, 5), (1, 1, 0, 3), (1, 1, 3, 5), (2, 0, 0, 5)):
                    if start > 0:
                        high(2)
                    with e.Fori(start, end) as i:
                        for p in range(2):
                            n = i * 2 + (p + l * NT)
                            e.wait_ge(h_mm, n + 2)
                            e.wait_ge(ho_sent[p], i * 16 + l * 16 * NT // 2)
                            e.activation(ho[:, p].rearrange("p (c n) -> p c n", c=2),
                                         (A, B)[p][0:T, 0:1024].rearrange("p (c n) -> p c n", c=2)[:, :, 0:HALF],
                                         ACT.Copy).then_inc(h_out, 1)
                            e.wait_ge(h_out, n + 2)
                            e.dma_start(g.h[layer * GH:(layer + 1) * GH, bass.ds((i * 2 + p) * T, T), :].rearrange("h p c -> p h c"),
                                        ho[:, p].rearrange("p (h c) -> p h c", h=GH)).then_inc(ho_sent[p], 16)
                    if l == 0:
                        e.wait_ge(h_mm, NT + 1)
                        e.dma_start(w[:, 0], weight_view(W[0])).then_inc(w_in[0], 16)
                for s in ho_sent:
                    e.wait_ge(s, 16 * GL * NT // 2)
                e.wait_ge(uvt_mm, 1)
                for b, (t0, t1) in enumerate(((0, 4), (4, 8), (8, 10))):
                    ins = e.activation(rows[:, t0 * T:t1 * T], A[0:2 * GI, b * 512:b * 512 + (t1 - t0) * T], ACT.Copy)
                ins.then_inc(uvt_ok, 1)

            @block.vector
            def _(e):
                seq = Tally(e, dve)

                def low(l):
                    e.wait_ge(hi_ok, l + 1)
                    e.tensor_tensor(wlow[:, l % 2], w[:, l % 2], HIGH[l][:].bitcast(F32), ALU.subtract).then_inc(wl_ok, 1)

                for i in range(GL):
                    e.wait_ge(w_in[i % 2], 32 if i == 2 else 16)
                    for c in range(2):
                        e.wait_ge(ar_in[c], 16 * (i + 1))
                        for hf in range(2):
                            ks = slice(hf * KT // 2, (hf + 1) * KT // 2)
                            seq.step(e.tensor_tensor(prod[:], w[:, i % 2, ks], arow[:, c].unsqueeze(1).to_broadcast([128, KT // 2, D]),
                                                     ALU.mult))
                            ins = e.tensor_reduce(watt[:, ks, c * GI + i * GH:c * GI + (i + 1) * GH],
                                                  prod[:].rearrange("p k (h c) -> p k h c", h=GH), AX.X, ALU.add)
                            ins.then_inc(watt_ok, 1)
                            e.wait_ge(watt_ok, 4 * i + 2 * c + hf + 1)
                for s in range(NT + 1):
                    if s < NT:
                        e.wait_ge(cnt_in[s % 2], 16 * (s // 2 + 1))
                        e.tensor_tensor(cnt[:, s % 2, tile(s)], cnt[:, s % 2, tile(s)], g.ident[0:T, 0:T], ALU.add).then_inc(loop_ok, 1)
                    if s > 0:
                        bank = (B, A)[(s - 1) % 2]
                        e.wait_ge(mt_mm, s)
                        for b, (d0, d1) in enumerate(((0, 4), (4, 8), (8, 10))):
                            ins = e.tensor_scalar(maskT[:, d0:d1, tile(s - 1)],
                                                  bank[0:T, b * 512:b * 512 + (d1 - d0) * T].rearrange("p (d s) -> p d s", s=T),
                                                  0.0, NEG, ALU.is_equal, ALU.mult)
                        ins.then_inc(mt_ok, 1)
                    if s in (5, 7):
                        low((s - 5) // 2)
                e.wait_ge(col_mm, 1)
                seq.step(e.tensor_copy(g.asad[:].rearrange("p t c -> p (t c)"), C[0:T, 0, 0:NT * 2 * GI]))
                e.wait_ge(mt_ok, NT)
                e.sem_inc(seg_ok, 1)
                for i in range(GI):
                    if i == 7:
                        low(2)
                    e.wait_ge(srow_in[i % 2], 16 * (i // 2 + 1))
                    for d in range(NT):
                        seq.step(e.tensor_tensor_reduce(junk[:], srow[:, i % 2], maskT[:, d], 1.0, NEG, ALU.add, ALU.max,
                                                        top[:, i % 2, d:d + 1]))
                    e.tensor_copy(topd[:, :, i:i + 1], top[:, i % 2].unsqueeze(2)).then_inc(seg_ok, 1)
                e.wait_ge(seg_ok, GI + 1)
                s_term, d_term = g.asad[:, :, 0:GI], g.asad[:, :, GI:2 * GI]
                seq.mark(e.tensor_scalar(g.as02[:], s_term, 0.2, None, ALU.mult))
                seq.step(e.tensor_tensor(m1[:], topd[:], d_term, ALU.add))
                seq.step(e.tensor_scalar(m2[:], m1[:], 0.2, None, ALU.mult))
                seq.step(e.tensor_tensor(m1[:], m1[:], m2[:], ALU.max))
                seq.mark(e.tensor_tensor(uv[:, :, 0:GI], d_term, m1[:], ALU.subtract))
                seq.settle()
                e.scalar_tensor_tensor(out=uv[:, :, GI:2 * GI], in0=d_term, scalar=0.2, in1=m1[:], op0=ALU.mult,
                                       op1=ALU.subtract).then_inc(uv_ok, 1)


def graph(nc, g):
    RING = 4
    HC = GC + 1
    STEPS = 2 * NT
    LAST = GI // 2 - 1

    def over_pairs(e, pair):
        pair(0)
        with e.Fori(1, LAST) as i:
            pair(i)
        pair(LAST)

    first = lambda i: isinstance(i, int) and i == 0
    last = lambda i: isinstance(i, int) and i == LAST
    with ExitStack() as ctx:
        sb = lambda n, s, d=F32: ctx.enter_context(nc.sbuf_tensor("gr_" + n, s, d))
        ps = lambda n, s: ctx.enter_context(nc.psum_tensor("gr_" + n, s, F32))
        sem = lambda n: g.sem("gr_" + n)
        tile = lambda t: slice(t * T, (t + 1) * T)
        cnt = sb("cnt", [T, NT, N])
        ub, vb = sb("ub", [T, 2, N]), sb("vb", [T, 2, N])
        h = sb("h", [T, 2, NT, HC])
        ring = sb("ring", [T, RING, N])
        bias = sb("bias", [T, GI * GC])
        node = sb("node", [T, 2, NT, GC])
        raw = sb("raw", [T, NT, HC])
        den, rec = sb("den", [T, NT]), sb("rec", [T, NT])
        acc = ps("acc", [128, 5, 512])
        cnt_in, b_in = [sem(f"cnt_in{q}") for q in range(NT // 2)], sem("b_in")
        started = sem("started")
        den_ok, rec_ok, sc_ok, bi_ok = sem("den_ok"), sem("rec_ok"), sem("sc_ok"), sem("bi_ok")
        uv_in = [sem("uv_in0"), sem("uv_in1")]
        h_in = [sem("h_in0"), sem("h_in1")]
        sent = [sem("sent0"), sem("sent1")]
        ones_ok, loop_ok = sem("ones_ok"), sem("loop_ok")
        a_ok, t_ok, e_ok, p_ok, mm, acc_out, node_ok, dve = (
            sem(n) for n in ("a_ok", "t_ok", "e_ok", "p_ok", "mm", "acc_out", "node_ok", "dve"))

        with nc.Block() as block:
            @block.sync
            def _(sp):
                def fetch(n, p):
                    sp.dma_start(ub[:, p], g.uv[bass.ds(n, 1), :].rearrange("a n -> (a n)").partition_broadcast(T)).then_inc(uv_in[p], 16)
                    sp.dma_start(vb[:, p], g.uv[bass.ds(n + GI, 1), :].rearrange("a n -> (a n)").partition_broadcast(T)).then_inc(uv_in[p], 16)
                    sp.dma_start(h[:, p, :, 0:GC], g.h[bass.ds(n, 1)].rearrange("a (t p) c -> p (a t) c", p=T)).then_inc(h_in[p], 16)

                fetch(0, 0)
                for q in range(NT // 2):
                    sp.dma_start(cnt[:, 2 * q:2 * q + 2], g.table[2 * q * T * N:2 * (q + 1) * T * N].rearrange(
                        "(t p n) o -> p t (n o)", p=T, n=N)).then_inc(cnt_in[q], 16)
                for i, b in enumerate((g.gnn_b0, g.gnn_b1, g.gnn_b2)):
                    sp.dma_start(bias[:, i * D:(i + 1) * D], b.partition_broadcast(T)).then_inc(b_in, 16)
                fetch(1, 1)
                with sp.Fori(0, GI // 2 - 1) as i:
                    for p in range(2):
                        sp.wait_ge(mm, (i * 2 + (p + 1)) * NT + RING)
                        fetch(i * 2 + p + 2, p)

            @block.gpsimd
            def _(e):
                e.memset(h[:, :, :, GC:HC], 1.0).then_inc(ones_ok, 1)
                nodes = g.node.rearrange("(t p) (i c) -> p t i c", p=T, c=GC)
                e.wait_ge(b_in, 48)
                with e.Fori(0, GI // 2) as i:
                    for p in range(2):
                        n = i * 2 + p
                        e.wait_ge(sc_ok, n + 1)
                        e.tensor_tensor(node[:, p], node[:, p], bias[:, bass.ds(n * GC, GC)].unsqueeze(1).to_broadcast([T, NT, GC]),
                                        ALU.add).then_inc(bi_ok, 1)
                        e.wait_ge(bi_ok, n + 1)
                        e.sem_inc(started, 1)
                        e.tensor_scalar(node[:, p], node[:, p], 0.0, None, ALU.max).then_inc(node_ok, 1)
                        e.wait_ge(node_ok, n + 1)
                        e.sem_inc(started, 1)
                        e.dma_start(nodes[:, :, bass.ds(n, 1), :].rearrange("p t i c -> p t (i c)"), node[:, p]).then_inc(sent[p], 16)
                for s in sent:
                    e.wait_ge(s, 16 * GI // 2)

            @block.scalar
            def _(e):
                def sums(i, j):
                    p, s = j // NT, j % NT
                    if s == 0:
                        e.wait_ge(uv_in[p], i * 32 + 32)
                    e.wait_ge(mm, i * STEPS + j + 1)
                    e.activation(ring[:, j % RING], ub[:, p], ACT.Identity, bias=g.asad[:, s, bass.ds(i * 2 + p, 1)]).then_inc(a_ok, 1)

                def take(n):
                    e.wait_ge(mm, n * NT + NT + RING)
                    if not (isinstance(n, int) and n == 0):
                        e.wait_ge(sc_ok, n)
                    for b in range(5):
                        e.activation(raw[:, 2 * b:2 * b + 2], acc[0:T, b].rearrange("p (d c) -> p d c", d=2)[:, :, 0:HC],
                                     ACT.Copy).then_inc(acc_out, 1)

                def pair(i):
                    for j in range(STEPS):
                        if j + 1 < STEPS:
                            sums(i, j + 1)
                        elif not last(i):
                            sums(i + 1, 0)
                        e.wait_ge(t_ok, i * STEPS + j + 1)
                        e.activation(ring[:, j % RING], ring[:, j % RING], ACT.Exp).then_inc(e_ok, 1)
                        if j == 1 and not first(i):
                            take(i * 2 - 1)
                        if j == NT + 1:
                            take(i * 2)
                    if last(i):
                        take(2 * LAST + 1)

                sums(0, 0)
                over_pairs(e, pair)

            @block.vector
            def _(e):
                def bound(i, j):
                    e.wait_ge(a_ok, i * STEPS + j + 1)
                    e.scalar_tensor_tensor(out=ring[:, j % RING], in0=vb[:, j // NT], scalar=g.as02[:, j % NT, bass.ds(i * 2 + j // NT, 1)],
                                           in1=ring[:, j % RING], op0=ALU.add, op1=ALU.max).then_inc(t_ok, 1)

                def scale(n, p, turns):
                    e.wait_ge(acc_out, (n + 2) * 5)
                    e.tensor_scalar(den[:], raw[:, :, GC], 1e-16, None, ALU.add).then_inc(den_ok, 1)
                    e.wait_ge(den_ok, n + 1)
                    e.reciprocal(rec[:], den[:]).then_inc(rec_ok, 1)
                    e.wait_ge(rec_ok, n + 1)
                    if turns is not None:
                        e.wait_ge(sent[p], turns * 16)
                    for d in range(NT):
                        ins = e.tensor_scalar(node[:, p, d], raw[:, d, 0:GC], rec[:, d:d + 1], None, ALU.mult)
                    ins.then_inc(sc_ok, 1)

                def pair(i):
                    for j in range(STEPS):
                        if i_is(i, 0) and j % 2 == 1 and j < NT:
                            loops(j // 2 + 1)
                        if j + 1 < STEPS:
                            bound(i, j + 1)
                        elif not last(i):
                            bound(i + 1, 0)
                        e.wait_ge(e_ok, i * STEPS + j + 1)
                        if i_is(i, 0) and j < NT:
                            e.wait_ge(loop_ok, j // 2 * 2 + 2)
                        e.scalar_tensor_tensor(out=ring[:, j % RING], in0=ring[:, j % RING], scalar=1.0, in1=cnt[:, j % NT],
                                               op0=ALU.min, op1=ALU.mult).then_inc(p_ok, 1)
                        if j == 4 and not first(i):
                            scale(i * 2 - 1, 1, None if i_is(i, 1) else i - 1)
                        if j == NT + 4:
                            scale(i * 2, 0, None if first(i) else i)
                    if last(i):
                        scale(2 * LAST + 1, 1, LAST)

                def loops(q):
                    if q < NT // 2:
                        e.wait_ge(cnt_in[q], 16)
                        for s in (2 * q, 2 * q + 1):
                            e.tensor_tensor(cnt[:, s, tile(s)], cnt[:, s, tile(s)], g.ident[0:T, 0:T], ALU.add).then_inc(loop_ok, 1)

                i_is = lambda i, v: isinstance(i, int) and i == v
                loops(0)
                bound(0, 0)
                over_pairs(e, pair)

            @block.tensor
            def _(e):
                e.sem_inc(mm, RING)
                e.sem_inc(acc_out, 5)
                e.wait_ge(ones_ok, 1)
                with e.Fori(0, GI // 2) as i:
                    for j in range(STEPS):
                        p, s = j // NT, j % NT
                        e.wait_ge(p_ok, i * STEPS + j + 1)
                        if s == 0:
                            e.wait_ge(h_in[p], i * 16 + 16)
                        for d in range(NT):
                            if s == 0 and d % 2 == 0:
                                e.wait_ge(acc_out, (i * 2 + p) * 5 + d // 2 + 1)
                            ins = e.matmul(acc[0:T, d // 2, d % 2 * 256:d % 2 * 256 + HC], ring[:, j % RING, tile(d)],
                                           h[:, p, s], start=(s == 0 and d % 2 == 0), stop=(s == NT - 1 and d % 2 == 1),
                                           skip_group_check=True)
                        ins.then_inc(mm, 1)


def join(nc, g):
    KO = GL * KT
    KC = 3
    with ExitStack() as ctx:
        sb = lambda n, s, d=F32: ctx.enter_context(nc.sbuf_tensor("jo_" + n, s, d))
        ps = lambda n, s: ctx.enter_context(nc.psum_tensor("jo_" + n, s, F32))
        sem = lambda n: g.sem("jo_" + n)
        wh, wl = sb("wh", [128, KO, D], F32R), sb("wl", [128, KO, D], F32R)
        raw = sb("raw", [128, 2, KC, D])
        node = sb("node", [T, 2, D])
        xt, mt = sb("xt", [T, 2, D]), sb("mt", [T, 2, D])
        bias = sb("bias", [T, D])
        sh, sl = sb("sh", [128, 2, KT, T], F32R), sb("sl", [128, 2, KT, T], F32R)
        tmp = sb("tmp", [T, 2, D])
        TR, O = ps("TR", [128, 2, 2, 512]), ps("O", [128, 2, 2, 512])
        raw_in, b_in = [sem("raw_in0"), sem("raw_in1")], sem("b_in")
        nd_in = [sem("nd_in0"), sem("nd_in1")]
        wh_ok, wl_ok, lo_ok = sem("wh_ok"), sem("wl_ok"), sem("lo_ok")
        stats_ok, started = sem("stats_ok"), sem("started")
        in_, sent = [sem("in0"), sem("in1")], [sem("sent0"), sem("sent1")]
        tr_mm, st_ok, mm, xm_ok, pre_ok, x_ok = (sem(n) for n in ("tr_mm", "st_ok", "mm", "xm_ok", "pre_ok", "x_ok"))

        with nc.Block() as block:
            @block.sync
            def _(sp):
                def third(n, c, p):
                    sp.dma_start(node[:, p], g.node[bass.ds(n * T, T), c * D:(c + 1) * D]).then_inc(nd_in[p], 16)

                third(0, 0, 0)
                for c in range(KO // KC):
                    if c >= 2:
                        sp.wait_ge(wl_ok, c - 1)
                    sp.dma_start(raw[:, c % 2], weight_view(g.gnn_W_out)[:, c * KC:(c + 1) * KC]).then_inc(raw_in[c % 2], 16)
                    if c == 0:
                        third(0, 1, 1)
                sp.dma_start(bias[:], g.gnn_b_out.partition_broadcast(T)).then_inc(b_in, 16)

                def pair(i, last):
                    for u in range(6):
                        n, c = i * 2 + (u + 2) // 3, (u + 2) % 3
                        if not last or u < 4:
                            sp.wait_ge(tr_mm, i * 6 + u + 1)
                            third(n, c, u % 2)

                with sp.Fori(0, NT // 2 - 1) as i:
                    pair(i, False)
                pair(NT // 2 - 1, True)

            @block.gpsimd
            def _(e):
                def fetch(n, p):
                    rows = bass.ds(n * T, T)
                    e.dma_start(xt[:, p], g.x[rows, :]).then_inc(in_[p], 16)
                    e.dma_start(mt[:, p], g.mix_out[rows, :]).then_inc(in_[p], 16)

                def pair(i, last):
                    for p in range(2):
                        n = i * 2 + p
                        e.wait_ge(x_ok, n + 1)
                        e.sem_inc(started, 1)
                        e.dma_start(g.xj[bass.ds(n * T, T), :], g.y[:, n, :]).then_inc(sent[p], 16)
                        if not last:
                            fetch(n + 2, p)

                fetch(0, 0)
                fetch(1, 1)
                with e.Fori(0, NT // 2 - 1) as i:
                    pair(i, False)
                pair(NT // 2 - 1, True)
                for s in sent:
                    e.wait_ge(s, 16 * NT // 2)

            @block.tensor
            def _(e):
                def turn(i, u):
                    e.wait_ge(nd_in[u % 2], (i * 3 + u // 2 + 1) * 16)
                    e.wait_ge(lo_ok, i * 6 + max(u - 1, 0))
                    for k in range(KT):
                        ins = e.transpose(TR[:, u % 2, k // 3, k % 3 * T:(k % 3 + 1) * T],
                                          node[:, u % 2, k * 128:(k + 1) * 128], g.ident[0:T, 0:T])
                    ins.then_inc(tr_mm, 1)

                def pair(i, last):
                    for u in range(6):
                        p, c = u // 3, u % 3
                        if not last or u < 5:
                            turn(i, u + 1)
                        e.wait_ge(lo_ok, i * 6 + u + 1)
                        if c == 0:
                            e.wait_ge(pre_ok, i * 2 + p)
                        for k in range(KT):
                            if k % KC == 0:
                                e.wait_ge(wl_ok, (c * KT + k) // KC + 1)
                            for hf in range(2):
                                for x, w in ((sh, wh), (sh, wl), (sl, wh)):
                                    ins = e.matmul(O[0:T, p, hf, 0:HALF], x[:, u % 2, k], w[:, c * KT + k, hf * HALF:(hf + 1) * HALF],
                                                   start=(c == 0 and k == 0 and x is sh and w is wh),
                                                   stop=(c == 2 and k == KT - 1 and x is sl))
                        ins.then_inc(mm, 1)

                e.sem_inc(pre_ok, 1)
                turn(0, 0)
                with e.Fori(0, NT // 2 - 1) as i:
                    pair(i, False)
                pair(NT // 2 - 1, True)

            @block.scalar
            def _(e):
                def high(i, u):
                    e.wait_ge(tr_mm, i * 6 + u + 1)
                    e.wait_ge(mm, i * 6 + max(u - 1, 0))
                    e.activation(sh[:, u % 2].rearrange("p (b k) t -> p b (k t)", b=2), TR[:, u % 2, :, 0:3 * T], ACT.Copy).then_inc(st_ok, 1)

                high(0, 0)
                for c in range(KO // KC):
                    e.wait_ge(raw_in[c % 2], 16 * (c // 2 + 1))
                    e.activation(wh[:, c * KC:(c + 1) * KC], raw[:, c % 2], ACT.Copy).then_inc(wh_ok, 1)
                for u in range(1, 6):
                    high(0, u)
                with e.Fori(1, NT // 2) as i:
                    for u in range(6):
                        high(i, u)

            @block.vector
            def _(e):
                def low(i, u):
                    e.wait_ge(st_ok, i * 6 + u + 1)
                    e.tensor_tensor(sl[:, u % 2].rearrange("p (b k) t -> p b (k t)", b=2), TR[:, u % 2, :, 0:3 * T],
                                    sh[:, u % 2].rearrange("p (b k) t -> p b (k t)", b=2).bitcast(F32), ALU.subtract).then_inc(lo_ok, 1)

                low(0, 0)
                for c in range(KO // KC):
                    e.wait_ge(wh_ok, c + 1)
                    e.tensor_tensor(wl[:, c * KC:(c + 1) * KC], raw[:, c % 2], wh[:, c * KC:(c + 1) * KC].bitcast(F32),
                                    ALU.subtract).then_inc(wl_ok, 1)
                e.wait_ge(b_in, 16)
                low(0, 1)

                def finish(n, p, i):
                    e.wait_ge(in_[p], i * 32 + 32)
                    e.tensor_tensor(xt[:, p], xt[:, p], mt[:, p], ALU.add).then_inc(xm_ok, 1)
                    e.wait_ge(mm, 3 * n + 3)
                    e.tensor_tensor(tmp[:, p].rearrange("p (c n) -> p c n", c=2), O[0:T, p, :, 0:HALF],
                                    bias[:].rearrange("p (c n) -> p c n", c=2), ALU.add).then_inc(pre_ok, 1)
                    e.wait_ge(pre_ok, n + 2)
                    e.wait_ge(xm_ok, n + 1)
                    e.scalar_tensor_tensor(out=g.y[:, n, :], in0=tmp[:, p], scalar=0.0, in1=xt[:, p],
                                           op0=ALU.max, op1=ALU.add).then_inc(x_ok, 1)
                    e.wait_ge(x_ok, n + 1)
                    for c in range(2):
                        e.bn_stats(g.stats[:, bass.ds(n, 1), 6 * c:6 * c + 6].rearrange("p a s -> p (a s)"),
                                   g.y[:, n, c * HALF:(c + 1) * HALF]).then_inc(stats_ok, 1)

                def pair(i, last):
                    for u in range(6):
                        if not last or u < 4:
                            low(i, u + 2)
                        if u % 3 == 2:
                            finish(i * 2 + u // 3, u // 3, i)

                with e.Fori(0, NT // 2 - 1) as i:
                    pair(i, False)
                pair(NT // 2 - 1, True)
                e.wait_ge(stats_ok, 2 * NT)


def route(nc, g):
    NG = 4
    NPB = NB // NG

    def over_tiles(e, pair):
        pair(0)
        with e.Fori(1, NT // 2 - 1) as i:
            pair(i)
        pair(NT // 2 - 1)
    with ExitStack() as ctx:
        sb = lambda n, s, d=F32: ctx.enter_context(nc.sbuf_tensor("ro_" + n, s, d))
        ps = lambda n, s: ctx.enter_context(nc.psum_tensor("ro_" + n, s, F32))
        sem = lambda n: g.sem("ro_" + n)
        stats, mv, mv2 = sb("stats", [T, NT, 12]), sb("mv", [T, NT, 2]), sb("mv2", [T, NT, 2])
        veps, std, rstd, tmp = (sb(n, [T, NT]) for n in ("veps", "std", "rstd", "tmp"))
        gain, shift = sb("gain", [128, KT]), sb("shift", [128, KT])
        recipe, rmax, rsum, rrec = sb("recipe", [NN, NB]), sb("rmax", [NN, 1]), sb("rsum", [NN, 1]), sb("rrec", [NN, 1])
        pat, gate, gated = sb("pat", [NN, MH]), sb("gate", [NN, 1]), sb("gated", [NN, NN])
        ones = sb("ones", [NN, T])
        gateB = sb("gateB", [T, NN])
        bemb = sb("bemb", [NB, D])
        recT = sb("recT", [NB, NN])
        nemb = sb("nemb", [128, KT, NN])
        basis = sb("basis", [128, KT, NB, RANK])
        vw, vb = sb("vw", [RANK, D]), sb("vb", [T, D])
        z = sb("z", [T, 2, D])
        stage = sb("stage", [128, 2, KT, T])
        fin, rep, ex, sel = (sb(n, [T, NN]) for n in ("fin", "rep", "ex", "sel"))
        top, ntop, ssum, srec = sb("top", [T, 8]), sb("ntop", [T, 1]), sb("ssum", [T, 1]), sb("srec", [T, 1])
        selT = sb("selT", [NN, T])
        mixw = sb("mixw", [T, NB])
        pw = sb("pw", [T, NB, RANK])
        vs = sb("vs", [T, 128])
        vsT = sb("vsT", [RANK, T])
        TR, PR, S1, S2 = ps("TR", [128, 2, 512]), ps("PR", [128, NG, 512]), ps("S1", [128, 512]), ps("S2", [128, 512])
        gs_in, small_in, bas_in, vw_in = sem("gs_in"), sem("small_in"), sem("bas_in"), sem("vw_in")
        var_ok, std_ok, ones_ok, dve, act = sem("var_ok"), sem("std_ok"), sem("ones_ok"), sem("dve"), sem("act")
        rmax_ok, rexp_ok, rec_ok, pat_ok, pexp_ok, gd_ok = (sem(n) for n in ("rmax_ok", "rexp_ok", "rec_ok", "pat_ok", "pexp_ok", "gd_ok"))
        recT_mm, recT_ok, nemb_mm, gateB_mm, setup = (sem(n) for n in ("recT_mm", "recT_ok", "nemb_mm", "gateB_mm", "setup"))
        z_ok, tr_mm, st_ok, nT_ok, sem_mm, pr_mm = (sem(n) for n in ("z_ok", "tr_mm", "st_ok", "nT_ok", "sem_mm", "pr_mm"))
        top8_ok, rep_ok, sum_ok = sem("top8_ok"), sem("rep_ok"), sem("sum_ok")
        fin_ok, y_ok, y_sent = sem("fin_ok"), sem("y_ok"), sem("y_sent")
        top_ok, ex_ok, sel_ok, selT_mm, selT_ok, mixw_mm, mixw_ok, pw_ok, vs_ok, vsT_mm, vsT_ok, v_mm, v_ok = (
            sem(n) for n in ("top_ok", "ex_ok", "sel_ok", "selT_mm", "selT_ok", "mixw_mm", "mixw_ok", "pw_ok", "vs_ok", "vsT_mm",
                             "vsT_ok", "v_mm", "v_ok"))

        with nc.Block() as block:
            @block.sync
            def _(sp):
                sp.dma_start(recipe[:], g.ffn_recipe).then_inc(small_in, 16)
                sp.dma_start(pat[:], g.ffn_ctx_pat).then_inc(small_in, 16)
                sp.dma_start(bemb[:], g.ffn_basis_emb).then_inc(small_in, 16)
                for dst, v in ((gain, g.ffn_n1_g), (shift, g.ffn_n1_b)):
                    sp.dma_start(dst[:], v.rearrange("(k p) -> p k", p=128), allow_slow_non_contiguous=True).then_inc(gs_in, 16)
                for k in range(KT):
                    sp.dma_start(basis[:, k], g.ffn_basis_A[:, k * 128:(k + 1) * 128, :].rearrange("n p r -> p n r")).then_inc(bas_in, 16)
                sp.dma_start(vw[:], g.ffn_vout_w).then_inc(vw_in, 16)
                sp.dma_start(vb[:], g.ffn_vout_b.partition_broadcast(T)).then_inc(vw_in, 16)
                sp.wait_ge(y_ok, NT)
                sp.dma_start(node_view(g.y_dram), g.y[:]).then_inc(y_sent, 16)
                sp.wait_ge(y_sent, 16)

            @block.gpsimd
            def _(e):
                e.memset(ones[:], 1.0).then_inc(ones_ok, 1)
                e.memset(g.v[:], 1.0).then_inc(ones_ok, 1)
                e.memset(vs[:], 0.0).then_inc(ones_ok, 1)
                with e.Fori(0, NT // 2) as i:
                    for p in range(2):
                        n = i * 2 + p
                        cols = bass.ds(n * T, T)
                        e.wait_ge(st_ok, (n + 1) * KT)
                        e.tensor_copy(g.nTh[:, :, cols], stage[:, p]).then_inc(nT_ok, 1)
                        e.wait_ge(nT_ok, 2 * n + 1)
                        e.tensor_tensor(g.nTl[:, :, cols], stage[:, p], g.nTh[:, :, cols].bitcast(F32), ALU.subtract).then_inc(nT_ok, 1)

            @block.vector
            def _(e):
                seq = Tally(e, dve)
                e.wait_ge(small_in, 48)
                e.tensor_reduce(rmax[:], recipe[:], AX.X, ALU.max, negate=True).then_inc(rmax_ok, 1)
                seq.step(e.tensor_reduce(gate[:], pat[:], AX.X, ALU.add))
                e.tensor_scalar(gate[:], gate[:], -1.0 / N, None, ALU.mult).then_inc(pat_ok, 1)
                e.wait_ge(pexp_ok, 1)
                seq.step(e.tensor_scalar(gate[:], gate[:], 1.0, None, ALU.add))
                seq.step(e.reciprocal(gate[:], gate[:]))
                e.tensor_scalar(gated[:], g.ident[0:NN, 0:NN], gate[:], None, ALU.mult).then_inc(gd_ok, 1)
                e.wait_ge(rexp_ok, 1)
                seq.step(e.reciprocal(rrec[:], rsum[:]))
                e.tensor_scalar(recipe[:], recipe[:], rrec[:], None, ALU.mult).then_inc(rec_ok, 1)
                e.wait_ge(recT_mm, 1)
                e.tensor_copy(recT[:], S1[0:NB, 0:NN]).then_inc(recT_ok, 1)
                e.wait_ge(nemb_mm, 1)
                e.tensor_copy(nemb[:, 0:3], TR[:, 0, 0:3 * NN].rearrange("p (k n) -> p k n", k=3)).then_inc(setup, 1)
                e.tensor_copy(nemb[:, 3:6], TR[:, 1, 0:3 * NN].rearrange("p (k n) -> p k n", k=3)).then_inc(setup, 1)
                e.wait_ge(gateB_mm, 1)
                e.tensor_copy(gateB[:], S2[0:T, 0:NN]).then_inc(setup, 1)
                for t in range(NT):
                    seq.mark(e.bn_aggr(mv[:, t, :], g.stats[:, t, :]))
                seq.settle()
                e.tensor_scalar(veps[:], mv[:, :, 1], LN_EPS, None, ALU.add).then_inc(var_ok, 1)
                e.wait_ge(std_ok, 1)
                newton_rstd(e, seq, rstd[:], std[:], veps[:], tmp[:])
                for t in range(NT):
                    e.tensor_scalar(g.y[:, t], g.y[:, t], mv[:, t, 0:1], rstd[:, t:t + 1], ALU.subtract, ALU.mult).then_inc(y_ok, 1)
                e.wait_ge(y_ok, NT)
                norm_stats(e, seq, g.y, stats, mv2, veps).then_inc(var_ok, 1)
                e.wait_ge(std_ok, 2)
                newton_rstd(e, seq, rstd[:], std[:], veps[:], tmp[:])

                def centre(n, p):
                    e.tensor_scalar(z[:, p], g.y[:, n, :], mv2[:, n, 0:1], rstd[:, bass.ds(n, 1)],
                                    ALU.subtract, ALU.mult).then_inc(z_ok, 1)

                def add_bias(n):
                    e.wait_ge(v_mm, n + 1)
                    e.tensor_tensor(g.v[:, n, :].rearrange("p (c h d) -> p c h d", c=2, h=MP)[:, :, :, 0:DH],
                                    TR[0:T, :, 0:HALF].rearrange("p c (h d) -> p c h d", h=MP),
                                    vb[:].rearrange("p (c h d) -> p c h d", c=2, h=MP), ALU.add).then_inc(v_ok, 1)

                centre(0, 0)
                e.wait_ge(setup, 3)
                e.wait_ge(vw_in, 32)
                e.wait_ge(ones_ok, 3)

                def pair(i):
                    for p in range(2):
                        n = i * 2 + p
                        if not isinstance(n, int) or n + 1 < NT:
                            if not isinstance(n, int) or n > 0:
                                e.wait_ge(tr_mm, n)
                            centre(n + 1, 1 - p)
                        e.wait_ge(sem_mm, n + 1)
                        e.tensor_tensor(fin[:], S1[0:T, 0:NN], gateB[:], ALU.mult).then_inc(fin_ok, 1)
                        e.wait_ge(fin_ok, 2 * n + 1)
                        e.sem_inc(fin_ok, 1)
                        e.max(top[:], fin[:]).then_inc(top8_ok, 1)
                        e.wait_ge(top8_ok, n + 1)
                        e.tensor_scalar(ntop[:], top[:, 0:1], -1.0, None, ALU.mult).then_inc(top_ok, 1)
                        e.match_replace(rep[:], top[:], fin[:], NEG).then_inc(rep_ok, 1)
                        e.wait_ge(ex_ok, n + 1)
                        e.wait_ge(rep_ok, n + 1)
                        e.scalar_tensor_tensor(out=sel[:], in0=rep[:], scalar=NEG, in1=ex[:], op0=ALU.is_equal,
                                               op1=ALU.mult, accum_out=ssum[:]).then_inc(sum_ok, 1)
                        e.wait_ge(sum_ok, 2 * n + 1)
                        e.reciprocal(srec[:], ssum[:]).then_inc(sum_ok, 1)
                        e.wait_ge(sum_ok, 2 * n + 2)
                        e.tensor_scalar(sel[:], sel[:], srec[:], None, ALU.mult).then_inc(sel_ok, 1)
                        if not isinstance(n, int) or n > 0:
                            add_bias(n - 1)
                        e.wait_ge(mixw_mm, n + 1)
                        e.tensor_copy(mixw[:], S1[0:T, 128:128 + NB]).then_inc(mixw_ok, 1)
                        e.wait_ge(mixw_ok, n + 1)
                        for c in range(NG):
                            e.wait_ge(pr_mm, n * NG + c + 1)
                            e.tensor_tensor(pw[:, c * NPB:(c + 1) * NPB], PR[0:T, c].rearrange("p (n r) -> p n r", r=RANK),
                                            mixw[:, c * NPB:(c + 1) * NPB].unsqueeze(2).to_broadcast([T, NPB, RANK]),
                                            ALU.mult).then_inc(pw_ok, 1)
                        e.wait_ge(pw_ok, (n + 1) * NG)
                        e.tensor_reduce(vs[:, 0:RANK], pw[:].rearrange("p n r -> p r n"), AX.X, ALU.add).then_inc(vs_ok, 1)

                over_tiles(e, pair)
                add_bias(NT - 1)

            @block.scalar
            def _(e):
                e.wait_ge(rmax_ok, 1)
                e.activation(recipe[:], recipe[:], ACT.Exp, bias=rmax[:], accum_out=rsum[:]).then_inc(rexp_ok, 1)
                e.wait_ge(pat_ok, 1)
                e.activation(gate[:], gate[:], ACT.Exp).then_inc(pexp_ok, 1)
                for i in range(2):
                    e.wait_ge(var_ok, i + 1)
                    e.activation(std[:], veps[:], ACT.Sqrt).then_inc(std_ok, 1)
                e.wait_ge(gs_in, 32)

                def pair(i):
                    for p in range(2):
                        n = i * 2 + p
                        if isinstance(n, int) and n == 0:
                            affine(0, 0)
                        e.wait_ge(top_ok, n + 1)
                        e.activation(ex[:], fin[:], ACT.Exp, bias=ntop[:]).then_inc(ex_ok, 1)
                        if not isinstance(n, int) or n > 0:
                            turn_values(n - 1)
                        e.wait_ge(selT_mm, n + 1)
                        e.activation(selT[:], S2[0:NN, 0:T], ACT.Copy).then_inc(selT_ok, 1)
                        if not isinstance(n, int) or n + 1 < NT:
                            affine(n + 1, 1 - p)

                def affine(n, p):
                    e.wait_ge(tr_mm, n + 1)
                    if not isinstance(n, int) or n > 1:
                        e.wait_ge(nT_ok, 2 * (n - 1))
                        e.wait_ge(pr_mm, (n - 1) * NG)
                    for k in range(KT):
                        e.activation(stage[:, p, k], TR[:, k // 3, k % 3 * T:(k % 3 + 1) * T], ACT.Identity,
                                     bias=shift[:, k:k + 1], scale=gain[:, k:k + 1]).then_inc(st_ok, 1)

                def turn_values(n):
                    e.wait_ge(vsT_mm, n + 1)
                    e.activation(vsT[:], S2[0:RANK, 128:128 + T], ACT.Copy).then_inc(vsT_ok, 1)

                over_tiles(e, pair)
                turn_values(NT - 1)

            @block.tensor
            def _(e):
                e.wait_ge(rec_ok, 1)
                e.transpose(S1[0:NB, 0:NN], recipe[:], g.ident[0:NN, 0:NN]).then_inc(recT_mm, 1)
                e.wait_ge(recT_ok, 1)
                for k in range(KT):
                    ins = e.matmul(TR[:, k // 3, k % 3 * NN:(k % 3 + 1) * NN], bemb[:, k * 128:(k + 1) * 128], recT[:],
                                   start=True, stop=True)
                ins.then_inc(nemb_mm, 1)
                e.wait_ge(gd_ok, 1)
                e.wait_ge(ones_ok, 3)
                e.matmul(S2[0:T, 0:NN], ones[:], gated[:], start=True, stop=True).then_inc(gateB_mm, 1)
                e.wait_ge(setup, 3)

                def turn(n, p):
                    e.wait_ge(z_ok, n + 1)
                    if not isinstance(n, int) or n > 1:
                        e.wait_ge(v_ok, n - 1)
                    for k in range(KT):
                        ins = e.transpose(TR[:, k // 3, k % 3 * T:(k % 3 + 1) * T], z[:, p, k * 128:(k + 1) * 128],
                                          g.ident[0:T, 0:T])
                    ins.then_inc(tr_mm, 1)

                def semantic(n, p):
                    e.wait_ge(st_ok, (n + 1) * KT)
                    if not isinstance(n, int) or n > 0:
                        e.wait_ge(mixw_ok, n)
                    for k in range(KT):
                        ins = e.matmul(S1[0:T, 0:NN], stage[:, p, k], nemb[:, k], start=(k == 0), stop=(k == KT - 1))
                    ins.then_inc(sem_mm, 1)

                def turn_vs(n):
                    e.wait_ge(vs_ok, n + 1)
                    e.transpose(S2[:, 128:128 + T], vs[:], g.ident[0:T, 0:T]).then_inc(vsT_mm, 1)

                def values(n):
                    e.wait_ge(vsT_ok, n + 1)
                    for c in range(2):
                        ins = e.matmul(TR[0:T, c, 0:HALF], vsT[:], vw[:, c * HALF:(c + 1) * HALF], start=True, stop=True)
                    ins.then_inc(v_mm, 1)

                turn(0, 0)
                semantic(0, 0)
                e.wait_ge(vw_in, 32)

                def pair(i):
                    for p in range(2):
                        n = i * 2 + p
                        for c in range(NG):
                            if isinstance(n, int) and n == 0:
                                e.wait_ge(bas_in, 16 * KT)
                            else:
                                e.wait_ge(pw_ok, (n - 1) * NG + c + 1)
                            for k in range(KT):
                                ins = e.matmul(PR[0:T, c], stage[:, p, k], basis[:, k, c * NPB:(c + 1) * NPB].rearrange("p n r -> p (n r)"),
                                               start=(k == 0), stop=(k == KT - 1))
                            ins.then_inc(pr_mm, 1)
                            before = not isinstance(n, int) or n > 0
                            after = not isinstance(n, int) or n + 1 < NT
                            if c == 0 and before:
                                turn_vs(n - 1)
                            if c == 1:
                                if before:
                                    values(n - 1)
                                e.wait_ge(sel_ok, n + 1)
                                e.transpose(S2[0:NN, 0:T], sel[:], g.ident[0:T, 0:T]).then_inc(selT_mm, 1)
                            if c == 2:
                                e.wait_ge(selT_ok, n + 1)
                                e.matmul(S1[0:T, 128:128 + NB], selT[:], recipe[:], start=True, stop=True).then_inc(mixw_mm, 1)
                                if after:
                                    turn(n + 1, 1 - p)
                            if c == 3 and after:
                                semantic(n + 1, 1 - p)

                over_tiles(e, pair)
                turn_vs(NT - 1)
                values(NT - 1)


def attend(nc, g):
    STEPS = 2 * NT
    CW, CS = 418, 416
    W2 = 2 * (DH + 1)
    NA = 500
    with ExitStack() as ctx:
        sb = lambda n, s, d=F32: ctx.enter_context(nc.sbuf_tensor("at_" + n, s, d))
        ps = lambda n, s: ctx.enter_context(nc.psum_tensor("at_" + n, s, F32))
        sem = lambda n: g.sem("at_" + n)
        qw, kw = sb("qw", [128, KT, 128]), sb("kw", [128, KT, 128])
        qb, kb = sb("qb", [128, KT]), sb("kb", [128, KT])
        wqh, wql, wkh, wkl = (sb(n, [128, KT, 128], F32R) for n in ("wqh", "wql", "wkh", "wkl"))
        qf, kf = sb("qf", [128, N]), sb("kf", [128, N])
        qq, kh, kl = sb("qq", [128, 2, N], F32R), sb("kh", [128, 2, N], F32R), sb("kl", [128, 2, N], F32R)
        nmax, rc = sb("nmax", [T, 2]), sb("rc", [T, 2])
        A = sb("A", [T, 2, N])
        AT = sb("AT", [T, 2, N])
        S, O = ps("S", [128, 2, 3, 512]), ps("O", [128, 2, 512])
        b_in, qw_in, kw_in, ws_ok = sem("b_in"), sem("qw_in"), sem("kw_in"), sem("ws_ok")
        q_mm, k_mm, qf_ok, kf_ok, qb_ok = sem("q_mm"), sem("k_mm"), sem("qf_ok"), sem("kf_ok"), sem("qb_ok")
        qs_ok, k0v_ok, k0a_ok, k1_ok = sem("qs_ok"), sem("k0v_ok"), sem("k0a_ok"), sem("k1_ok")
        started = sem("started")
        halves = [slice(0, DH), slice(DH, 128)]
        s_mm, max_ok, exp_ok, tt_mm, at_v, at_a, av_mm, rc_ok, ao_ok = (
            sem(n) for n in ("s_mm", "max_ok", "exp_ok", "tt_mm", "at_v", "at_a", "av_mm", "rc_ok", "ao_ok"))

        def over_pairs(e, pair):
            with e.Fori(0, MP - 1) as m:
                pair(m, False)
            pair(MP - 1, True)

        with nc.Block() as block:
            @block.sync
            def _(sp):
                sp.dma_start(qw[:], weight_view(g.ffn_q_w)[:, :, 0:128]).then_inc(qw_in, 16)
                sp.dma_start(kw[:], weight_view(g.ffn_k_w)[:, :, 0:128]).then_inc(kw_in, 16)
                for dst, v in ((qb, g.ffn_q_b), (kb, g.ffn_k_b)):
                    sp.dma_start(dst[:], v.rearrange("(k p) -> p k", p=128), allow_slow_non_contiguous=True).then_inc(b_in, 16)
                with sp.Fori(1, MP) as m:
                    sp.wait_ge(ws_ok, m * 4)
                    sp.dma_start(qw[:], weight_view(g.ffn_q_w)[:, :, bass.ds(m * 128, 128)]).then_inc(qw_in, 16)
                    sp.dma_start(kw[:], weight_view(g.ffn_k_w)[:, :, bass.ds(m * 128, 128)]).then_inc(kw_in, 16)

            @block.gpsimd
            def _(e):
                def weights(m):
                    for w, into, high, low, used in ((qw, qw_in, wqh, wql, q_mm), (kw, kw_in, wkh, wkl, k_mm)):
                        e.wait_ge(into, m * 16 + 16)
                        e.wait_ge(used, m)
                        e.sem_inc(started, 1)
                        e.tensor_copy(high[:], w[:]).then_inc(ws_ok, 1)
                        e.wait_ge(ws_ok, m * 4 + (1 if w is qw else 3))
                        e.tensor_tensor(low[:], w[:], high[:].bitcast(F32), ALU.subtract).then_inc(ws_ok, 1)

                def pair(m, last):
                    e.wait_ge(kf_ok, m + 1)
                    e.sem_inc(started, 1)
                    e.tensor_copy(kh[halves[1], 1], kf[halves[1]]).then_inc(k1_ok, 1)
                    e.wait_ge(k1_ok, m * 4 + 1)
                    for h in (1, 0):
                        e.tensor_tensor(kl[halves[h], 1], kf[halves[1]], kh[halves[1], 1].bitcast(F32), ALU.subtract).then_inc(k1_ok, 1)
                        e.wait_ge(k1_ok, m * 4 + 3 - h)
                    e.sem_inc(started, 1)
                    e.tensor_copy(kh[halves[0], 1], kf[halves[1]]).then_inc(k1_ok, 1)
                    e.wait_ge(k1_ok, m * 4 + 4)
                    if not last:
                        weights(m + 1)

                weights(0)
                over_pairs(e, pair)

            @block.tensor
            def _(e):
                def linear(high, low, slot):
                    for b in range(3):
                        for k in range(KT):
                            cols = slice(b * CS, b * CS + CW)
                            for w, x in ((high, g.nTh), (high, g.nTl), (low, g.nTh)):
                                ins = e.matmul(S[:, slot, b, 0:CW], w[:, k], x[:, k, cols], start=(k == 0 and w is high and x is g.nTh),
                                               stop=(k == KT - 1 and w is low))
                    return ins

                def scores(u):
                    h = u // NT
                    q = qq[:, h, u % NT * T:(u % NT + 1) * T]
                    for b in range(3):
                        cols = slice(b * CS, b * CS + CW)
                        e.matmul(S[0:T, u % 2, b, 0:CW], q, kh[:, h, cols], start=True, stop=False)
                        ins = e.matmul(S[0:T, u % 2, b, 0:CW], q, kl[:, h, cols], start=False, stop=True)
                    ins.then_inc(s_mm, 1)

                def values(m, u):
                    e.wait_ge(at_v, m * STEPS + u + 1)
                    e.wait_ge(at_a, m * STEPS + u + 1)
                    e.wait_ge(ao_ok, m * STEPS + max(u - 1, 0))
                    for t in range(NT):
                        ins = e.matmul(O[0:T, u % 2, 0:W2], AT[:, u % 2, t * T:(t + 1) * T], g.v[:, t, bass.ds(m * W2, W2)],
                                       start=(t == 0), stop=(t == NT - 1))
                    ins.then_inc(av_mm, 1)

                def pair(m, last):
                    e.wait_ge(qs_ok, 4 * m + 4)
                    e.wait_ge(k0v_ok, 3 * m + 3)
                    e.wait_ge(k0a_ok, m + 1)
                    scores(0)
                    scores(1)
                    for u in range(STEPS):
                        e.wait_ge(exp_ok, m * STEPS + u + 1)
                        for t in range(NT):
                            ins = e.transpose(S[0:T, u % 2, t // 4, t % 4 * T:(t % 4 + 1) * T], A[:, u % 2, t * T:(t + 1) * T], g.ident[0:T, 0:T])
                        ins.then_inc(tt_mm, 1)
                        if u > 0:
                            values(m, u - 1)
                        if not last or u + 2 < STEPS:
                            e.wait_ge(at_v, m * STEPS + u + 1)
                            e.wait_ge(at_a, m * STEPS + u + 1)
                        if u + 2 == NT:
                            e.wait_ge(k1_ok, 4 * m + 4)
                        if u + 2 < STEPS:
                            scores(u + 2)
                        elif not last:
                            high, low, done, c = ((wqh, wql, q_mm, 2), (wkh, wkl, k_mm, 4))[u + 2 - STEPS]
                            e.wait_ge(ws_ok, 4 * (m + 1) + c)
                            linear(high, low, u % 2).then_inc(done, 1)
                    values(m, STEPS - 1)

                e.wait_ge(ws_ok, 2)
                linear(wqh, wql, 0).then_inc(q_mm, 1)
                e.wait_ge(ws_ok, 4)
                linear(wkh, wkl, 1).then_inc(k_mm, 1)
                over_pairs(e, pair)

            @block.scalar
            def _(e):
                def wide(out, slot, rows, fn, **kw):
                    e.activation(out[:, 0:3 * CS].rearrange("p (b n) -> p b n", b=3), S[rows, slot, :, 0:CS], fn, **kw)
                    return e.activation(out[:, 3 * CS:N], S[rows, slot, 2, CS:CW], fn, **kw)

                def queries(m):
                    e.wait_ge(q_mm, m + 1)
                    e.wait_ge(qs_ok, 4 * m)
                    wide(qf, 0, slice(0, 128), ACT.Identity, bias=qb[:, bass.ds(m, 1)], scale=DH ** -0.5).then_inc(qf_ok, 1)

                def keys(m):
                    e.wait_ge(k_mm, m + 1)
                    e.wait_ge(k1_ok, 4 * m)
                    wide(kf, 1, slice(0, 128), ACT.Identity, bias=kb[:, bass.ds(m, 1)]).then_inc(kf_ok, 1)
                    e.wait_ge(kf_ok, m + 1)
                    e.activation(kh[halves[1], 0], kf[halves[0]], ACT.Copy).then_inc(k0a_ok, 1)

                def pair(m, last):
                    for s in range(STEPS + 1):
                        u = s - 1
                        if u >= 0:
                            e.wait_ge(tt_mm, m * STEPS + u + 1)
                            e.wait_ge(av_mm, m * STEPS + max(u - 1, 0))
                            e.activation(AT[:, u % 2, 0:NA], S[0:T, u % 2, 0, 0:NA], ACT.Copy)
                            e.activation(AT[:, u % 2, 2 * NA:N], S[0:T, u % 2, 2, 0:N - 2 * NA], ACT.Copy).then_inc(at_a, 1)
                        if s < STEPS:
                            e.wait_ge(max_ok, m * STEPS + s + 1)
                            e.wait_ge(tt_mm, m * STEPS + max(s - 1, 0))
                            wide(A[:, s % 2], s % 2, slice(0, T), ACT.Exp, bias=nmax[:, s % 2:s % 2 + 1]).then_inc(exp_ok, 1)
                        if s == STEPS - 1 and not last:
                            queries(m + 1)
                    if not last:
                        keys(m + 1)

                e.wait_ge(qb_ok, 1)
                queries(0)
                keys(0)
                over_pairs(e, pair)

            @block.vector
            def _(e):
                def queries(m):
                    e.wait_ge(qf_ok, m + 1)
                    for h in range(2):
                        e.tensor_copy(qq[halves[h], h], qf[halves[h]]).then_inc(qs_ok, 1)
                    e.wait_ge(qs_ok, 4 * m + 2)
                    for h in range(2):
                        e.tensor_tensor(qq[halves[1 - h], h], qf[halves[h]], qq[halves[h], h].bitcast(F32), ALU.subtract).then_inc(qs_ok, 1)

                def keys(m):
                    e.wait_ge(kf_ok, m + 1)
                    e.tensor_copy(kh[halves[0], 0], kf[halves[0]]).then_inc(k0v_ok, 1)
                    e.wait_ge(k0v_ok, 3 * m + 1)
                    for h in range(2):
                        e.tensor_tensor(kl[halves[h], 0], kf[halves[0]], kh[halves[0], 0].bitcast(F32), ALU.subtract).then_inc(k0v_ok, 1)

                def pair(m, last):
                    for s in range(STEPS + 2):
                        if s < STEPS:
                            e.wait_ge(s_mm, m * STEPS + s + 1)
                            e.tensor_reduce(nmax[:, s % 2:s % 2 + 1], S[0:T, s % 2, :, 0:CW], AX.XY, ALU.max,
                                            negate=True).then_inc(max_ok, 1)
                        u = s - 1
                        if 0 <= u < STEPS:
                            e.wait_ge(tt_mm, m * STEPS + u + 1)
                            e.wait_ge(av_mm, m * STEPS + max(u - 1, 0))
                            e.tensor_copy(AT[:, u % 2, NA:2 * NA], S[0:T, u % 2, 1, 0:NA]).then_inc(at_v, 1)
                        if s == STEPS and not last:
                            queries(m + 1)
                        u = s - 2
                        if u >= 0:
                            e.wait_ge(av_mm, m * STEPS + u + 1)
                            c = u // NT * (DH + 1)
                            e.reciprocal(rc[:, u % 2:u % 2 + 1], O[0:T, u % 2, c + DH:c + DH + 1]).then_inc(rc_ok, 1)
                            e.wait_ge(rc_ok, m * STEPS + u + 1)
                            e.tensor_scalar(g.ao[:, u % NT, bass.ds(m * 128 + u // NT * DH, DH)], O[0:T, u % 2, c:c + DH],
                                            rc[:, u % 2:u % 2 + 1], None, ALU.mult).then_inc(ao_ok, 1)
                    if not last:
                        keys(m + 1)

                e.wait_ge(b_in, 32)
                e.tensor_scalar(qb[:], qb[:], DH ** -0.5, None, ALU.mult).then_inc(qb_ok, 1)
                queries(0)
                keys(0)
                over_pairs(e, pair)


def tail(nc, g):
    with ExitStack() as ctx:
        sb = lambda n, s, d=F32: ctx.enter_context(nc.sbuf_tensor("ta_" + n, s, d))
        ps = lambda n, s: ctx.enter_context(nc.psum_tensor("ta_" + n, s, F32))
        sem = lambda n: g.sem("ta_" + n)
        wo, wu, wd = sb("wo", [128, KT, D]), sb("wu", [128, KT, FF]), sb("wd", [128, FJ, D])
        x2 = sb("x2", [T, NT, D])
        bo, bd = sb("bo", [T, D]), sb("bd", [T, D])
        gain, shift, bu = sb("gain", [128, KT]), sb("shift", [128, KT]), sb("bu", [128, FJ])
        stats, mv = sb("stats", [T, NT, 12]), sb("mv", [T, NT, 2])
        veps, std, rstd, tmp = (sb(n, [T, NT]) for n in ("veps", "std", "rstd", "tmp"))
        stage = sb("stage", [128, 2, KT, T])
        z, xt, res = sb("z", [T, 2, D]), sb("xt", [T, 2, D]), sb("res", [T, 2, D])
        uT = sb("uT", [128, 2, FJ, T])
        TR, O = ps("TR", [128, 2, 2, 512]), ps("O", [128, 2, 2, 512])
        y_in = [sem("y_in0"), sem("y_in1")]
        wo_in, w_in, b_in = sem("wo_in"), sem("w_in"), sem("b_in")
        in_, sent = [sem("in0"), sem("in1")], [sem("sent0"), sem("sent1")]
        tr_mm, st_ok, mm, add_ok, x2_ok, dve, var_ok, std_ok = (
            sem(n) for n in ("tr_mm", "st_ok", "mm", "add_ok", "x2_ok", "dve", "var_ok", "std_ok"))
        z_ok, zt_mm, zs_ok, up_mm, u_ok, dn_mm, xt_ok, res_ok = (
            sem(n) for n in ("z_ok", "zt_mm", "zs_ok", "up_mm", "u_ok", "dn_mm", "xt_ok", "res_ok"))
        split = lambda x: x.rearrange("p (c n) -> p c n", c=2)

        with nc.Block() as block:
            @block.sync
            def _(sp):
                sp.dma_start(wo[:], weight_view(g.ffn_ao_w)).then_inc(wo_in, 16)
                for c in range(2):
                    ts = slice(c * NT // 2, (c + 1) * NT // 2)
                    sp.dma_start(x2[:, ts], node_view(g.y_dram)[:, ts]).then_inc(y_in[c], 16)
                sp.dma_start(bo[:], g.ffn_ao_b.partition_broadcast(T)).then_inc(b_in, 16)
                sp.dma_start(bd[:], g.ffn_down_b.partition_broadcast(T)).then_inc(b_in, 16)
                for dst, v in ((gain, g.ffn_n2_g), (shift, g.ffn_n2_b), (bu, g.ffn_up_b)):
                    sp.dma_start(dst[:], v.rearrange("(k p) -> p k", p=128), allow_slow_non_contiguous=True).then_inc(b_in, 16)
                sp.dma_start(wu[:], weight_view(g.ffn_up_w)).then_inc(w_in, 16)
                sp.dma_start(wd[:], weight_view(g.ffn_down_w)).then_inc(w_in, 16)
                for p in range(2):
                    sp.dma_start(xt[:, p], g.xj[p * T:(p + 1) * T, :]).then_inc(in_[p], 16)
                with sp.Fori(0, NT // 2 - 1) as i:
                    for p in range(2):
                        n = i * 2 + p
                        sp.wait_ge(res_ok, n + 1)
                        sp.dma_start(g.out[bass.ds(n * T, T), :], res[:, p]).then_inc(sent[p], 16)
                        sp.dma_start(xt[:, p], g.xj[bass.ds((n + 2) * T, T), :]).then_inc(in_[p], 16)
                for n in range(NT - 2, NT):
                    sp.wait_ge(res_ok, n + 1)
                    sp.dma_start(g.out[n * T:(n + 1) * T, :], res[:, n % 2]).then_inc(sent[n % 2], 16)
                for s in sent:
                    sp.wait_ge(s, 16 * NT // 2)

            @block.tensor
            def _(e):
                e.wait_ge(wo_in, 16)
                for n in range(NT):
                    p = n % 2
                    if n > 0:
                        e.wait_ge(st_ok, n)
                    for k in range(KT):
                        ins = e.transpose(TR[:, p, k // 3, k % 3 * T:(k % 3 + 1) * T],
                                          g.ao[:, n, k * 128:(k + 1) * 128], g.ident[0:T, 0:T])
                    ins.then_inc(tr_mm, 1)
                    e.wait_ge(st_ok, n + 1)
                    if n >= 2:
                        e.wait_ge(add_ok, n - 1)
                    for c in range(2):
                        for k in range(KT):
                            ins = e.matmul(O[0:T, p, c, 0:HALF], stage[:, p, k], wo[:, k, c * HALF:(c + 1) * HALF],
                                           start=(k == 0), stop=(k == KT - 1))
                    ins.then_inc(mm, 1)
                e.wait_ge(w_in, 32)
                e.wait_ge(add_ok, NT)
                with e.Fori(0, NT // 2) as i:
                    for p in range(2):
                        n = i * 2 + p
                        e.wait_ge(z_ok, n + 1)
                        e.wait_ge(zs_ok, n)
                        for k in range(KT):
                            ins = e.transpose(TR[:, 0, k // 3, k % 3 * T:(k % 3 + 1) * T], z[:, p, k * 128:(k + 1) * 128],
                                              g.ident[0:T, 0:T])
                        ins.then_inc(zt_mm, 1)
                        e.wait_ge(zs_ok, n + 1)
                        e.wait_ge(u_ok, n)
                        for j in range(FJ):
                            for k in range(KT):
                                ins = e.matmul(TR[:, 1, p, j * T:(j + 1) * T], wu[:, k, j * 128:(j + 1) * 128], stage[:, p, k],
                                               start=(k == 0), stop=(k == KT - 1))
                        ins.then_inc(up_mm, 1)
                        e.wait_ge(u_ok, n + 1)
                        e.wait_ge(res_ok, i * 2)
                        for c in range(2):
                            for j in range(FJ):
                                ins = e.matmul(O[0:T, p, c, 0:HALF], uT[:, p, j], wd[:, j, c * HALF:(c + 1) * HALF],
                                               start=(j == 0), stop=(j == FJ - 1))
                        ins.then_inc(dn_mm, 1)

            @block.scalar
            def _(e):
                with e.Fori(0, NT // 2) as i:
                    for p in range(2):
                        n = i * 2 + p
                        e.wait_ge(tr_mm, n + 1)
                        e.wait_ge(mm, i * 2)
                        e.activation(stage[:, p].rearrange("p (c k) t -> p c (k t)", c=2), TR[:, p, :, 0:3 * T],
                                     ACT.Copy).then_inc(st_ok, 1)
                e.wait_ge(var_ok, 1)
                e.activation(std[:], veps[:], ACT.Sqrt).then_inc(std_ok, 1)
                e.wait_ge(b_in, 80)
                e.wait_ge(mm, NT)
                with e.Fori(0, NT // 2) as i:
                    for p in range(2):
                        n = i * 2 + p
                        e.wait_ge(zt_mm, n + 1)
                        for k in range(KT):
                            ins = e.activation(stage[:, p, k], TR[:, 0, k // 3, k % 3 * T:(k % 3 + 1) * T], ACT.Identity,
                                               bias=shift[:, k:k + 1], scale=gain[:, k:k + 1])
                        ins.then_inc(zs_ok, 1)
                        e.wait_ge(up_mm, n + 1)
                        e.wait_ge(dn_mm, i * 2)
                        for j in range(FJ):
                            ins = e.activation(uT[:, p, j], TR[:, 1, p, j * T:(j + 1) * T], ACT.Gelu, bias=bu[:, j:j + 1])
                        ins.then_inc(u_ok, 1)

            @block.vector
            def _(e):
                seq = Tally(e, dve)
                e.wait_ge(b_in, 80)
                for y in y_in:
                    e.wait_ge(y, 16)
                with e.Fori(0, NT // 2) as i:
                    for p in range(2):
                        n = i * 2 + p
                        e.wait_ge(mm, n + 1)
                        e.tensor_tensor(split(z[:, p]), O[0:T, p, :, 0:HALF], split(bo[:]), ALU.add).then_inc(add_ok, 1)
                        e.wait_ge(add_ok, n + 1)
                        e.tensor_tensor(x2[:, n, :], x2[:, n, :], z[:, p], ALU.add).then_inc(x2_ok, 1)
                e.wait_ge(x2_ok, NT)
                norm_stats(e, seq, x2, stats, mv, veps).then_inc(var_ok, 1)
                e.wait_ge(std_ok, 1)
                newton_rstd(e, seq, rstd[:], std[:], veps[:], tmp[:])
                with e.Fori(0, NT // 2) as i:
                    for p in range(2):
                        n = i * 2 + p
                        e.wait_ge(zt_mm, n)
                        e.tensor_scalar(z[:, p], x2[:, n, :], mv[:, n, 0:1], rstd[:, bass.ds(n, 1)],
                                        ALU.subtract, ALU.mult).then_inc(z_ok, 1)
                        e.wait_ge(in_[p], i * 16 + 16)
                        e.tensor_tensor(xt[:, p], xt[:, p], x2[:, n, :], ALU.add).then_inc(xt_ok, 1)
                        e.wait_ge(xt_ok, 2 * n + 1)
                        e.tensor_tensor(xt[:, p], xt[:, p], bd[:], ALU.add).then_inc(xt_ok, 1)
                        e.wait_ge(dn_mm, n + 1)
                        e.wait_ge(xt_ok, 2 * n + 2)
                        e.wait_ge(sent[p], i * 16)
                        e.tensor_tensor(split(res[:, p]), O[0:T, p, :, 0:HALF], split(xt[:, p]), ALU.add).then_inc(res_ok, 1)


def graph_transformer_layer(
    nc: bass.Bass,
    x: bass.AP,
    src: bass.AP,
    dst: bass.AP,
    gnn_W_ah: bass.AP,
    gnn_b_ah: bass.AP,
    gnn_W0: bass.AP,
    gnn_a_src0: bass.AP,
    gnn_a_dst0: bass.AP,
    gnn_b0: bass.AP,
    gnn_W1: bass.AP,
    gnn_a_src1: bass.AP,
    gnn_a_dst1: bass.AP,
    gnn_b1: bass.AP,
    gnn_W2: bass.AP,
    gnn_a_src2: bass.AP,
    gnn_a_dst2: bass.AP,
    gnn_b2: bass.AP,
    gnn_W_out: bass.AP,
    gnn_b_out: bass.AP,
    mix_Wq: bass.AP,
    mix_Wk: bass.AP,
    mix_Wv: bass.AP,
    mix_Wo: bass.AP,
    mix_proj: bass.AP,
    ffn_q_w: bass.AP,
    ffn_q_b: bass.AP,
    ffn_k_w: bass.AP,
    ffn_k_b: bass.AP,
    ffn_ao_w: bass.AP,
    ffn_ao_b: bass.AP,
    ffn_recipe: bass.AP,
    ffn_ctx_pat: bass.AP,
    ffn_basis_emb: bass.AP,
    ffn_basis_A: bass.AP,
    ffn_vout_w: bass.AP,
    ffn_vout_b: bass.AP,
    ffn_up_w: bass.AP,
    ffn_up_b: bass.AP,
    ffn_down_w: bass.AP,
    ffn_down_b: bass.AP,
    ffn_n1_g: bass.AP,
    ffn_n1_b: bass.AP,
    ffn_n2_g: bass.AP,
    ffn_n2_b: bass.AP,
    out: bass.AP,
):
    g = Env()
    g.x = x
    g.src = src
    g.dst = dst
    g.gnn_W_ah = gnn_W_ah
    g.gnn_b_ah = gnn_b_ah
    g.gnn_W0 = gnn_W0
    g.gnn_a_src0 = gnn_a_src0
    g.gnn_a_dst0 = gnn_a_dst0
    g.gnn_b0 = gnn_b0
    g.gnn_W1 = gnn_W1
    g.gnn_a_src1 = gnn_a_src1
    g.gnn_a_dst1 = gnn_a_dst1
    g.gnn_b1 = gnn_b1
    g.gnn_W2 = gnn_W2
    g.gnn_a_src2 = gnn_a_src2
    g.gnn_a_dst2 = gnn_a_dst2
    g.gnn_b2 = gnn_b2
    g.gnn_W_out = gnn_W_out
    g.gnn_b_out = gnn_b_out
    g.mix_Wq = mix_Wq
    g.mix_Wk = mix_Wk
    g.mix_Wv = mix_Wv
    g.mix_Wo = mix_Wo
    g.mix_proj = mix_proj
    g.ffn_q_w = ffn_q_w
    g.ffn_q_b = ffn_q_b
    g.ffn_k_w = ffn_k_w
    g.ffn_k_b = ffn_k_b
    g.ffn_ao_w = ffn_ao_w
    g.ffn_ao_b = ffn_ao_b
    g.ffn_recipe = ffn_recipe
    g.ffn_ctx_pat = ffn_ctx_pat
    g.ffn_basis_emb = ffn_basis_emb
    g.ffn_basis_A = ffn_basis_A
    g.ffn_vout_w = ffn_vout_w
    g.ffn_vout_b = ffn_vout_b
    g.ffn_up_w = ffn_up_w
    g.ffn_up_b = ffn_up_b
    g.ffn_down_w = ffn_down_w
    g.ffn_down_b = ffn_down_b
    g.ffn_n1_g = ffn_n1_g
    g.ffn_n1_b = ffn_n1_b
    g.ffn_n2_g = ffn_n2_g
    g.ffn_n2_b = ffn_n2_b
    g.out = out
    g.TABLE_ZERO = 16 * (NT // 2 + 1)
    scratch = lambda n, s: nc.dram_tensor(n, s, F32, kind="Internal").ap()
    g.table = scratch("edge_table", (CELLS + T, 1))
    g.mix_out = scratch("mixer_out", (N, D))
    g.rows, g.uv = scratch("score_rows", (2 * GI, N)), scratch("score_uv", (2 * GI, N))
    g.h = scratch("gnn_h", (GI, N, GC))
    g.node = scratch("gnn_nodes", (N, GL * D))
    g.xj, g.y_dram = scratch("residual", (N, D)), scratch("normed_residual", (N, D))
    g.sem = lambda n: nc.alloc_semaphore(name=n)
    keep = lambda scope, n, s, d=F32: scope.enter_context(nc.sbuf_tensor(n, s, d))
    with ExitStack() as whole:
        g.ident = keep(whole, "ident", [128, 128])
        with nc.cleanup_on_exit(), ExitStack() as gnn:
            g.table_sem, g.scattered = g.sem("table_zeroed"), g.sem("scattered")
            g.asad, g.as02 = keep(gnn, "asad", [T, NT, 2 * GI]), keep(gnn, "as02", [T, NT, GI])
            with ExitStack() as first:
                g.edge_add, g.edge_cell = keep(first, "edge_add", [T, EB]), keep(first, "edge_cell", [T, EB], I32)
                with ExitStack() as values:
                    g.xnT = keep(values, "xnT", [128, KT, N])
                    g.v = keep(values, "mix_v", [T, NT, MH * (DH + 1)])
                    front(nc, g)
                    mix(nc, g, range(EB))
                lift(nc, g)
            graph(nc, g)
        with nc.cleanup_on_exit(), ExitStack() as ffn:
            g.y = g.ao = keep(ffn, "y", [T, NT, D])
            g.stats = keep(ffn, "stats", [T, NT, 12])
            join(nc, g)
            with ExitStack() as attention:
                g.v = keep(attention, "ffn_v", [T, NT, MH * (DH + 1)])
                g.nTh, g.nTl = keep(attention, "normed_high", [128, KT, N], F32R), keep(attention, "normed_low", [128, KT, N], F32R)
                route(nc, g)
                attend(nc, g)
            tail(nc, g)


_INS = ['x', 'src', 'dst', 'L0_gnn_W_ah', 'L0_gnn_b_ah', 'L0_gnn_W0', 'L0_gnn_a_src0', 'L0_gnn_a_dst0', 'L0_gnn_b0', 'L0_gnn_W1', 'L0_gnn_a_src1', 'L0_gnn_a_dst1', 'L0_gnn_b1', 'L0_gnn_W2', 'L0_gnn_a_src2', 'L0_gnn_a_dst2', 'L0_gnn_b2', 'L0_gnn_W_out', 'L0_gnn_b_out', 'L0_mix_Wq', 'L0_mix_Wk', 'L0_mix_Wv', 'L0_mix_Wo', 'L0_mix_proj', 'L0_ffn_q_w', 'L0_ffn_q_b', 'L0_ffn_k_w', 'L0_ffn_k_b', 'L0_ffn_ao_w', 'L0_ffn_ao_b', 'L0_ffn_recipe', 'L0_ffn_ctx_pat', 'L0_ffn_basis_emb', 'L0_ffn_basis_A', 'L0_ffn_vout_w', 'L0_ffn_vout_b', 'L0_ffn_up_w', 'L0_ffn_up_b', 'L0_ffn_down_w', 'L0_ffn_down_b', 'L0_ffn_n1_g', 'L0_ffn_n1_b', 'L0_ffn_n2_g', 'L0_ffn_n2_b']


def kernel(**inputs):
    import numpy as _np
    import concourse.bacc as _bacc
    from concourse import mybir as _mybir
    from concourse.bass_utils import run_bass_kernel_spmd as _run

    nc = _bacc.Bacc("TRN2", target_bir_lowering=False, num_devices=1)
    arrays, args = {}, []
    for name in _INS:
        a = _np.ascontiguousarray(inputs[name])
        arrays[f"in_{name}_dram"] = a
        args.append(nc.dram_tensor(f"in_{name}_dram", a.shape, _mybir.dt.from_np(a.dtype), kind="ExternalInput").ap())
    args.append(nc.dram_tensor("out_0_dram", (1250, 768), _mybir.dt.float32, kind="ExternalOutput").ap())
    graph_transformer_layer(nc, *args)
    r = _run(nc, [arrays], core_ids=[0])
    return r.results[0]["out_0_dram"]
```

```python
from contextlib import ExitStack

import concourse.bass as bass
from concourse import mybir

F32 = mybir.dt.float32
I32 = mybir.dt.int32
U32 = mybir.dt.uint32
BF16 = mybir.dt.bfloat16
F32R = mybir.dt.float32r
ALU = mybir.AluOpType
ACT = mybir.ActivationFunctionType
AX = mybir.AxisListType

N, D = 1250, 768
T, NT = 125, 10
KT = D // 128
HALF = D // 2
E = 20000
EB = E // T
EG = EB // 4
GH, GC, GL = 4, 192, 3
GI = GL * GH
MH, DH = 12, 64
MP = MH // 2
M = 256
NB, RANK, NN = 32, 64, 96
FF = 384
FJ = FF // 128
LN_EPS = 1e-5
MIX_EPS = 1e-4
NEG = -1e30
CHUNKS = [(0, 512), (512, 512), (1024, 226)]
CELLS = N * N


class Tally:

    def __init__(self, eng, sem):
        self.eng, self.sem, self.n, self.i, self.per, self.start = eng, sem, 0, None, 0, 0

    def mark(self, ins):
        ins.then_inc(self.sem, 1)
        self.n += 1

    def settle(self):
        self.eng.wait_ge(self.sem, self.n if self.i is None else self.i * self.per + self.n)

    def step(self, ins):
        self.mark(ins)
        self.settle()

    def enter(self, i, per):
        self.i, self.per, self.start = i, per, self.n

    def leave(self, times):
        assert self.n - self.start == self.per, (self.n - self.start, self.per)
        self.n, self.i = self.start + self.per * times, None


class Env:
    pass


def shared(nc, sb, first, *later):
    name, shape, dtype = first
    with nc.sbuf_tensor(name, shape, dtype) as old:
        pass
    return [old] + [sb(*x) for x in later]


def weight_view(w):
    return w.rearrange("(k p) n -> p k n", p=128)


def strided_view(w):
    return w.rearrange("(p k) n -> p k n", p=128)


def node_view(x):
    return x.rearrange("(t p) d -> p t d", p=T)


def norm_stats(v, tally, src, stats, mv, veps):
    for t in range(NT):
        for c in range(2):
            tally.mark(v.bn_stats(stats[:, t, 6 * c:6 * c + 6], src[:, t, c * HALF:(c + 1) * HALF]))
    tally.settle()
    for t in range(NT):
        tally.mark(v.bn_aggr(mv[:, t, :], stats[:, t, :]))
    tally.settle()
    return v.tensor_scalar(veps[:, :], mv[:, :, 1], LN_EPS, None, ALU.add)


def newton_rstd(v, tally, rstd, std, veps, tmp):
    tally.step(v.reciprocal(rstd, std))
    tally.step(v.tensor_tensor(tmp, rstd, rstd, ALU.mult))
    tally.step(v.tensor_tensor(tmp, tmp, veps, ALU.mult))
    tally.step(v.tensor_scalar(tmp, tmp, -0.5, 1.5, ALU.mult, ALU.add))
    tally.step(v.tensor_tensor(rstd, rstd, tmp, ALU.mult))


def front(nc, g):
    with ExitStack() as ctx:
        sb = lambda n, s, d=F32: ctx.enter_context(nc.sbuf_tensor(n, s, d))
        ps = lambda n, s: ctx.enter_context(nc.psum_tensor(n, s, F32))
        sem = g.sem
        x = sb("fr_x", [T, NT, D])
        wv = sb("fr_wv", [128, KT, D])
        stage = sb("fr_stage", [128, 2, KT, T])
        wvh, wvl = sb("fr_wvh", [128, KT, D], F32R), sb("fr_wvl", [128, KT, D], F32R)
        sh, sl = sb("fr_sh", [128, 2, KT, T], F32R), sb("fr_sl", [128, 2, KT, T], F32R)
        wvh_ok, wvl_ok, sh_ok, sl_ok, started = (sem(f"fr_{n}") for n in ("wvh_ok", "wvl_ok", "sh_ok", "sl_ok", "started"))
        stats, mv = sb("fr_stats", [T, NT, 12]), sb("fr_mv", [T, NT, 2])
        veps, std, rstd = (sb(f"fr_{n}", [T, NT]) for n in ("veps", "std", "rstd"))
        tmp = sb("fr_tmp", [T, NT])
        zeros = sb("fr_zeros", [T, 2 * N])
        srci, dsti = sb("fr_src", [T, EB], I32), sb("fr_dst", [T, EB], I32)
        key, tot = sb("fr_key", [T, EB + 4]), sb("fr_tot", [T, EB])
        xn = sb("fr_xn", [T, 2, D])
        ones = sb("fr_ones", [T, T])
        before = sb("fr_before", [T, T])
        spare = sb("fr_spare", [T, 1])
        sparei = sb("fr_sparei", [T, 1], I32)
        diag = sb("fr_diag", [T, 2, 4, T])
        junk = sb("fr_junk", [T, 2, 4, T])
        first, idxf = sb("fr_first", [T, EB]), sb("fr_idxf", [T, EB])
        tr = ps("fr_tr", [128, 2, 2, 512])
        vps = ps("fr_vps", [128, 2, 512])
        kps = ps("fr_kps", [128, 2, 512])
        x_in, e_in, wv_in = sem("fr_x_in"), sem("fr_e_in"), sem("fr_wv_in")
        zeroed, setup, spare_ok = sem("fr_zeroed"), sem("fr_setup"), sem("fr_spare_ok")
        dve, pool = sem("fr_dve"), sem("fr_pool")
        var_ok, std_ok, xn_ok = sem("fr_var"), sem("fr_std"), sem("fr_xn_ok")
        tr_ok, st_ok, xnT_ok, v_ok, v_out = (sem(f"fr_{n}") for n in ("tr_ok", "st_ok", "xnT_ok", "v_ok", "v_out"))
        diag_ok, row_ok, row_used = sem("fr_diag_ok"), sem("fr_row_ok"), sem("fr_row_used")

        is_first = lambda n: isinstance(n, int) and n == 0

        def over_tiles(e, pair):
            pair(0)
            with e.Fori(1, NT // 2) as i:
                pair(i)

        with nc.Block() as block:
            @block.sync
            def _(sp):
                sp.dma_start(x[:], node_view(g.x)).then_inc(x_in, 16)
                sp.dma_start(srci[:], g.src.rearrange("(p b) -> p b", p=T)).then_inc(e_in, 16)
                sp.dma_start(dsti[:], g.dst.rearrange("(p b) -> p b", p=T)).then_inc(e_in, 16)
                sp.dma_start(wv[:], weight_view(g.mix_Wv)).then_inc(wv_in, 16)
                sp.wait_ge(zeroed, 1)
                cells = g.table[0:CELLS].rearrange("(q p r) o -> q p (r o)", p=T, r=2 * N)
                for q in range(NT // 2):
                    sp.dma_start(cells[q], zeros[:]).then_inc(g.table_sem, 16)
                sp.dma_start(g.table[CELLS:CELLS + T], zeros[:, 0:1]).then_inc(g.table_sem, 16)
                sp.wait_ge(g.table_sem, g.TABLE_ZERO)

            @block.gpsimd
            def _(e):
                seq = Tally(e, pool)
                seq.step(e.memset(g.ident[:], 0.0))
                seq.step(e.affine_select(out=g.ident[:], in_=g.ident[:], compare_op=ALU.not_equal, fill=1.0,
                                         base=0, pattern=[[-1, 128]], channel_multiplier=1))
                e.memset(zeros[:], 0.0).then_inc(zeroed, 1)
                e.memset(ones[:], 1.0).then_inc(setup, 1)
                seq.step(e.memset(before[:], float(1 + 2 * T)))
                e.affine_select(out=before[:], in_=before[:], compare_op=ALU.is_gt, fill=1.0,
                                base=0, pattern=[[-1, T]], channel_multiplier=1).then_inc(setup, 1)
                e.memset(g.v[:], 1.0).then_inc(setup, 1)
                e.iota(sparei[:], pattern=[[0, 1]], base=CELLS, channel_multiplier=1).then_inc(spare_ok, 1)
                with e.Fori(0, NT // 2) as i:
                    for par in range(2):
                        n = i * 2 + par
                        e.wait_ge(st_ok, n + 1)
                        e.wait_ge(v_ok, n + 1)
                        e.sem_inc(started, 1)
                        e.tensor_copy(sh[:, par], stage[:, par]).then_inc(sh_ok, 1)
                        e.wait_ge(sh_ok, n + 1)
                        e.sem_inc(started, 1)
                        e.tensor_tensor(sl[:, par], stage[:, par], sh[:, par].bitcast(F32), ALU.subtract).then_inc(sl_ok, 1)
                        e.tensor_copy(g.xnT[:, :, bass.ds(n * T, T)], stage[:, par]).then_inc(xnT_ok, 1)

            @block.vector
            def _(e):
                seq = Tally(e, dve)
                e.wait_ge(x_in, 16)
                norm_stats(e, seq, x, stats, mv, veps).then_inc(var_ok, 1)
                e.wait_ge(e_in, 32)
                seq.mark(e.memset(key[:, EB:EB + 4], 0.0))
                seq.mark(e.scalar_tensor_tensor(out=key[:, 0:EB], in0=srci[:], scalar=float(N), in1=dsti[:],
                                                op0=ALU.mult, op1=ALU.add))
                e.wait_ge(std_ok, 1)
                newton_rstd(e, seq, rstd[:], std[:], veps[:], tmp[:])
                e.wait_ge(setup, 2)

                def spread(n, slot):
                    e.tensor_tensor(diag[:, slot], g.ident[0:T, 0:T].unsqueeze(1).to_broadcast([T, 4, T]),
                                    key[:, bass.ds(n * 4, 4)].unsqueeze(2).to_broadcast([T, 4, T]),
                                    ALU.mult).then_inc(diag_ok, 1)

                spread(0, 0)

                def pair(i):
                    for par in range(2):
                        n = i * 2 + par
                        e.wait_ge(tr_ok, n)
                        e.tensor_scalar(xn[:, par], x[:, n, :], mv[:, n, 0:1], rstd[:, bass.ds(n, 1)],
                                        ALU.subtract, ALU.mult).then_inc(xn_ok, 1)
                        if isinstance(n, int) and n == 1:
                            for k in range(KT):
                                e.wait_ge(wvh_ok, k + 1)
                                e.tensor_tensor(wvl[:, k], wv[:, k], wvh[:, k].bitcast(F32), ALU.subtract).then_inc(wvl_ok, 1)
                        for q in range(4):
                            grp = n * 4 + q
                            e.wait_ge(row_ok, grp)
                            spread(grp + 1, (q + 1) % 2)
                            e.wait_ge(row_ok, grp + 1)
                            e.wait_ge(row_used, grp)
                            for j in range(4):
                                ins = e.scalar_tensor_tensor(
                                    out=junk[:, q % 2, j], in0=kps[0:T, q % 2, j * T:(j + 1) * T],
                                    scalar=key[:, bass.ds(grp * 4 + j, 1)], in1=before[:], op0=ALU.is_equal,
                                    op1=ALU.mult, accum_out=tot[:, bass.ds(grp * 4 + j, 1)])
                            ins.then_inc(row_used, 1)

                over_tiles(e, pair)
                e.wait_ge(row_used, EG + 1)
                e.wait_ge(spare_ok, 1)
                seq.mark(e.tensor_copy(spare[:], sparei[:]))
                seq.step(e.tensor_scalar(first[:], tot[:], float(2 * T), None, ALU.is_lt))
                seq.mark(e.tensor_tensor(g.edge_add[:], tot[:], first[:], ALU.mult))
                seq.step(e.scalar_tensor_tensor(out=idxf[:], in0=key[:, 0:EB], scalar=spare[:], in1=first[:],
                                                op0=ALU.subtract, op1=ALU.mult))
                seq.step(e.tensor_scalar(g.edge_cell[:], idxf[:], spare[:], None, ALU.add))

            @block.scalar
            def _(e):
                e.wait_ge(var_ok, 1)
                e.activation(std[:], veps[:], ACT.Sqrt).then_inc(std_ok, 1)
                e.wait_ge(setup, 3)

                def values_out(n):
                    e.wait_ge(v_ok, n + 3)
                    e.activation(g.v[:, n, :].rearrange("p (c h d) -> p c h d", c=2, h=MP)[:, :, :, 0:DH],
                                 vps[0:T, :, 0:HALF].rearrange("p c (h d) -> p c h d", h=MP), ACT.Copy).then_inc(v_out, 1)

                def pair(i):
                    for par in range(2):
                        n = i * 2 + par
                        e.wait_ge(tr_ok, n + 1)
                        e.wait_ge(xnT_ok, n)
                        e.activation(stage[:, par].rearrange("p (c k) t -> p c (k t)", c=2),
                                     tr[:, par, :, 0:3 * T], ACT.Copy).then_inc(st_ok, 1)
                        if is_first(n):
                            e.wait_ge(wv_in, 16)
                            for k in range(KT):
                                e.activation(wvh[:, k], wv[:, k], ACT.Copy).then_inc(wvh_ok, 1)
                        else:
                            values_out(n - 1)

                over_tiles(e, pair)
                values_out(NT - 1)

            @block.tensor
            def _(e):
                e.wait_ge(setup, 3)
                e.sem_inc(row_used, 1)
                e.sem_inc(v_ok, 2)

                def values(n, p, c, ks):
                    if c == 0 and ks[0] == 0:
                        e.wait_ge(sl_ok, n + 1)
                        if not is_first(n):
                            e.wait_ge(v_out, n)
                        e.wait_ge(wvl_ok, KT)
                    for k in ks:
                        for x, w in ((sh, wvh), (sh, wvl), (sl, wvh)):
                            ins = e.matmul(vps[0:T, c, 0:HALF], x[:, p, k], w[:, k, c * HALF:(c + 1) * HALF],
                                           start=(k == 0 and x is sh and w is wvh), stop=(k == KT - 1 and x is sl))
                    if c == 1 and ks[-1] == KT - 1:
                        ins.then_inc(v_ok, 1)

                def pair(i):
                    for par in range(2):
                        n = i * 2 + par
                        e.wait_ge(xn_ok, n + 1)
                        for k in range(KT):
                            ins = e.transpose(tr[:, par, k // 3, (k % 3) * T:(k % 3 + 1) * T],
                                              xn[:, par, k * 128:(k + 1) * 128], g.ident[0:T, 0:T])
                        ins.then_inc(tr_ok, 1)
                        for q in range(4):
                            grp = n * 4 + q
                            e.wait_ge(diag_ok, grp + 1)
                            e.wait_ge(row_used, grp)
                            e.matmul(kps[0:T, q % 2, 0:4 * T], ones[:], diag[:, q % 2].rearrange("p j f -> p (j f)"),
                                     start=True, stop=True).then_inc(row_ok, 1)
                            if not is_first(n):
                                values(n - 1, 1 - par, q // 2, range(q % 2 * 3, q % 2 * 3 + 3))

                over_tiles(e, pair)
                for q in range(4):
                    values(NT - 1, 1, q // 2, range(q % 2 * 3, q % 2 * 3 + 3))


def scatter_counts(e, g, blocks):
    for b in blocks:
        if b > 0:
            e.wait_ge(g.scattered, 16 * b)
        e.indirect_dma_start(out=g.table, out_offset=bass.IndirectOffsetOnAxis(
            ap=g.edge_cell[:, b:b + 1].bitcast(U32), axis=0), in_=g.edge_add[:, b:b + 1], in_offset=None,
            compute_op=ALU.add, bounds_check=CELLS + T - 1).then_inc(g.scattered, 16)
    e.wait_ge(g.scattered, 16 * (blocks[-1] + 1))


def mix(nc, g, blocks):
    NORM = DH ** -0.25
    RATIO = M ** -0.5
    W2 = 2 * (DH + 1)
    with ExitStack() as ctx:
        sb = lambda n, s, d=F32: ctx.enter_context(nc.sbuf_tensor("mx_" + n, s, d))
        ps = lambda n, s: ctx.enter_context(nc.psum_tensor("mx_" + n, s, F32))
        sem = lambda n: g.sem("mx_" + n)
        wk, wq = sb("wk", [128, KT, 128]), sb("wq", [128, KT, 128])
        wo, wol = shared(nc, sb, ("mx_wo", [128, KT, D], F32), ("wol", [128, KT, D], F32R))
        proj2 = sb("proj2", [128, 2, 2, DH])
        fraw, fh, fl = sb("fraw", [128, M]), sb("fh", [128, M], F32R), sb("fl", [128, M], F32R)
        halves = sb("halves", [128, 128])
        ones2 = sb("ones2", [2, T])
        lin, sq = sb("lin", [128, N]), sb("sq", [128, N])
        kk, qq = sb("kk", [128, 2, N], F32R), sb("qq", [128, 2, N], F32R)
        head = [slice(0, DH), slice(DH, 128)]
        dk, dq = sb("dk", [T, NT, 2]), sb("dq", [T, NT, 2])
        kf, woh, _ = shared(nc, sb, ("mx_kf", [T, NT, 2 * M], F32), ("woh", [128, KT, D], F32R),
                            ("woh_rest", [128, NT * 2 * M - KT * D], F32))
        khalf = sb("khalf", [T, 2, 2])
        kmax, gmax, gdiag, kbias = sb("kmax", [T, 2]), sb("gmax", [2, 1]), sb("gdiag", [2, 2]), sb("kbias", [T, NT, 2])
        cx = sb("cx", [128, 2, 2 * W2])
        qm, nb, rc = sb("qm", [T, 2, 2]), sb("nb", [T, 2, 2]), sb("rc", [T, 2, 2])
        qf = sb("qf", [T, 3, 2 * M])
        qfT = sb("qfT", [128, 2, 4, T])
        mo = sb("mo", [T, NT, D])
        sh, sl = sb("sh", [128, 2, KT, T], F32R), sb("sl", [128, 2, KT, T], F32R)
        res = sb("res", [T, 2, D])
        LQ, DD, TT, CO = ps("LQ", [128, 3 * 512]), ps("DD", [128, 2, 512]), ps("TT", [128, 2, 512]), ps("CO", [128, 512])
        wk_in, wq_in, wo_in, pr_in = sem("wk_in"), sem("wq_in"), sem("wo_in"), sem("pr_in")
        pset, ptr, pdone, sp_ok = sem("pset"), sem("ptr"), sem("pdone"), sem("sp_ok")
        woh_ok, wol_ok = sem("woh_ok"), sem("wol_ok")
        klin, qlin = sem("klin"), sem("qlin")
        kdg, qdg, d_out = sem("kdg"), sem("qdg"), sem("d_out")
        kdd, kf_ok, kmax_ok, kmT, gd_ok, kmB, kb_ok = (sem(n) for n in ("kdd", "kf_ok", "kmax_ok", "kmT", "gd_ok", "kmB", "kb_ok"))
        ke_ok, kp_ok, cx_ok, cx_out = sem("ke_ok"), sem("kp_ok"), sem("cx_ok"), sem("cx_out")
        qdd, nb_ok, qe_ok, qp_ok, qtr, qfT_ok, out_ok, mo_ok = (
            sem(n) for n in ("qdd", "nb_ok", "qe_ok", "qp_ok", "qtr", "qfT_ok", "out_ok", "mo_ok"))
        otr, ost, olo, omm, ores = (sem(n) for n in ("otr", "ost", "olo", "omm", "ores"))
        sent = [sem("sent0"), sem("sent1")]
        kh_ok, sq_ok = sem("kh_ok"), sem("sq_ok")
        gmax_ok, qm_ok, rc_ok, lin_ok = sem("gmax_ok"), sem("qm_ok"), sem("rc_ok"), sem("lin_ok")
        tile = lambda t: slice(t * T, (t + 1) * T)

        def over_pairs(e, pair):
            with e.Fori(0, MP - 1) as m:
                pair(m, False)
            pair(MP - 1, True)

        with nc.Block() as block:
            @block.sync
            def _(sp):
                for c in range(2):
                    for d in range(2):
                        sp.dma_start(proj2[:, c, d], g.mix_proj[c * 128:(c + 1) * 128, :]).then_inc(pr_in, 16)
                for w, dram, into, used in ((wk, g.mix_Wk, wk_in, None), (wq, g.mix_Wq, wq_in, None)):
                    sp.dma_start(w[:], weight_view(dram)[:, :, 0:128]).then_inc(into, 16)
                sp.dma_start(wo[:], weight_view(g.mix_Wo)).then_inc(wo_in, 16)
                with sp.Fori(1, MP) as m:
                    sp.wait_ge(klin, m)
                    sp.dma_start(wk[:], weight_view(g.mix_Wk)[:, :, bass.ds(m * 128, 128)]).then_inc(wk_in, 16)
                    sp.wait_ge(qlin, m)
                    sp.dma_start(wq[:], weight_view(g.mix_Wq)[:, :, bass.ds(m * 128, 128)]).then_inc(wq_in, 16)
                for t in range(NT):
                    sp.wait_ge(ores, t + 1)
                    sp.dma_start(g.mix_out[tile(t), :], res[:, t % 2]).then_inc(sent[t % 2], 16)
                for s in sent:
                    sp.wait_ge(s, 16 * NT // 2)

            @block.gpsimd
            def _(e):
                e.memset(ones2[:], 1.0).then_inc(pset, 1)
                e.memset(halves[:], 0.0).then_inc(pset, 1)
                e.wait_ge(pset, 2)
                e.memset(halves[0:DH, 0:DH], 0.5).then_inc(pset, 1)
                e.memset(halves[DH:128, DH:128], 0.5).then_inc(pset, 1)
                e.wait_ge(pset, 4)
                scatter_counts(e, g, blocks)

            @block.tensor
            def _(e):
                e.wait_ge(pr_in, 64)
                for c in range(2):
                    ins = e.transpose(CO[:, c * 128:(c + 1) * 128], proj2[:, c].rearrange("p a b -> p (a b)"), g.ident[:])
                ins.then_inc(ptr, 1)
                e.wait_ge(pdone, 3)
                e.wait_ge(pset, 4)

                def linear(w, steps=range(3 * KT)):
                    for s in steps:
                        (a, n), k = CHUNKS[s // KT], s % KT
                        ins = e.matmul(LQ[:, a:a + n], w[:, k], g.xnT[:, k, a:a + n], start=(k == 0), stop=(k == KT - 1))
                    return ins

                def features(x, t, bank):
                    for h in range(2):
                        for f in (fh, fl):
                            ins = e.matmul(DD[0:T, bank, h * M:(h + 1) * M], x[:, h, tile(t)], f[:], start=(f is fh), stop=(f is fl))
                    return ins

                def norms(j, bank):
                    for c in range(2):
                        ins = e.matmul(DD[0:T, bank, c * 128:(c + 1) * 128], sq[:, tile(2 * j + c)], halves[:],
                                       start=True, stop=True)
                    return ins

                def pair(m, last):
                    e.wait_ge(sq_ok, m * 2 + 1)
                    for j in range(5):
                        e.wait_ge(qe_ok, m * NT) if j < 2 else e.wait_ge(d_out, m * 10 + j - 1)
                        norms(j, j % 2).then_inc(kdg, 1)
                    for t in range(NT):
                        e.wait_ge(d_out, m * 10 + 4 + t) if t < 2 else e.wait_ge(kf_ok, m * NT + t - 1)
                        if t == 0:
                            e.wait_ge(sp_ok, m * 8 + 4)
                        features(kk, t, (t + 1) % 2).then_inc(kdd, 1)
                    e.wait_ge(wq_in, m * 16 + 16)
                    e.wait_ge(lin_ok, m * 2 + 1)
                    linear(wq, range(0, 7))
                    e.wait_ge(kmax_ok, m + 1)
                    e.wait_ge(mo_ok, m * NT)
                    e.transpose(CO[0:2, 0:T], kmax[:], g.ident[0:T, 0:T]).then_inc(kmT, 1)
                    linear(wq, range(7, 9))
                    e.wait_ge(gd_ok, m + 1)
                    e.matmul(CO[0:T, 0:2], ones2[:], gdiag[:], start=True, stop=True).then_inc(kmB, 1)
                    linear(wq, range(9, 18)).then_inc(qlin, 1)
                    for h in range(2):
                        if h == 1:
                            e.wait_ge(sq_ok, m * 2 + 2)
                            for j in range(5):
                                e.wait_ge(kf_ok, m * NT + 9 + j) if j < 2 else e.wait_ge(d_out, m * 10 + 5 + j - 1)
                                norms(j, (j + 1) % 2).then_inc(qdg, 1)
                        e.wait_ge(qfT_ok, m * NT)
                        for c in range(2):
                            for t in range(NT):
                                if h == 0 and c == 0 and t % 5 == 0:
                                    e.wait_ge(kp_ok, m * 2 + t // 5 + 1)
                                ins = e.matmul(TT[:, h, c * W2:(c + 1) * W2], kf[:, t, h * M + c * 128:h * M + (c + 1) * 128],
                                               g.v[:, t, bass.ds(m * W2, W2)], start=(t == 0), stop=(t == NT - 1))
                        ins.then_inc(cx_ok, 1)
                    for s in range(NT + 3):
                        if s < NT:
                            e.wait_ge(d_out, m * 10 + 9 + s) if s < 2 else e.wait_ge(qe_ok, m * NT + s - 1)
                            if s == 0:
                                e.wait_ge(sp_ok, m * 8 + 8)
                            features(qq, s, s % 2).then_inc(qdd, 1)
                        t = s - 2
                        if 0 <= t < NT:
                            e.wait_ge(qp_ok, m * NT + t + 1)
                            e.wait_ge(cx_out, m * 2 + 2) if t < 2 else e.wait_ge(qfT_ok, m * NT + t - 1)
                            for c in range(4):
                                ins = e.transpose(TT[:, t % 2, c * T:(c + 1) * T], qf[:, t % 3, c * 128:(c + 1) * 128],
                                                  g.ident[0:T, 0:T])
                            ins.then_inc(qtr, 1)
                        t = s - 3
                        if t >= 0:
                            e.wait_ge(qfT_ok, m * NT + t + 1)
                            e.wait_ge(mo_ok, m * NT + t)
                            for h in range(2):
                                for c in range(2):
                                    ins = e.matmul(CO[0:T, h * W2:(h + 1) * W2], qfT[:, t % 2, 2 * h + c],
                                                   cx[:, h, c * W2:(c + 1) * W2], start=(c == 0), stop=(c == 1))
                            ins.then_inc(out_ok, 1)
                        if not last and s < 9:
                            if s == 0:
                                e.wait_ge(wk_in, m * 16 + 32)
                                e.wait_ge(lin_ok, m * 2 + 2)
                            ins = linear(wk, range(2 * s, 2 * s + 2))
                            if s == 8:
                                ins.then_inc(klin, 1)

                e.wait_ge(wk_in, 16)
                linear(wk).then_inc(klin, 1)
                over_pairs(e, pair)
                e.wait_ge(wo_in, 16)
                e.wait_ge(mo_ok, MP * NT)
                e.wait_ge(qfT_ok, MP * NT)
                for t in range(NT + 1):
                    if t < NT:
                        if t > 0:
                            e.wait_ge(olo, t)
                        for k in range(KT):
                            ins = e.transpose(LQ[:, k // 3 * 512 + k % 3 * T:k // 3 * 512 + (k % 3 + 1) * T],
                                              mo[:, t, k * 128:(k + 1) * 128], g.ident[0:T, 0:T])
                        ins.then_inc(otr, 1)
                    if t > 0:
                        u = t - 1
                        bank = (DD, TT)[u % 2]
                        e.wait_ge(olo, u + 1)
                        if u >= 2:
                            e.wait_ge(ores, u - 1)
                        for c in range(2):
                            for k in range(KT):
                                if u == 0 and c == 0:
                                    e.wait_ge(wol_ok, k + 1)
                                for x, w in ((sh, woh), (sh, wol), (sl, woh)):
                                    ins = e.matmul(bank[0:T, c, 0:HALF], x[:, u % 2, k], w[:, k, c * HALF:(c + 1) * HALF],
                                                   start=(k == 0 and x is sh and w is woh), stop=(k == KT - 1 and x is sl))
                        ins.then_inc(omm, 1)

            @block.scalar
            def _(e):
                def linear_out(m, which):
                    e.wait_ge((klin, qlin)[which], m + 1)
                    e.wait_ge(sp_ok, m * 8 + which * 4)
                    e.activation(sq[:], LQ[:, 0:N], ACT.Square, scale=NORM).then_inc(sq_ok, 1)
                    e.activation(lin[:], LQ[:, 0:N], ACT.Copy, scale=NORM).then_inc(lin_ok, 1)

                def pair(m, last):
                    for t in range(NT):
                        e.wait_ge(kdd, m * NT + t + 1)
                        e.activation(kf[:, t], DD[0:T, (t + 1) % 2, :], ACT.Copy).then_inc(kf_ok, 1)
                    e.wait_ge(kb_ok, m + 1)
                    for t in range(NT):
                        for h in range(2):
                            ins = e.activation(kf[:, t, h * M:(h + 1) * M], kf[:, t, h * M:(h + 1) * M], ACT.Exp,
                                               bias=kbias[:, t, h:h + 1])
                        if t % 5 == 4:
                            ins.then_inc(ke_ok, 1)
                    linear_out(m, 1)
                    for s in range(NT + 2):
                        if s < NT:
                            e.wait_ge(nb_ok, m * NT + s + 1)
                            e.wait_ge(qtr, m * NT + max(s - 2, 0))
                            for h in range(2):
                                ins = e.activation(qf[:, s % 3, h * M:(h + 1) * M], DD[0:T, s % 2, h * M:(h + 1) * M],
                                                   ACT.Exp, bias=nb[:, s % 2, h:h + 1])
                            ins.then_inc(qe_ok, 1)
                        t = s - 2
                        if t >= 0:
                            e.wait_ge(qtr, m * NT + t + 1)
                            e.wait_ge(out_ok, m * NT + max(t - 1, 0))
                            e.activation(qfT[:, t % 2].rearrange("p c t -> p (c t)"), TT[:, t % 2, 0:4 * T],
                                         ACT.Copy).then_inc(qfT_ok, 1)
                        if s == NT and not last:
                            linear_out(m + 1, 0)

                linear_out(0, 0)
                over_pairs(e, pair)
                e.wait_ge(wo_in, 16)
                e.wait_ge(cx_ok, 2 * MP)
                for k in range(KT):
                    e.activation(woh[:, k], wo[:, k], ACT.Copy).then_inc(woh_ok, 1)
                for t in range(NT):
                    e.wait_ge(otr, t + 1)
                    if t >= 2:
                        e.wait_ge(omm, t - 1)
                    e.activation(sh[:, t % 2].rearrange("p (c k) t -> p c (k t)", c=2),
                                 LQ[:, 0:1024].rearrange("p (c n) -> p c n", c=2)[:, :, 0:3 * T], ACT.Copy).then_inc(ost, 1)

            @block.vector
            def _(e):
                e.wait_ge(ptr, 1)
                e.wait_ge(pset, 4)
                e.tensor_copy(fraw[:], CO[:, 0:M]).then_inc(pdone, 1)
                e.wait_ge(pdone, 1)
                e.tensor_copy(fh[:], fraw[:]).then_inc(pdone, 1)
                e.wait_ge(pdone, 2)
                e.tensor_tensor(fl[:], fraw[:], fh[:].bitcast(F32), ALU.subtract).then_inc(pdone, 1)

                def rescale(m, c):
                    e.wait_ge(ke_ok, m * 2 + c + 1)
                    e.tensor_scalar(kf[:, 5 * c:5 * c + 5], kf[:, 5 * c:5 * c + 5], MIX_EPS, RATIO,
                                    ALU.add, ALU.mult).then_inc(kp_ok, 1)

                def split(dst, m, which):
                    e.wait_ge(lin_ok, m * 2 + which + 1)
                    for h in range(2):
                        e.tensor_copy(dst[head[h], h], lin[head[h]]).then_inc(sp_ok, 1)
                    e.wait_ge(sp_ok, m * 8 + which * 4 + 2)
                    for h in range(2):
                        e.tensor_tensor(dst[head[1 - h], h], lin[head[h]], dst[head[h], h].bitcast(F32), ALU.subtract).then_inc(sp_ok, 1)

                diag_of = lambda bank: DD[0:T, bank, 0:256].rearrange("p (t h r) -> p t h r", t=2, h=2)[:, :, :, 0]
                def pair(m, last):
                    for j in range(5):
                        e.wait_ge(kdg, m * 5 + j + 1)
                        e.tensor_copy(dk[:, 2 * j:2 * j + 2, :], diag_of(j % 2)).then_inc(d_out, 1)
                    for c in range(2):
                        e.wait_ge(kf_ok, m * NT + 5 * c + 5)
                        e.tensor_reduce(khalf[:, c], kf[:, 5 * c:5 * c + 5].rearrange("p t (h m) -> p h t m", h=2), AX.XY,
                                        ALU.max).then_inc(kh_ok, 1)
                    e.wait_ge(kh_ok, m * 2 + 2)
                    e.tensor_tensor(kmax[:], khalf[:, 0], khalf[:, 1], ALU.max).then_inc(kmax_ok, 1)
                    e.wait_ge(kmT, m + 1)
                    e.tensor_reduce(gmax[:], CO[0:2, 0:T], AX.X, ALU.max).then_inc(gmax_ok, 1)
                    e.wait_ge(gmax_ok, m + 1)
                    e.tensor_scalar(gdiag[:], g.ident[0:2, 0:2], gmax[:, 0:1], None, ALU.mult).then_inc(gd_ok, 1)
                    e.wait_ge(kmB, m + 1)
                    e.wait_ge(d_out, m * 10 + 5)
                    e.scalar_tensor_tensor(out=kbias[:], in0=dk[:], scalar=-1.0,
                                           in1=CO[0:T, 0:2].unsqueeze(1).to_broadcast([T, NT, 2]),
                                           op0=ALU.mult, op1=ALU.subtract).then_inc(kb_ok, 1)
                    rescale(m, 0)
                    rescale(m, 1)
                    split(qq, m, 1)
                    for j in range(5):
                        e.wait_ge(qdg, m * 5 + j + 1)
                        e.tensor_copy(dq[:, 2 * j:2 * j + 2, :], diag_of((j + 1) % 2)).then_inc(d_out, 1)
                    for h in range(2):
                        e.wait_ge(cx_ok, m * 2 + h + 1)
                        e.tensor_copy(cx[:, h], TT[:, h, 0:2 * W2]).then_inc(cx_out, 1)
                    e.wait_ge(d_out, m * 10 + 10)
                    for s in range(NT + 3):
                        if s < NT:
                            e.wait_ge(qdd, m * NT + s + 1)
                            e.tensor_reduce(qm[:, s % 2], DD[0:T, s % 2, :].rearrange("p (h m) -> p h m", h=2),
                                            AX.X, ALU.max).then_inc(qm_ok, 1)
                            e.wait_ge(qm_ok, m * NT + s + 1)
                            e.scalar_tensor_tensor(out=nb[:, s % 2], in0=qm[:, s % 2], scalar=-1.0, in1=dq[:, s],
                                                   op0=ALU.mult, op1=ALU.subtract).then_inc(nb_ok, 1)
                        t = s - 1
                        if 0 <= t < NT:
                            e.wait_ge(qe_ok, m * NT + t + 1)
                            e.tensor_scalar(qf[:, t % 3], qf[:, t % 3], MIX_EPS, RATIO, ALU.add, ALU.mult).then_inc(qp_ok, 1)
                        t = s - 3
                        if t >= 0:
                            e.wait_ge(out_ok, m * NT + t + 1)
                            heads = CO[0:T, 0:2 * 3 * (DH + 1)].rearrange("p (h c) -> p h c", h=2)
                            e.reciprocal(rc[:, t % 2], heads[:, :, DH]).then_inc(rc_ok, 1)
                            e.wait_ge(rc_ok, m * NT + t + 1)
                            e.tensor_tensor(mo[:, t, bass.ds(m * 128, 128)].rearrange("p (h c) -> p h c", h=2),
                                            heads[:, :, 0:DH], rc[:, t % 2].unsqueeze(2).to_broadcast([T, 2, DH]),
                                            ALU.mult).then_inc(mo_ok, 1)
                        if s == NT + 1 and not last:
                            split(kk, m + 1, 0)

                split(kk, 0, 0)
                over_pairs(e, pair)
                for k in range(KT):
                    e.wait_ge(woh_ok, k + 1)
                    e.tensor_tensor(wol[:, k], wo[:, k], woh[:, k].bitcast(F32), ALU.subtract).then_inc(wol_ok, 1)

                def low(t):
                    e.wait_ge(ost, t + 1)
                    e.tensor_tensor(sl[:, t % 2].rearrange("p (c k) t -> p c (k t)", c=2),
                                    LQ[:, 0:1024].rearrange("p (c n) -> p c n", c=2)[:, :, 0:3 * T],
                                    sh[:, t % 2].rearrange("p (c k) t -> p c (k t)", c=2).bitcast(F32), ALU.subtract).then_inc(olo, 1)

                low(0)
                for t in range(NT):
                    if t + 1 < NT:
                        low(t + 1)
                    e.wait_ge(omm, t + 1)
                    if t >= 2:
                        e.wait_ge(sent[t % 2], 16 * (t // 2))
                    e.tensor_copy(res[:, t % 2].rearrange("p (c n) -> p c n", c=2),
                                  (DD, TT)[t % 2][0:T, :, 0:HALF]).then_inc(ores, 1)


def lift(nc, g):
    with ExitStack() as ctx:
        sb = lambda n, s, d=F32: ctx.enter_context(nc.sbuf_tensor("li_" + n, s, d))
        ps = lambda n, s: ctx.enter_context(nc.psum_tensor("li_" + n, s, F32))
        sem = lambda n: g.sem("li_" + n)
        tile = lambda t: slice(t * T, (t + 1) * T)
        high_b = sb("high_b", [128, KT, D], F32R)
        xl = sb("xl", [128, 2, KT, T], F32R)
        sb("rest", [128, KT * N - KT * D - 2 * KT * T])
        wa = sb("wa", [128, 2, KT, 128])
        bah = sb("bah", [128, KT])
        x1T = sb("x1T", [128, KT, N])
        w, wlow = shared(nc, sb, ("li_w", [128, 2, KT, D], F32), ("wlow", [128, 2, KT, D], F32R))
        arow = sb("arow", [128, 2, D])
        prod = sb("prod", [128, KT // 2, D])
        watt = sb("watt", [128, KT, 2 * GI])
        rows = sb("rows", [2 * GI, N])
        cnt = sb("cnt", [T, 2, N])
        maskT = sb("maskT", [T, NT, N], BF16)
        srow = cnt
        high_a = sb("high_a", [128, KT, D], F32R)
        HIGH = (high_a, high_b, high_a)
        junk = sb("junk", [T, N])
        top, topd = sb("top", [T, 2, NT]), sb("topd", [T, NT, GI])
        m1, m2, uv = sb("m1", [T, NT, GI]), sb("m2", [T, NT, GI]), sb("uv", [T, NT, 2 * GI])
        xs = sb("xs", [128, 2, KT, T], F32R)
        ho = sb("ho", [T, 2, D])
        A, B, C = ps("A", [128, 3 * 512]), ps("B", [128, 3 * 512]), ps("C", [128, 2, 512])
        wa_in = [sem("wa_in0"), sem("wa_in1"), sem("wa_in2"), sem("wa_in3")]
        w_in = [sem("w_in0"), sem("w_in1")]
        ar_in = [sem("ar_in0"), sem("ar_in1")]
        cnt_in = [sem("cnt_in0"), sem("cnt_in1")]
        srow_in = [sem("srow_in0"), sem("srow_in1")]
        ho_sent = [sem("ho_sent0"), sem("ho_sent1")]
        b_in, rows_sent, uv_sent = sem("b_in"), sem("rows_sent"), sem("uv_sent")
        x1_mm, x1_ok, watt_ok, rows_mm, rows_ok = (sem(n) for n in ("x1_mm", "x1_ok", "watt_ok", "rows_mm", "rows_ok"))
        loop_ok, mt_mm, mt_ok, col_mm, col_ok = (sem(n) for n in ("loop_ok", "mt_mm", "mt_ok", "col_mm", "col_ok"))
        seg_ok, uv_ok, uvt_mm, uvt_ok = (sem(n) for n in ("seg_ok", "uv_ok", "uvt_mm", "uvt_ok"))
        xs_ok, h_mm, h_out, dve = (sem(n) for n in ("xs_ok", "h_mm", "h_out", "dve"))
        hi_ok, wl_ok, started = sem("hi_ok"), sem("wl_ok"), sem("started")
        ORDER = (2, 1, 0)
        W = (g.gnn_W0, g.gnn_W1, g.gnn_W2)
        AV = ((g.gnn_a_src0, g.gnn_a_src1, g.gnn_a_src2), (g.gnn_a_dst0, g.gnn_a_dst1, g.gnn_a_dst2))

        with nc.Block() as block:
            @block.sync
            def _(sp):
                sp.dma_start(bah[:], g.gnn_b_ah.rearrange("(k p) -> p k", p=128), allow_slow_non_contiguous=True).then_inc(b_in, 16)
                for p in range(2):
                    sp.dma_start(wa[:, p], weight_view(g.gnn_W_ah)[:, :, p * 128:(p + 1) * 128]).then_inc(wa_in[p], 16)
                for i in range(2):
                    sp.dma_start(w[:, i], weight_view(W[i])).then_inc(w_in[i], 16)
                for i in range(GL):
                    for c in range(2):
                        if i > 0:
                            sp.wait_ge(watt_ok, 4 * i + 2 * c - 2)
                        sp.dma_start(arow[:, c], AV[c][i].rearrange("h c -> (h c)").partition_broadcast(128)).then_inc(ar_in[c], 16)
                    if i == 1:
                        sp.wait_ge(watt_ok, 4)
                        sp.dma_start(w[:, 0], weight_view(W[2])).then_inc(w_in[0], 16)
                for s in range(NT):
                    if s >= 2:
                        sp.wait_ge(mt_mm, s - 1)
                    sp.dma_start(cnt[:, s % 2], g.table[s * T * N:(s + 1) * T * N].rearrange("(p n) o -> p (n o)", p=T)
                                 ).then_inc(cnt_in[s % 2], 16)
                sp.wait_ge(rows_ok, 1)
                sp.dma_start(g.rows, rows[:]).then_inc(rows_sent, 16)
                sp.wait_ge(rows_sent, 16)
                sp.wait_ge(mt_mm, NT)
                with sp.Fori(0, GI // 2) as i:
                    for p in range(2):
                        sp.wait_ge(seg_ok, i * 2 + p)
                        sp.dma_start(srow[:, p], g.rows[bass.ds(i * 2 + p, 1), :].rearrange("a n -> (a n)").partition_broadcast(T)
                                     ).then_inc(srow_in[p], 16)
                sp.wait_ge(uvt_ok, 1)
                sp.dma_start(g.uv, rows[:]).then_inc(uv_sent, 16)
                sp.wait_ge(uv_sent, 16)

            @block.gpsimd
            def _(e):
                for k in range(2, KT):
                    e.wait_ge(x1_mm, k - 1)
                    e.dma_start(wa[:, k % 2], weight_view(g.gnn_W_ah)[:, :, k * 128:(k + 1) * 128]).then_inc(wa_in[2 + k % 2], 16)
                e.wait_ge(x1_ok, KT)
                for l in range(GL):
                    with e.Fori(0, NT // 2) as i:
                        for p in range(2):
                            n = i * 2 + (p + l * NT)
                            cols = bass.ds((i * 2 + p) * T, T)
                            e.wait_ge(h_mm, n)
                            e.tensor_copy(xs[:, p], x1T[:, :, cols]).then_inc(xs_ok, 1)
                            e.wait_ge(xs_ok, 2 * n + 1)
                            e.sem_inc(started, 1)
                            e.tensor_tensor(xl[:, p], x1T[:, :, cols], xs[:, p].bitcast(F32), ALU.subtract).then_inc(xs_ok, 1)

            @block.tensor
            def _(e):
                for k in range(KT):
                    e.wait_ge(wa_in[k], 16) if k < 2 else e.wait_ge(wa_in[2 + k % 2], 16 * (k // 2))
                    if k >= 2:
                        e.wait_ge(x1_ok, k - 1)
                    bank = (A, B)[k % 2]
                    for a, n in CHUNKS:
                        for kk in range(KT):
                            ins = e.matmul(bank[:, a:a + n], wa[:, k % 2, kk], g.xnT[:, kk, a:a + n],
                                           start=(kk == 0), stop=(kk == KT - 1))
                    ins.then_inc(x1_mm, 1)
                e.wait_ge(watt_ok, 4 * GL)
                e.wait_ge(x1_ok, KT)
                for a, n in CHUNKS:
                    for k in range(KT):
                        ins = e.matmul(A[0:2 * GI, a:a + n], watt[:, k], x1T[:, k, a:a + n], start=(k == 0), stop=(k == KT - 1))
                ins.then_inc(rows_mm, 1)
                for s in range(NT):
                    bank = (B, A)[s % 2]
                    e.wait_ge(loop_ok, s + 1)
                    if s == 1:
                        e.wait_ge(rows_ok, 1)
                    if s >= 2:
                        e.wait_ge(mt_ok, s - 1)
                    for d in range(NT):
                        ins = e.transpose(bank[0:T, d // 4 * 512 + d % 4 * T:d // 4 * 512 + (d % 4 + 1) * T],
                                          cnt[:, s % 2, tile(d)], g.ident[0:T, 0:T])
                    ins.then_inc(mt_mm, 1)
                for t in range(NT):
                    ins = e.transpose(C[0:T, 0, t * 2 * GI:(t + 1) * 2 * GI], rows[:, tile(t)], g.ident[0:2 * GI, 0:2 * GI])
                ins.then_inc(col_mm, 1)
                e.wait_ge(mt_ok, NT)
                e.sem_inc(h_mm, 1)
                for l, layer in enumerate(ORDER):
                    e.wait_ge(wl_ok, l + 1)
                    low = wlow[:, l % 2]
                    with e.Fori(0, NT // 2) as i:
                        for p in range(2):
                            n = i * 2 + (p + l * NT)
                            bank = (A, B)[p]
                            e.wait_ge(xs_ok, 2 * n + 2)
                            e.wait_ge(h_out, n)
                            for c in range(2):
                                for k in range(KT):
                                    for x, y in ((xs, HIGH[l]), (xs, low), (xl, HIGH[l])):
                                        ins = e.matmul(bank[0:T, c * 512:c * 512 + HALF], x[:, p, k], y[:, k, c * HALF:(c + 1) * HALF],
                                                       start=(k == 0 and x is xs and y is HIGH[l]), stop=(k == KT - 1 and x is xl))
                            ins.then_inc(h_mm, 1)
                e.wait_ge(uv_ok, 1)
                e.wait_ge(h_out, GL * NT + 1)
                for t in range(NT):
                    ins = e.transpose(A[0:2 * GI, t // 4 * 512 + t % 4 * T:t // 4 * 512 + (t % 4 + 1) * T], uv[:, t],
                                      g.ident[0:T, 0:T])
                ins.then_inc(uvt_mm, 1)

            @block.scalar
            def _(e):
                e.wait_ge(b_in, 16)
                for k in range(KT):
                    e.wait_ge(x1_mm, k + 1)
                    e.activation(x1T[:, k], (A, B)[k % 2][:, 0:N], ACT.Relu, bias=bah[:, k:k + 1]).then_inc(x1_ok, 1)
                e.wait_ge(rows_mm, 1)
                e.activation(rows[:], A[0:2 * GI, 0:N], ACT.Copy).then_inc(rows_ok, 1)
                e.sem_inc(h_out, 1)

                def high(l):
                    e.wait_ge(w_in[l % 2], (32, 16, 48)[l])
                    e.activation(HIGH[l][:], w[:, l % 2], ACT.Copy).then_inc(hi_ok, 1)

                high(0)
                high(1)
                for l, layer, start, end in ((0, 2, 0, 5), (1, 1, 0, 3), (1, 1, 3, 5), (2, 0, 0, 5)):
                    if start > 0:
                        high(2)
                    with e.Fori(start, end) as i:
                        for p in range(2):
                            n = i * 2 + (p + l * NT)
                            e.wait_ge(h_mm, n + 2)
                            e.wait_ge(ho_sent[p], i * 16 + l * 16 * NT // 2)
                            e.activation(ho[:, p].rearrange("p (c n) -> p c n", c=2),
                                         (A, B)[p][0:T, 0:1024].rearrange("p (c n) -> p c n", c=2)[:, :, 0:HALF],
                                         ACT.Copy).then_inc(h_out, 1)
                            e.wait_ge(h_out, n + 2)
                            e.dma_start(g.h[layer * GH:(layer + 1) * GH, bass.ds((i * 2 + p) * T, T), :].rearrange("h p c -> p h c"),
                                        ho[:, p].rearrange("p (h c) -> p h c", h=GH)).then_inc(ho_sent[p], 16)
                    if l == 0:
                        e.wait_ge(h_mm, NT + 1)
                        e.dma_start(w[:, 0], weight_view(W[0])).then_inc(w_in[0], 16)
                for s in ho_sent:
                    e.wait_ge(s, 16 * GL * NT // 2)
                e.wait_ge(uvt_mm, 1)
                for b, (t0, t1) in enumerate(((0, 4), (4, 8), (8, 10))):
                    ins = e.activation(rows[:, t0 * T:t1 * T], A[0:2 * GI, b * 512:b * 512 + (t1 - t0) * T], ACT.Copy)
                ins.then_inc(uvt_ok, 1)

            @block.vector
            def _(e):
                seq = Tally(e, dve)

                def low(l):
                    e.wait_ge(hi_ok, l + 1)
                    e.tensor_tensor(wlow[:, l % 2], w[:, l % 2], HIGH[l][:].bitcast(F32), ALU.subtract).then_inc(wl_ok, 1)

                for i in range(GL):
                    e.wait_ge(w_in[i % 2], 32 if i == 2 else 16)
                    for c in range(2):
                        e.wait_ge(ar_in[c], 16 * (i + 1))
                        for hf in range(2):
                            ks = slice(hf * KT // 2, (hf + 1) * KT // 2)
                            seq.step(e.tensor_tensor(prod[:], w[:, i % 2, ks], arow[:, c].unsqueeze(1).to_broadcast([128, KT // 2, D]),
                                                     ALU.mult))
                            ins = e.tensor_reduce(watt[:, ks, c * GI + i * GH:c * GI + (i + 1) * GH],
                                                  prod[:].rearrange("p k (h c) -> p k h c", h=GH), AX.X, ALU.add)
                            ins.then_inc(watt_ok, 1)
                            e.wait_ge(watt_ok, 4 * i + 2 * c + hf + 1)
                for s in range(NT + 1):
                    if s < NT:
                        e.wait_ge(cnt_in[s % 2], 16 * (s // 2 + 1))
                        e.tensor_tensor(cnt[:, s % 2, tile(s)], cnt[:, s % 2, tile(s)], g.ident[0:T, 0:T], ALU.add).then_inc(loop_ok, 1)
                    if s > 0:
                        bank = (B, A)[(s - 1) % 2]
                        e.wait_ge(mt_mm, s)
                        for b, (d0, d1) in enumerate(((0, 4), (4, 8), (8, 10))):
                            ins = e.tensor_scalar(maskT[:, d0:d1, tile(s - 1)],
                                                  bank[0:T, b * 512:b * 512 + (d1 - d0) * T].rearrange("p (d s) -> p d s", s=T),
                                                  0.0, NEG, ALU.is_equal, ALU.mult)
                        ins.then_inc(mt_ok, 1)
                    if s in (5, 7):
                        low((s - 5) // 2)
                e.wait_ge(col_mm, 1)
                seq.step(e.tensor_copy(g.asad[:].rearrange("p t c -> p (t c)"), C[0:T, 0, 0:NT * 2 * GI]))
                e.wait_ge(mt_ok, NT)
                e.sem_inc(seg_ok, 1)
                for i in range(GI):
                    if i == 7:
                        low(2)
                    e.wait_ge(srow_in[i % 2], 16 * (i // 2 + 1))
                    for d in range(NT):
                        seq.step(e.tensor_tensor_reduce(junk[:], srow[:, i % 2], maskT[:, d], 1.0, NEG, ALU.add, ALU.max,
                                                        top[:, i % 2, d:d + 1]))
                    e.tensor_copy(topd[:, :, i:i + 1], top[:, i % 2].unsqueeze(2)).then_inc(seg_ok, 1)
                e.wait_ge(seg_ok, GI + 1)
                s_term, d_term = g.asad[:, :, 0:GI], g.asad[:, :, GI:2 * GI]
                seq.mark(e.tensor_scalar(g.as02[:], s_term, 0.2, None, ALU.mult))
                seq.step(e.tensor_tensor(m1[:], topd[:], d_term, ALU.add))
                seq.step(e.tensor_scalar(m2[:], m1[:], 0.2, None, ALU.mult))
                seq.step(e.tensor_tensor(m1[:], m1[:], m2[:], ALU.max))
                seq.mark(e.tensor_tensor(uv[:, :, 0:GI], d_term, m1[:], ALU.subtract))
                seq.settle()
                e.scalar_tensor_tensor(out=uv[:, :, GI:2 * GI], in0=d_term, scalar=0.2, in1=m1[:], op0=ALU.mult,
                                       op1=ALU.subtract).then_inc(uv_ok, 1)


def graph(nc, g):
    RING = 4
    HC = GC + 1
    STEPS = 2 * NT
    LAST = GI // 2 - 1

    def over_pairs(e, pair):
        pair(0)
        with e.Fori(1, LAST) as i:
            pair(i)
        pair(LAST)

    first = lambda i: isinstance(i, int) and i == 0
    last = lambda i: isinstance(i, int) and i == LAST
    with ExitStack() as ctx:
        sb = lambda n, s, d=F32: ctx.enter_context(nc.sbuf_tensor("gr_" + n, s, d))
        ps = lambda n, s: ctx.enter_context(nc.psum_tensor("gr_" + n, s, F32))
        sem = lambda n: g.sem("gr_" + n)
        tile = lambda t: slice(t * T, (t + 1) * T)
        cnt = sb("cnt", [T, NT, N])
        ub, vb = sb("ub", [T, 2, N]), sb("vb", [T, 2, N])
        h = sb("h", [T, 2, NT, HC])
        ring = sb("ring", [T, RING, N])
        bias = sb("bias", [T, GI * GC])
        node = sb("node", [T, 2, NT, GC])
        raw = sb("raw", [T, NT, HC])
        den, rec = sb("den", [T, NT]), sb("rec", [T, NT])
        wo_raw = g.raw_weights = first_weights(nc, sb)
        wo_in = sem("wo_in")
        acc = ps("acc", [128, 5, 512])
        cnt_in, b_in = [sem(f"cnt_in{q}") for q in range(NT // 2)], sem("b_in")
        started = sem("started")
        den_ok, rec_ok, sc_ok, bi_ok = sem("den_ok"), sem("rec_ok"), sem("sc_ok"), sem("bi_ok")
        uv_in = [sem("uv_in0"), sem("uv_in1")]
        h_in = [sem("h_in0"), sem("h_in1")]
        sent = [sem("sent0"), sem("sent1")]
        ones_ok, loop_ok = sem("ones_ok"), sem("loop_ok")
        a_ok, t_ok, e_ok, p_ok, mm, acc_out, node_ok, dve = (
            sem(n) for n in ("a_ok", "t_ok", "e_ok", "p_ok", "mm", "acc_out", "node_ok", "dve"))

        with nc.Block() as block:
            @block.sync
            def _(sp):
                def fetch(n, p):
                    sp.dma_start(ub[:, p], g.uv[bass.ds(n, 1), :].rearrange("a n -> (a n)").partition_broadcast(T)).then_inc(uv_in[p], 16)
                    sp.dma_start(vb[:, p], g.uv[bass.ds(n + GI, 1), :].rearrange("a n -> (a n)").partition_broadcast(T)).then_inc(uv_in[p], 16)
                    sp.dma_start(h[:, p, :, 0:GC], g.h[bass.ds(n, 1)].rearrange("a (t p) c -> p (a t) c", p=T)).then_inc(h_in[p], 16)

                fetch(0, 0)
                for q in range(NT // 2):
                    sp.dma_start(cnt[:, 2 * q:2 * q + 2], g.table[2 * q * T * N:2 * (q + 1) * T * N].rearrange(
                        "(t p n) o -> p t (n o)", p=T, n=N)).then_inc(cnt_in[q], 16)
                for i, b in enumerate((g.gnn_b0, g.gnn_b1, g.gnn_b2)):
                    sp.dma_start(bias[:, i * D:(i + 1) * D], b.partition_broadcast(T)).then_inc(b_in, 16)
                fetch(1, 1)
                with sp.Fori(0, GI // 2 - 1) as i:
                    for p in range(2):
                        sp.wait_ge(mm, (i * 2 + (p + 1)) * NT + RING)
                        fetch(i * 2 + p + 2, p)
                sp.dma_start(wo_raw[:].rearrange("p c k n -> p (c k) n"), weight_view(g.gnn_W_out)[:, 0:2 * KC]).then_inc(wo_in, 16)
                sp.wait_ge(wo_in, 16)

            @block.gpsimd
            def _(e):
                e.memset(h[:, :, :, GC:HC], 1.0).then_inc(ones_ok, 1)
                nodes = g.node.rearrange("(t p) (i c) -> p t i c", p=T, c=GC)
                e.wait_ge(b_in, 48)
                with e.Fori(0, GI // 2) as i:
                    for p in range(2):
                        n = i * 2 + p
                        e.wait_ge(sc_ok, n + 1)
                        e.tensor_tensor(node[:, p], node[:, p], bias[:, bass.ds(n * GC, GC)].unsqueeze(1).to_broadcast([T, NT, GC]),
                                        ALU.add).then_inc(bi_ok, 1)
                        e.wait_ge(bi_ok, n + 1)
                        e.sem_inc(started, 1)
                        e.tensor_scalar(node[:, p], node[:, p], 0.0, None, ALU.max).then_inc(node_ok, 1)
                        e.wait_ge(node_ok, n + 1)
                        e.sem_inc(started, 1)
                        e.dma_start(nodes[:, :, bass.ds(n, 1), :].rearrange("p t i c -> p t (i c)"), node[:, p]).then_inc(sent[p], 16)
                for s in sent:
                    e.wait_ge(s, 16 * GI // 2)

            @block.scalar
            def _(e):
                def sums(i, j):
                    p, s = j // NT, j % NT
                    if s == 0:
                        e.wait_ge(uv_in[p], i * 32 + 32)
                    e.wait_ge(mm, i * STEPS + j + 1)
                    e.activation(ring[:, j % RING], ub[:, p], ACT.Identity, bias=g.asad[:, s, bass.ds(i * 2 + p, 1)]).then_inc(a_ok, 1)

                def take(n):
                    e.wait_ge(mm, n * NT + NT + RING)
                    if not (isinstance(n, int) and n == 0):
                        e.wait_ge(sc_ok, n)
                    for b in range(5):
                        e.activation(raw[:, 2 * b:2 * b + 2], acc[0:T, b].rearrange("p (d c) -> p d c", d=2)[:, :, 0:HC],
                                     ACT.Copy).then_inc(acc_out, 1)

                def pair(i):
                    for j in range(STEPS):
                        if j + 1 < STEPS:
                            sums(i, j + 1)
                        elif not last(i):
                            sums(i + 1, 0)
                        e.wait_ge(t_ok, i * STEPS + j + 1)
                        e.activation(ring[:, j % RING], ring[:, j % RING], ACT.Exp).then_inc(e_ok, 1)
                        if j == 1 and not first(i):
                            take(i * 2 - 1)
                        if j == NT + 1:
                            take(i * 2)
                    if last(i):
                        take(2 * LAST + 1)

                sums(0, 0)
                over_pairs(e, pair)

            @block.vector
            def _(e):
                def bound(i, j):
                    e.wait_ge(a_ok, i * STEPS + j + 1)
                    e.scalar_tensor_tensor(out=ring[:, j % RING], in0=vb[:, j // NT], scalar=g.as02[:, j % NT, bass.ds(i * 2 + j // NT, 1)],
                                           in1=ring[:, j % RING], op0=ALU.add, op1=ALU.max).then_inc(t_ok, 1)

                def scale(n, p, turns):
                    e.wait_ge(acc_out, (n + 2) * 5)
                    e.tensor_scalar(den[:], raw[:, :, GC], 1e-16, None, ALU.add).then_inc(den_ok, 1)
                    e.wait_ge(den_ok, n + 1)
                    e.reciprocal(rec[:], den[:]).then_inc(rec_ok, 1)
                    e.wait_ge(rec_ok, n + 1)
                    if turns is not None:
                        e.wait_ge(sent[p], turns * 16)
                    for d in range(NT):
                        ins = e.tensor_scalar(node[:, p, d], raw[:, d, 0:GC], rec[:, d:d + 1], None, ALU.mult)
                    ins.then_inc(sc_ok, 1)

                def pair(i):
                    for j in range(STEPS):
                        if i_is(i, 0) and j % 2 == 1 and j < NT:
                            loops(j // 2 + 1)
                        if j + 1 < STEPS:
                            bound(i, j + 1)
                        elif not last(i):
                            bound(i + 1, 0)
                        e.wait_ge(e_ok, i * STEPS + j + 1)
                        if i_is(i, 0) and j < NT:
                            e.wait_ge(loop_ok, j // 2 * 2 + 2)
                        e.scalar_tensor_tensor(out=ring[:, j % RING], in0=ring[:, j % RING], scalar=1.0, in1=cnt[:, j % NT],
                                               op0=ALU.min, op1=ALU.mult).then_inc(p_ok, 1)
                        if j == 4 and not first(i):
                            scale(i * 2 - 1, 1, None if i_is(i, 1) else i - 1)
                        if j == NT + 4:
                            scale(i * 2, 0, None if first(i) else i)
                    if last(i):
                        scale(2 * LAST + 1, 1, LAST)

                def loops(q):
                    if q < NT // 2:
                        e.wait_ge(cnt_in[q], 16)
                        for s in (2 * q, 2 * q + 1):
                            e.tensor_tensor(cnt[:, s, tile(s)], cnt[:, s, tile(s)], g.ident[0:T, 0:T], ALU.add).then_inc(loop_ok, 1)

                i_is = lambda i, v: isinstance(i, int) and i == v
                loops(0)
                bound(0, 0)
                over_pairs(e, pair)

            @block.tensor
            def _(e):
                e.sem_inc(mm, RING)
                e.sem_inc(acc_out, 5)
                e.wait_ge(ones_ok, 1)
                with e.Fori(0, GI // 2) as i:
                    for j in range(STEPS):
                        p, s = j // NT, j % NT
                        e.wait_ge(p_ok, i * STEPS + j + 1)
                        if s == 0:
                            e.wait_ge(h_in[p], i * 16 + 16)
                        for d in range(NT):
                            if s == 0 and d % 2 == 0:
                                e.wait_ge(acc_out, (i * 2 + p) * 5 + d // 2 + 1)
                            ins = e.matmul(acc[0:T, d // 2, d % 2 * 256:d % 2 * 256 + HC], ring[:, j % RING, tile(d)],
                                           h[:, p, s], start=(s == 0 and d % 2 == 0), stop=(s == NT - 1 and d % 2 == 1),
                                           skip_group_check=True)
                        ins.then_inc(mm, 1)


KC = 3
RAW_AT = 194 * 1024


def first_weights(nc, sb):
    sb("gap", [128, (RAW_AT - nc.sbuf_base) // 4])
    return sb("first_weights", [128, 2, KC, D])


def join(nc, g):
    KO = GL * KT
    with ExitStack() as ctx:
        sb = lambda n, s, d=F32: ctx.enter_context(nc.sbuf_tensor("jo_" + n, s, d))
        ps = lambda n, s: ctx.enter_context(nc.psum_tensor("jo_" + n, s, F32))
        sem = lambda n: g.sem("jo_" + n)
        wh, wl = sb("wh", [128, KO, D], F32R), sb("wl", [128, KO, D], F32R)
        node = sb("node", [T, 2, D])
        xt, mt = sb("xt", [T, 2, D]), sb("mt", [T, 2, D])
        bias = sb("bias", [T, D])
        sh, sl = sb("sh", [128, 2, KT, T], F32R), sb("sl", [128, 2, KT, T], F32R)
        tmp = sb("tmp", [T, 2, D])
        first_weights(nc, sb)
        raw = g.raw_weights
        TR, O = ps("TR", [128, 2, 2, 512]), ps("O", [128, 2, 2, 512])
        raw_in, b_in = [sem("raw_in0"), sem("raw_in1")], sem("b_in")
        nd_in = [sem("nd_in0"), sem("nd_in1")]
        wh_ok, wl_ok, lo_ok = sem("wh_ok"), sem("wl_ok"), sem("lo_ok")
        stats_ok, started = sem("stats_ok"), sem("started")
        in_, sent = [sem("in0"), sem("in1")], [sem("sent0"), sem("sent1")]
        tr_mm, st_ok, mm, xm_ok, pre_ok, x_ok = (sem(n) for n in ("tr_mm", "st_ok", "mm", "xm_ok", "pre_ok", "x_ok"))

        with nc.Block() as block:
            @block.sync
            def _(sp):
                def third(n, c, p):
                    sp.dma_start(node[:, p], g.node[bass.ds(n * T, T), c * D:(c + 1) * D]).then_inc(nd_in[p], 16)

                third(0, 0, 0)
                third(0, 1, 1)
                for c in range(2, KO // KC):
                    sp.wait_ge(wl_ok, c - 1)
                    sp.dma_start(raw[:, c % 2], weight_view(g.gnn_W_out)[:, c * KC:(c + 1) * KC]).then_inc(raw_in[c % 2], 16)
                sp.dma_start(bias[:], g.gnn_b_out.partition_broadcast(T)).then_inc(b_in, 16)

                def pair(i, last):
                    for u in range(6):
                        n, c = i * 2 + (u + 2) // 3, (u + 2) % 3
                        if not last or u < 4:
                            sp.wait_ge(tr_mm, i * 6 + u + 1)
                            third(n, c, u % 2)

                with sp.Fori(0, NT // 2 - 1) as i:
                    pair(i, False)
                pair(NT // 2 - 1, True)

            @block.gpsimd
            def _(e):
                def fetch(n, p):
                    rows = bass.ds(n * T, T)
                    e.dma_start(xt[:, p], g.x[rows, :]).then_inc(in_[p], 16)
                    e.dma_start(mt[:, p], g.mix_out[rows, :]).then_inc(in_[p], 16)

                def pair(i, last):
                    for p in range(2):
                        n = i * 2 + p
                        e.wait_ge(x_ok, n + 1)
                        e.sem_inc(started, 1)
                        e.dma_start(g.xj[bass.ds(n * T, T), :], g.y[:, n, :]).then_inc(sent[p], 16)
                        if not last:
                            fetch(n + 2, p)

                fetch(0, 0)
                fetch(1, 1)
                with e.Fori(0, NT // 2 - 1) as i:
                    pair(i, False)
                pair(NT // 2 - 1, True)
                for s in sent:
                    e.wait_ge(s, 16 * NT // 2)

            @block.tensor
            def _(e):
                def turn(i, u):
                    e.wait_ge(nd_in[u % 2], (i * 3 + u // 2 + 1) * 16)
                    e.wait_ge(lo_ok, i * 6 + max(u - 1, 0))
                    for k in range(KT):
                        ins = e.transpose(TR[:, u % 2, k // 3, k % 3 * T:(k % 3 + 1) * T],
                                          node[:, u % 2, k * 128:(k + 1) * 128], g.ident[0:T, 0:T])
                    ins.then_inc(tr_mm, 1)

                def pair(i, last):
                    for u in range(6):
                        p, c = u // 3, u % 3
                        if not last or u < 5:
                            turn(i, u + 1)
                        e.wait_ge(lo_ok, i * 6 + u + 1)
                        if c == 0:
                            e.wait_ge(pre_ok, i * 2 + p)
                        for k in range(KT):
                            if k % KC == 0:
                                e.wait_ge(wl_ok, (c * KT + k) // KC + 1)
                            for hf in range(2):
                                for x, w in ((sh, wh), (sh, wl), (sl, wh)):
                                    ins = e.matmul(O[0:T, p, hf, 0:HALF], x[:, u % 2, k], w[:, c * KT + k, hf * HALF:(hf + 1) * HALF],
                                                   start=(c == 0 and k == 0 and x is sh and w is wh),
                                                   stop=(c == 2 and k == KT - 1 and x is sl))
                        ins.then_inc(mm, 1)

                e.sem_inc(pre_ok, 1)
                turn(0, 0)
                with e.Fori(0, NT // 2 - 1) as i:
                    pair(i, False)
                pair(NT // 2 - 1, True)

            @block.scalar
            def _(e):
                def high(i, u):
                    e.wait_ge(tr_mm, i * 6 + u + 1)
                    e.wait_ge(mm, i * 6 + max(u - 1, 0))
                    e.activation(sh[:, u % 2].rearrange("p (b k) t -> p b (k t)", b=2), TR[:, u % 2, :, 0:3 * T], ACT.Copy).then_inc(st_ok, 1)

                high(0, 0)
                for c in range(KO // KC):
                    if c >= 2:
                        e.wait_ge(raw_in[c % 2], 16 * (c // 2))
                    e.activation(wh[:, c * KC:(c + 1) * KC], raw[:, c % 2], ACT.Copy).then_inc(wh_ok, 1)
                    if c in (1, 3):
                        high(0, c // 2 + 1)
                for u in range(3, 6):
                    high(0, u)
                with e.Fori(1, NT // 2) as i:
                    for u in range(6):
                        high(i, u)

            @block.vector
            def _(e):
                def low(i, u):
                    e.wait_ge(st_ok, i * 6 + u + 1)
                    e.tensor_tensor(sl[:, u % 2].rearrange("p (b k) t -> p b (k t)", b=2), TR[:, u % 2, :, 0:3 * T],
                                    sh[:, u % 2].rearrange("p (b k) t -> p b (k t)", b=2).bitcast(F32), ALU.subtract).then_inc(lo_ok, 1)

                low(0, 0)
                for c in range(KO // KC):
                    e.wait_ge(wh_ok, c + 1)
                    e.tensor_tensor(wl[:, c * KC:(c + 1) * KC], raw[:, c % 2], wh[:, c * KC:(c + 1) * KC].bitcast(F32),
                                    ALU.subtract).then_inc(wl_ok, 1)
                    if c in (1, 3):
                        low(0, c // 2 + 1)
                e.wait_ge(b_in, 16)

                def finish(n, p, i):
                    e.wait_ge(in_[p], i * 32 + 32)
                    e.tensor_tensor(xt[:, p], xt[:, p], mt[:, p], ALU.add).then_inc(xm_ok, 1)
                    e.wait_ge(mm, 3 * n + 3)
                    e.tensor_tensor(tmp[:, p].rearrange("p (c n) -> p c n", c=2), O[0:T, p, :, 0:HALF],
                                    bias[:].rearrange("p (c n) -> p c n", c=2), ALU.add).then_inc(pre_ok, 1)
                    e.wait_ge(pre_ok, n + 2)
                    e.wait_ge(xm_ok, n + 1)
                    e.scalar_tensor_tensor(out=g.y[:, n, :], in0=tmp[:, p], scalar=0.0, in1=xt[:, p],
                                           op0=ALU.max, op1=ALU.add).then_inc(x_ok, 1)
                    e.wait_ge(x_ok, n + 1)
                    for c in range(2):
                        e.bn_stats(g.stats[:, bass.ds(n, 1), 6 * c:6 * c + 6].rearrange("p a s -> p (a s)"),
                                   g.y[:, n, c * HALF:(c + 1) * HALF]).then_inc(stats_ok, 1)

                def pair(i, last):
                    for u in range(6):
                        if (not last or u < 4) and not (isinstance(i, int) and i == 0 and u == 0):
                            low(i, u + 2)
                        if u % 3 == 2:
                            finish(i * 2 + u // 3, u // 3, i)

                pair(0, False)
                with e.Fori(1, NT // 2 - 1) as i:
                    pair(i, False)
                pair(NT // 2 - 1, True)
                e.wait_ge(stats_ok, 2 * NT)


def route(nc, g):
    NG = 4
    NPB = NB // NG

    def over_tiles(e, pair):
        pair(0)
        with e.Fori(1, NT // 2 - 1) as i:
            pair(i)
        pair(NT // 2 - 1)
    with ExitStack() as ctx:
        sb = lambda n, s, d=F32: ctx.enter_context(nc.sbuf_tensor("ro_" + n, s, d))
        ps = lambda n, s: ctx.enter_context(nc.psum_tensor("ro_" + n, s, F32))
        sem = lambda n: g.sem("ro_" + n)
        stats, mv, mv2 = sb("stats", [T, NT, 12]), sb("mv", [T, NT, 2]), sb("mv2", [T, NT, 2])
        veps, std, rstd, tmp = (sb(n, [T, NT]) for n in ("veps", "std", "rstd", "tmp"))
        gain, shift = sb("gain", [128, KT]), sb("shift", [128, KT])
        recipe, rmax, rsum, rrec = sb("recipe", [NN, NB]), sb("rmax", [NN, 1]), sb("rsum", [NN, 1]), sb("rrec", [NN, 1])
        pat, gate, gated = sb("pat", [NN, MH]), sb("gate", [NN, 1]), sb("gated", [NN, NN])
        ones = sb("ones", [NN, T])
        gateB = sb("gateB", [T, NN])
        bemb = sb("bemb", [NB, D])
        recT = sb("recT", [NB, NN])
        nemb = sb("nemb", [128, KT, NN])
        basis = sb("basis", [128, NB, KT * RANK])
        vw, vb = sb("vw", [RANK, D]), sb("vb", [T, D])
        z = sb("z", [T, 2, D])
        stage = sb("stage", [128, 2, KT, T])
        fin, rep, ex, sel = (sb(n, [T, NN]) for n in ("fin", "rep", "ex", "sel"))
        top, ntop, ssum, srec = sb("top", [T, 8]), sb("ntop", [T, 1]), sb("ssum", [T, 1]), sb("srec", [T, 1])
        selT = sb("selT", [NN, T])
        mixw = sb("mixw", [T, NB])
        pw = sb("pw", [T, NB, RANK])
        vs = sb("vs", [T, 128])
        vsT = sb("vsT", [RANK, T])
        TR, PR, S1, S2 = ps("TR", [128, 2, 512]), ps("PR", [128, NG, 512]), ps("S1", [128, 512]), ps("S2", [128, 512])
        vt = sb("vt", [T, 2, D])
        v_sent = [sem("v_sent0"), sem("v_sent1")]
        gs_in, small_in, vw_in = sem("gs_in"), sem("small_in"), sem("vw_in")
        bas_in = [sem(f"bas_in{c}") for c in range(NG)]
        var_ok, std_ok, ones_ok, dve, act = sem("var_ok"), sem("std_ok"), sem("ones_ok"), sem("dve"), sem("act")
        rmax_ok, rexp_ok, rec_ok, pat_ok, pexp_ok, gd_ok = (sem(n) for n in ("rmax_ok", "rexp_ok", "rec_ok", "pat_ok", "pexp_ok", "gd_ok"))
        recT_mm, recT_ok, nemb_mm, gateB_mm, setup = (sem(n) for n in ("recT_mm", "recT_ok", "nemb_mm", "gateB_mm", "setup"))
        z_ok, tr_mm, st_ok, nT_ok, sem_mm, pr_mm = (sem(n) for n in ("z_ok", "tr_mm", "st_ok", "nT_ok", "sem_mm", "pr_mm"))
        top8_ok, rep_ok, sum_ok = sem("top8_ok"), sem("rep_ok"), sem("sum_ok")
        fin_ok, y_ok, y_sent = sem("fin_ok"), sem("y_ok"), sem("y_sent")
        top_ok, ex_ok, sel_ok, selT_mm, selT_ok, mixw_mm, mixw_ok, pw_ok, vs_ok, vsT_mm, vsT_ok, v_mm, v_ok = (
            sem(n) for n in ("top_ok", "ex_ok", "sel_ok", "selT_mm", "selT_ok", "mixw_mm", "mixw_ok", "pw_ok", "vs_ok", "vsT_mm",
                             "vsT_ok", "v_mm", "v_ok"))

        with nc.Block() as block:
            @block.sync
            def _(sp):
                sp.dma_start(recipe[:], g.ffn_recipe).then_inc(small_in, 16)
                sp.dma_start(pat[:], g.ffn_ctx_pat).then_inc(small_in, 16)
                sp.dma_start(bemb[:], g.ffn_basis_emb).then_inc(small_in, 16)
                for dst, v in ((gain, g.ffn_n1_g), (shift, g.ffn_n1_b)):
                    sp.dma_start(dst[:], v.rearrange("(p k) -> p k", p=128)).then_inc(gs_in, 16)
                for c in range(NG):
                    ns = slice(c * NPB, (c + 1) * NPB)
                    sp.dma_start(basis[:, ns], g.ffn_basis_A[ns].rearrange("n (p k) r -> p n (k r)", p=128)).then_inc(bas_in[c], 16)
                sp.dma_start(vw[:], g.ffn_vout_w).then_inc(vw_in, 16)
                sp.dma_start(vb[:], g.ffn_vout_b.partition_broadcast(T)).then_inc(vw_in, 16)
                sp.wait_ge(y_ok, NT)
                sp.dma_start(node_view(g.y_dram), g.y[:]).then_inc(y_sent, 16)
                with sp.Fori(0, NT // 2) as i:
                    for p in range(2):
                        n = i * 2 + p
                        sp.wait_ge(v_ok, n + 1)
                        sp.dma_start(g.v_dram[bass.ds(n * T, T), :], vt[:, p]).then_inc(v_sent[p], 16)
                for s in v_sent:
                    sp.wait_ge(s, 16 * NT // 2)
                sp.wait_ge(y_sent, 16)

            @block.gpsimd
            def _(e):
                e.memset(ones[:], 1.0).then_inc(ones_ok, 1)
                e.memset(vs[:], 0.0).then_inc(ones_ok, 1)
                with e.Fori(0, NT // 2) as i:
                    for p in range(2):
                        n = i * 2 + p
                        cols = bass.ds(n * T, T)
                        e.wait_ge(st_ok, (n + 1) * KT)
                        e.tensor_copy(g.nTh[:, :, cols], stage[:, p]).then_inc(nT_ok, 1)
                        e.wait_ge(nT_ok, 2 * n + 1)
                        e.tensor_tensor(g.nTl[:, :, cols], stage[:, p], g.nTh[:, :, cols].bitcast(F32), ALU.subtract).then_inc(nT_ok, 1)

            @block.vector
            def _(e):
                seq = Tally(e, dve)
                def statistics(tiles):
                    for t in tiles:
                        for c in range(2):
                            seq.mark(e.bn_stats(stats[:, t, 6 * c:6 * c + 6], g.y[:, t, c * HALF:(c + 1) * HALF]))

                for t in range(NT):
                    seq.mark(e.bn_aggr(mv[:, t, :], g.stats[:, t, :]))
                seq.settle()
                e.tensor_scalar(veps[:], mv[:, :, 1], LN_EPS, None, ALU.add).then_inc(var_ok, 1)
                e.wait_ge(std_ok, 1)
                newton_rstd(e, seq, rstd[:], std[:], veps[:], tmp[:])
                for t in range(NT):
                    e.tensor_scalar(g.y[:, t], g.y[:, t], mv[:, t, 0:1], rstd[:, t:t + 1], ALU.subtract, ALU.mult).then_inc(y_ok, 1)
                e.wait_ge(small_in, 48)
                e.tensor_reduce(rmax[:], recipe[:], AX.X, ALU.max, negate=True).then_inc(rmax_ok, 1)
                seq.step(e.tensor_reduce(gate[:], pat[:], AX.X, ALU.add))
                e.tensor_scalar(gate[:], gate[:], -1.0 / N, None, ALU.mult).then_inc(pat_ok, 1)
                e.wait_ge(y_ok, NT)
                statistics(range(0, 4))
                e.wait_ge(pexp_ok, 1)
                seq.step(e.tensor_scalar(gate[:], gate[:], 1.0, None, ALU.add))
                seq.step(e.reciprocal(gate[:], gate[:]))
                e.tensor_scalar(gated[:], g.ident[0:NN, 0:NN], gate[:], None, ALU.mult).then_inc(gd_ok, 1)
                e.wait_ge(rexp_ok, 1)
                seq.step(e.reciprocal(rrec[:], rsum[:]))
                e.tensor_scalar(recipe[:], recipe[:], rrec[:], None, ALU.mult).then_inc(rec_ok, 1)
                statistics(range(4, 7))
                e.wait_ge(recT_mm, 1)
                e.tensor_copy(recT[:], S1[0:NB, 0:NN]).then_inc(recT_ok, 1)
                statistics(range(7, NT))
                seq.settle()
                for t in range(NT):
                    seq.mark(e.bn_aggr(mv2[:, t, :], stats[:, t, :]))
                seq.settle()
                e.tensor_scalar(veps[:], mv2[:, :, 1], LN_EPS, None, ALU.add).then_inc(var_ok, 1)
                e.wait_ge(nemb_mm, 1)
                e.tensor_copy(nemb[:, 0:3], TR[:, 0, 0:3 * NN].rearrange("p (k n) -> p k n", k=3)).then_inc(setup, 1)
                e.tensor_copy(nemb[:, 3:6], TR[:, 1, 0:3 * NN].rearrange("p (k n) -> p k n", k=3)).then_inc(setup, 1)
                e.wait_ge(gateB_mm, 1)
                e.tensor_copy(gateB[:], S2[0:T, 0:NN]).then_inc(setup, 1)
                e.wait_ge(std_ok, 2)
                newton_rstd(e, seq, rstd[:], std[:], veps[:], tmp[:])

                def centre(n, p):
                    e.tensor_scalar(z[:, p], g.y[:, n, :], mv2[:, n, 0:1], rstd[:, bass.ds(n, 1)],
                                    ALU.subtract, ALU.mult).then_inc(z_ok, 1)

                def add_bias(n, p, turns):
                    e.wait_ge(v_mm, n + 1)
                    if turns is not None:
                        e.wait_ge(v_sent[p], turns * 16)
                    e.tensor_tensor(vt[:, p].rearrange("p (c n) -> p c n", c=2), TR[0:T, :, 0:HALF],
                                    vb[:].rearrange("p (c n) -> p c n", c=2), ALU.add).then_inc(v_ok, 1)

                centre(0, 0)
                e.wait_ge(setup, 3)
                e.wait_ge(vw_in, 32)
                e.wait_ge(ones_ok, 2)

                def pair(i):
                    for p in range(2):
                        n = i * 2 + p
                        if not isinstance(n, int) or n + 1 < NT:
                            if not isinstance(n, int) or n > 0:
                                e.wait_ge(tr_mm, n)
                            centre(n + 1, 1 - p)
                        e.wait_ge(sem_mm, n + 1)
                        e.tensor_tensor(fin[:], S1[0:T, 0:NN], gateB[:], ALU.mult).then_inc(fin_ok, 1)
                        e.wait_ge(fin_ok, 2 * n + 1)
                        e.sem_inc(fin_ok, 1)
                        e.max(top[:], fin[:]).then_inc(top8_ok, 1)
                        e.wait_ge(top8_ok, n + 1)
                        e.tensor_scalar(ntop[:], top[:, 0:1], -1.0, None, ALU.mult).then_inc(top_ok, 1)
                        e.match_replace(rep[:], top[:], fin[:], NEG).then_inc(rep_ok, 1)
                        e.wait_ge(ex_ok, n + 1)
                        e.wait_ge(rep_ok, n + 1)
                        e.scalar_tensor_tensor(out=sel[:], in0=rep[:], scalar=NEG, in1=ex[:], op0=ALU.is_equal,
                                               op1=ALU.mult, accum_out=ssum[:]).then_inc(sum_ok, 1)
                        e.wait_ge(sum_ok, 2 * n + 1)
                        e.reciprocal(srec[:], ssum[:]).then_inc(sum_ok, 1)
                        e.wait_ge(sum_ok, 2 * n + 2)
                        e.tensor_scalar(sel[:], sel[:], srec[:], None, ALU.mult).then_inc(sel_ok, 1)
                        if not isinstance(n, int) or n > 0:
                            add_bias(n - 1, 1 - p, (None if isinstance(i, int) and i == 0 else i) if p else (None if isinstance(i, int) and i < 2 else i - 1))
                        e.wait_ge(mixw_mm, n + 1)
                        e.tensor_copy(mixw[:], S1[0:T, 128:128 + NB]).then_inc(mixw_ok, 1)
                        e.wait_ge(mixw_ok, n + 1)
                        for c in range(NG):
                            e.wait_ge(pr_mm, n * NG + c + 1)
                            e.tensor_tensor(pw[:, c * NPB:(c + 1) * NPB], PR[0:T, c].rearrange("p (n r) -> p n r", r=RANK),
                                            mixw[:, c * NPB:(c + 1) * NPB].unsqueeze(2).to_broadcast([T, NPB, RANK]),
                                            ALU.mult).then_inc(pw_ok, 1)
                        e.wait_ge(pw_ok, (n + 1) * NG)
                        e.tensor_reduce(vs[:, 0:RANK], pw[:].rearrange("p n r -> p r n"), AX.X, ALU.add).then_inc(vs_ok, 1)

                over_tiles(e, pair)
                add_bias(NT - 1, 1, NT // 2 - 1)

            @block.scalar
            def _(e):
                e.wait_ge(var_ok, 1)
                e.activation(std[:], veps[:], ACT.Sqrt).then_inc(std_ok, 1)
                e.wait_ge(rmax_ok, 1)
                e.activation(recipe[:], recipe[:], ACT.Exp, bias=rmax[:], accum_out=rsum[:]).then_inc(rexp_ok, 1)
                e.wait_ge(pat_ok, 1)
                e.activation(gate[:], gate[:], ACT.Exp).then_inc(pexp_ok, 1)
                e.wait_ge(var_ok, 2)
                e.activation(std[:], veps[:], ACT.Sqrt).then_inc(std_ok, 1)
                e.wait_ge(gs_in, 32)

                def pair(i):
                    for p in range(2):
                        n = i * 2 + p
                        if isinstance(n, int) and n == 0:
                            affine(0, 0)
                        e.wait_ge(top_ok, n + 1)
                        e.activation(ex[:], fin[:], ACT.Exp, bias=ntop[:]).then_inc(ex_ok, 1)
                        if not isinstance(n, int) or n > 0:
                            turn_values(n - 1)
                        e.wait_ge(selT_mm, n + 1)
                        e.activation(selT[:], S2[0:NN, 0:T], ACT.Copy).then_inc(selT_ok, 1)
                        if not isinstance(n, int) or n + 1 < NT:
                            affine(n + 1, 1 - p)

                def affine(n, p):
                    e.wait_ge(tr_mm, n + 1)
                    if not isinstance(n, int) or n > 1:
                        e.wait_ge(nT_ok, 2 * (n - 1))
                        e.wait_ge(pr_mm, (n - 1) * NG)
                    for k in range(KT):
                        e.activation(stage[:, p, k], TR[:, k // 3, k % 3 * T:(k % 3 + 1) * T], ACT.Identity,
                                     bias=shift[:, k:k + 1], scale=gain[:, k:k + 1]).then_inc(st_ok, 1)

                def turn_values(n):
                    e.wait_ge(vsT_mm, n + 1)
                    e.activation(vsT[:], S2[0:RANK, 128:128 + T], ACT.Copy).then_inc(vsT_ok, 1)

                over_tiles(e, pair)
                turn_values(NT - 1)

            @block.tensor
            def _(e):
                e.wait_ge(rec_ok, 1)
                e.transpose(S1[0:NB, 0:NN], recipe[:], g.ident[0:NN, 0:NN]).then_inc(recT_mm, 1)
                e.wait_ge(recT_ok, 1)
                for k in range(KT):
                    ins = e.matmul(TR[:, k // 3, k % 3 * NN:(k % 3 + 1) * NN], bemb[:].rearrange("b (q k) -> b k q", k=KT)[:, k], recT[:],
                                   start=True, stop=True)
                ins.then_inc(nemb_mm, 1)
                e.wait_ge(gd_ok, 1)
                e.wait_ge(ones_ok, 2)
                e.matmul(S2[0:T, 0:NN], ones[:], gated[:], start=True, stop=True).then_inc(gateB_mm, 1)
                e.wait_ge(setup, 3)

                def turn(n, p):
                    e.wait_ge(z_ok, n + 1)
                    if not isinstance(n, int) or n > 1:
                        e.wait_ge(v_ok, n - 1)
                    for k in range(KT):
                        ins = e.transpose(TR[:, k // 3, k % 3 * T:(k % 3 + 1) * T], z[:, p].rearrange("t (q k) -> t k q", k=KT)[:, k],
                                          g.ident[0:T, 0:T])
                    ins.then_inc(tr_mm, 1)

                def semantic(n, p):
                    e.wait_ge(st_ok, (n + 1) * KT)
                    if not isinstance(n, int) or n > 0:
                        e.wait_ge(mixw_ok, n)
                    for k in range(KT):
                        ins = e.matmul(S1[0:T, 0:NN], stage[:, p, k], nemb[:, k], start=(k == 0), stop=(k == KT - 1))
                    ins.then_inc(sem_mm, 1)

                def turn_vs(n):
                    e.wait_ge(vs_ok, n + 1)
                    e.transpose(S2[:, 128:128 + T], vs[:], g.ident[0:T, 0:T]).then_inc(vsT_mm, 1)

                def values(n):
                    e.wait_ge(vsT_ok, n + 1)
                    for c in range(2):
                        ins = e.matmul(TR[0:T, c, 0:HALF], vsT[:], vw[:, c * HALF:(c + 1) * HALF], start=True, stop=True)
                    ins.then_inc(v_mm, 1)

                turn(0, 0)
                semantic(0, 0)
                e.wait_ge(vw_in, 32)

                def pair(i):
                    for p in range(2):
                        n = i * 2 + p
                        for c in range(NG):
                            if isinstance(n, int) and n == 0:
                                e.wait_ge(bas_in[c], 16)
                            else:
                                e.wait_ge(pw_ok, (n - 1) * NG + c + 1)
                            for k in range(KT):
                                ins = e.matmul(PR[0:T, c].rearrange("p (n r) -> p n r", r=RANK), stage[:, p, k],
                                               basis[:, c * NPB:(c + 1) * NPB, k * RANK:(k + 1) * RANK],
                                               start=(k == 0), stop=(k == KT - 1))
                            ins.then_inc(pr_mm, 1)
                            before = not isinstance(n, int) or n > 0
                            after = not isinstance(n, int) or n + 1 < NT
                            if c == 0 and before:
                                turn_vs(n - 1)
                            if c == 1:
                                if before:
                                    values(n - 1)
                                e.wait_ge(sel_ok, n + 1)
                                e.transpose(S2[0:NN, 0:T], sel[:], g.ident[0:T, 0:T]).then_inc(selT_mm, 1)
                            if c == 2:
                                e.wait_ge(selT_ok, n + 1)
                                e.matmul(S1[0:T, 128:128 + NB], selT[:], recipe[:], start=True, stop=True).then_inc(mixw_mm, 1)
                                if after:
                                    turn(n + 1, 1 - p)
                            if c == 3 and after:
                                semantic(n + 1, 1 - p)

                over_tiles(e, pair)
                turn_vs(NT - 1)
                values(NT - 1)


def attend(nc, g):
    STEPS = 2 * NT
    SLOTS = 8
    BANK = ((0, 3), (3, 6), (6, 10))
    CW, CS = 418, 416
    PW = 256
    with ExitStack() as ctx:
        sb = lambda n, s, d=F32: ctx.enter_context(nc.sbuf_tensor("at_" + n, s, d))
        ps = lambda n, s: ctx.enter_context(nc.psum_tensor("at_" + n, s, F32))
        sem = lambda n: g.sem("at_" + n)
        qw, wql = shared(nc, sb, ("at_qw", [128, KT, 128], F32), ("wql", [128, KT, 128], F32R))
        kw, wkl = shared(nc, sb, ("at_kw", [128, KT, 128], F32), ("wkl", [128, KT, 128], F32R))
        qb, kb = sb("qb", [128, KT]), sb("kb", [128, KT])
        wqh, wkh = sb("wqh", [128, KT, 128], F32R), sb("wkh", [128, KT, 128], F32R)
        qf = kf = sb("qkf", [128, N])
        qq, kh, kl = sb("qq", [128, 2, N], F32R), sb("kh", [128, 2, N], F32R), sb("kl", [128, 2, N], F32R)
        nmax, part, sums, rc = sb("nmax", [T, 2]), sb("part", [T, SLOTS, 3]), sb("sums", [T, SLOTS]), sb("rc", [T, SLOTS])
        A = sb("A", [T, 2, N])
        ph, pl = sb("ph", [T, 2, NT, PW], F32R), sb("pl", [T, 2, NT, PW], F32R)
        zeros = sb("zeros", [T, PW - 2 * T])
        vraw = sb("vraw", [T, NT, 128])
        vp = sb("vp", [T, NT, 2, 128], F32R)
        twice = sb("twice", [128, DH])
        ot = sb("ot", [128, 2, PW])
        S, O = ps("S", [128, 2, 3, 512]), ps("O", [128, 2, 512])
        b_in, qw_in, kw_in, ws_ok = sem("b_in"), sem("qw_in"), sem("kw_in"), sem("ws_ok")
        q_mm, k_mm, qf_ok, kf_ok, qb_ok = sem("q_mm"), sem("k_mm"), sem("qf_ok"), sem("kf_ok"), sem("qb_ok")
        qs_ok, k0v_ok, k0a_ok, k1_ok = sem("qs_ok"), sem("k0v_ok"), sem("k0a_ok"), sem("k1_ok")
        started = sem("started")
        w0_ok = sem("w0_ok")
        z_ok, pad_ok, tw_ok, v_in, vp_ok, ot_ok, f_mm, sums_ok = (
            sem(n) for n in ("z_ok", "pad_ok", "tw_ok", "v_in", "vp_ok", "ot_ok", "f_mm", "sums_ok"))
        halves = [slice(0, DH), slice(DH, 128)]
        s_mm, max_ok, exp_ok, tt_mm, at_v, at_a, av_mm, rc_ok, ao_ok = (
            sem(n) for n in ("s_mm", "max_ok", "exp_ok", "tt_mm", "at_v", "at_a", "av_mm", "rc_ok", "ao_ok"))

        def over_pairs(e, pair):
            with e.Fori(0, MP - 1) as m:
                pair(m, False)
            pair(MP - 1, True)

        def turned(dst, u, b):
            t0, t1 = BANK[b]
            return (dst[:, u // 2 % 2, t0:t1, u % 2 * T:(u % 2 + 1) * T],
                    S[0:T, u % 2, b, 0:(t1 - t0) * T].rearrange("p (t s) -> p t s", s=T))

        with nc.Block() as block:
            @block.sync
            def _(sp):
                sp.dma_start(qw[:], strided_view(g.ffn_q_w)[:, :, 0:128]).then_inc(qw_in, 16)
                sp.dma_start(kw[:], strided_view(g.ffn_k_w)[:, :, 0:128]).then_inc(kw_in, 16)
                for dst, v in ((qb, g.ffn_q_b), (kb, g.ffn_k_b)):
                    sp.dma_start(dst[:], v.rearrange("(k p) -> p k", p=128), allow_slow_non_contiguous=True).then_inc(b_in, 16)
                sp.dma_start(vraw[:], node_view(g.v_dram)[:, :, 0:128]).then_inc(v_in, 16)
                with sp.Fori(1, MP) as m:
                    sp.wait_ge(vp_ok, m * 4)
                    sp.dma_start(vraw[:], node_view(g.v_dram)[:, :, bass.ds(m * 128, 128)]).then_inc(v_in, 16)
                    sp.wait_ge(q_mm, m)
                    sp.wait_ge(k_mm, m)
                    sp.dma_start(qw[:], strided_view(g.ffn_q_w)[:, :, bass.ds(m * 128, 128)]).then_inc(qw_in, 16)
                    sp.dma_start(kw[:], strided_view(g.ffn_k_w)[:, :, bass.ds(m * 128, 128)]).then_inc(kw_in, 16)

            @block.gpsimd
            def _(e):
                def weights(m):
                    for w, into, high, low, used in ((qw, qw_in, wqh, wql, q_mm), (kw, kw_in, wkh, wkl, k_mm)):
                        e.wait_ge(into, m * 16 + 16)
                        e.wait_ge(used, m)
                        e.sem_inc(started, 1)
                        e.tensor_copy(high[:], w[:]).then_inc(ws_ok, 1)
                        e.wait_ge(ws_ok, m * 4 + (1 if w is qw else 3))
                        e.tensor_tensor(low[:], w[:], high[:].bitcast(F32), ALU.subtract).then_inc(ws_ok, 1)

                def values(m, h):
                    e.wait_ge(v_in, m * 16 + 16)
                    if not isinstance(m, int) or m > 0:
                        e.wait_ge(av_mm, m * NT - NT // 2 * (1 - h))
                    e.sem_inc(started, 1)
                    e.tensor_copy(vp[:, :, h, 0:DH], vraw[:, :, halves[h]]).then_inc(vp_ok, 1)
                    e.wait_ge(vp_ok, m * 4 + 2 * h + 1)
                    e.tensor_tensor(vp[:, :, h, DH:128], vraw[:, :, halves[h]], vp[:, :, h, 0:DH].bitcast(F32), ALU.subtract).then_inc(vp_ok, 1)
                    e.wait_ge(vp_ok, m * 4 + 2 * h + 2)
                    e.sem_inc(started, 1)

                def pair(m, last):
                    e.wait_ge(kf_ok, m + 1)
                    e.sem_inc(started, 1)
                    e.tensor_copy(kh[halves[1], 1], kf[halves[1]]).then_inc(k1_ok, 1)
                    e.wait_ge(k1_ok, m * 4 + 1)
                    for h in (1, 0):
                        e.tensor_tensor(kl[halves[h], 1], kf[halves[1]], kh[halves[1], 1].bitcast(F32), ALU.subtract).then_inc(k1_ok, 1)
                        e.wait_ge(k1_ok, m * 4 + 3 - h)
                    e.sem_inc(started, 1)
                    e.tensor_copy(kh[halves[0], 1], kf[halves[1]]).then_inc(k1_ok, 1)
                    e.wait_ge(k1_ok, m * 4 + 4)
                    values(m, 1)
                    if not last:
                        weights(m + 1)
                        values(m + 1, 0)

                e.memset(zeros[:], 0.0).then_inc(z_ok, 1)
                e.tensor_copy(twice[0:DH], g.ident[0:DH, 0:DH]).then_inc(tw_ok, 1)
                e.wait_ge(tw_ok, 1)
                e.tensor_copy(twice[DH:128], g.ident[DH:128, DH:128]).then_inc(tw_ok, 1)
                e.wait_ge(tw_ok, 2)
                values(0, 0)
                over_pairs(e, pair)

            @block.tensor
            def _(e):
                def linear(high, low, slot, free=None):
                    for b in range(3):
                        if free is not None:
                            e.wait_ge(at_v, free + b + 1)
                        for k in range(KT):
                            cols = slice(b * CS, b * CS + CW)
                            for w, x in ((high, g.nTh), (high, g.nTl), (low, g.nTh)):
                                ins = e.matmul(S[:, slot, b, 0:CW], w[:, k], x[:, k, cols], start=(k == 0 and w is high and x is g.nTh),
                                               stop=(k == KT - 1 and w is low))
                    return ins

                def scores(u, free=None):
                    h = u // NT
                    q = qq[:, h, u % NT * T:(u % NT + 1) * T]
                    for b in range(3):
                        if free is not None:
                            e.wait_ge(at_v, free + b + 1)
                        cols = slice(b * CS, b * CS + CW)
                        e.matmul(S[0:T, u % 2, b, 0:CW], q, kh[:, h, cols], start=True, stop=False)
                        ins = e.matmul(S[0:T, u % 2, b, 0:CW], q, kl[:, h, cols], start=False, stop=True)
                    ins.then_inc(s_mm, 1)

                def values(m, gr, part):
                    h, p = gr // (NT // 2), gr % 2
                    x = (ph, pl)[part]
                    if part == 0:
                        e.wait_ge(at_v, 3 * (m * STEPS + 2 * gr + 2))
                        e.wait_ge(vp_ok, m * 4 + 2 * h + 2)
                        e.wait_ge(ot_ok, m * NT + gr)
                    for t in range(NT):
                        ins = e.matmul(O[:, 0, 0:PW], vp[:, t, h], x[:, p, t], start=(part == 0 and t == 0),
                                       stop=(part == 1 and t == NT - 1))
                    if part == 1:
                        ins.then_inc(av_mm, 1)

                def finals(m, gr):
                    e.wait_ge(ot_ok, m * NT + gr + 1)
                    e.wait_ge(ao_ok, m * STEPS + 2 * gr)
                    for c in range(2):
                        ins = e.matmul(O[0:T, 1, c * DH:(c + 1) * DH], ot[:, gr % 2, c * T:(c + 1) * T], twice[:], start=True, stop=True)
                    ins.then_inc(f_mm, 1)

                def pair(m, last):
                    e.wait_ge(qs_ok, 4 * m + 4)
                    e.wait_ge(k0v_ok, 3 * m + 3)
                    e.wait_ge(k0a_ok, m + 1)
                    scores(0)
                    scores(1)
                    for u in range(STEPS):
                        for b in range(3):
                            e.wait_ge(exp_ok, 3 * (m * STEPS + u) + b + 1)
                            for t in range(*BANK[b]):
                                c = t - BANK[b][0]
                                ins = e.transpose(S[0:T, u % 2, b, c * T:(c + 1) * T], A[:, u % 2, t * T:(t + 1) * T], g.ident[0:T, 0:T])
                            ins.then_inc(tt_mm, 1)
                        if u >= 2:
                            values(m, u // 2 - 1, u % 2)
                        if u >= 4 and u % 2 == 0:
                            finals(m, u // 2 - 2)
                        free = 3 * (m * STEPS + u)
                        if u + 2 == NT:
                            e.wait_ge(k1_ok, 4 * m + 4)
                        if u + 2 < STEPS:
                            scores(u + 2, free)
                        elif not last:
                            high, low, done, c = ((wqh, wql, q_mm, 2), (wkh, wkl, k_mm, 4))[u + 2 - STEPS]
                            e.wait_ge(ws_ok, 4 * (m + 1) + c)
                            linear(high, low, u % 2, free).then_inc(done, 1)
                    for part in range(2):
                        values(m, NT - 1, part)
                    for gr in (NT - 2, NT - 1):
                        finals(m, gr)

                e.wait_ge(tw_ok, 2)
                e.wait_ge(pad_ok, 4)
                e.wait_ge(ws_ok, 4)
                linear(wqh, wql, 0).then_inc(q_mm, 1)
                linear(wkh, wkl, 1).then_inc(k_mm, 1)
                over_pairs(e, pair)

            @block.scalar
            def _(e):
                def wide(out, slot, rows, fn, **kw):
                    e.activation(out[:, 0:3 * CS].rearrange("p (b n) -> p b n", b=3), S[rows, slot, :, 0:CS], fn, **kw)
                    return e.activation(out[:, 3 * CS:N], S[rows, slot, 2, CS:CW], fn, **kw)

                def queries(m):
                    e.wait_ge(q_mm, m + 1)
                    e.wait_ge(k1_ok, 4 * m)
                    e.wait_ge(k0v_ok, 3 * m)
                    wide(qf, 0, slice(0, 128), ACT.Identity, bias=qb[:, bass.ds(m, 1)], scale=DH ** -0.5).then_inc(qf_ok, 1)

                def keys(m):
                    e.wait_ge(k_mm, m + 1)
                    e.wait_ge(qs_ok, 4 * m + 4)
                    wide(kf, 1, slice(0, 128), ACT.Identity, bias=kb[:, bass.ds(m, 1)]).then_inc(kf_ok, 1)
                    e.wait_ge(kf_ok, m + 1)
                    e.activation(kh[halves[1], 0], kf[halves[0]], ACT.Copy).then_inc(k0a_ok, 1)

                def pair(m, last):
                    for s in range(STEPS + 1):
                        u = s - 1
                        if u >= 0:
                            if u % 2 == 0:
                                e.wait_ge(av_mm, m * NT + max(u // 2 - 1, 0))
                            for b in range(3):
                                e.wait_ge(tt_mm, 3 * (m * STEPS + u) + b + 1)
                                e.activation(*turned(ph, u, b), ACT.Copy).then_inc(at_a, 1)
                        if s < STEPS:
                            e.wait_ge(max_ok, m * STEPS + s + 1)
                            e.wait_ge(tt_mm, 3 * (m * STEPS + max(s - 1, 0)))
                            e.wait_ge(rc_ok, m * STEPS + max(s - 3, 0))
                            for b in range(3):
                                n = CW if b == 2 else CS
                                e.activation(A[:, s % 2, b * CS:b * CS + n], S[0:T, s % 2, b, 0:n], ACT.Exp,
                                             bias=nmax[:, s % 2:s % 2 + 1], accum_out=part[:, s % SLOTS, b:b + 1]).then_inc(exp_ok, 1)
                        if s == STEPS - 1 and not last:
                            queries(m + 1)
                    if not last:
                        keys(m + 1)

                for into, high, raw in ((qw_in, wqh, qw), (kw_in, wkh, kw)):
                    e.wait_ge(into, 16)
                    e.activation(high[:], raw[:], ACT.Copy).then_inc(w0_ok, 1)
                e.wait_ge(qb_ok, 1)
                queries(0)
                keys(0)
                over_pairs(e, pair)

            @block.vector
            def _(e):
                def queries(m):
                    e.wait_ge(qf_ok, m + 1)
                    for h in range(2):
                        e.tensor_copy(qq[halves[h], h], qf[halves[h]]).then_inc(qs_ok, 1)
                    e.wait_ge(qs_ok, 4 * m + 2)
                    for h in range(2):
                        e.tensor_tensor(qq[halves[1 - h], h], qf[halves[h]], qq[halves[h], h].bitcast(F32), ALU.subtract).then_inc(qs_ok, 1)

                def keys(m):
                    e.wait_ge(kf_ok, m + 1)
                    e.tensor_copy(kh[halves[0], 0], kf[halves[0]]).then_inc(k0v_ok, 1)
                    e.wait_ge(k0v_ok, 3 * m + 1)
                    for h in range(2):
                        e.tensor_tensor(kl[halves[h], 0], kf[halves[0]], kh[halves[0], 0].bitcast(F32), ALU.subtract).then_inc(k0v_ok, 1)

                def pair(m, last):
                    for s in range(STEPS + 4):
                        if s < STEPS:
                            e.wait_ge(s_mm, m * STEPS + s + 1)
                            e.tensor_reduce(nmax[:, s % 2:s % 2 + 1], S[0:T, s % 2, :, 0:CW], AX.XY, ALU.max,
                                            negate=True).then_inc(max_ok, 1)
                        u = s - 1
                        if 0 <= u < STEPS:
                            for b in range(3):
                                e.wait_ge(at_a, 3 * (m * STEPS + u) + b + 1)
                                out, transposed = turned(pl, u, b)
                                e.tensor_tensor(out, transposed, turned(ph, u, b)[0].bitcast(F32), ALU.subtract).then_inc(at_v, 1)
                            c = u % SLOTS
                            e.wait_ge(exp_ok, 3 * (m * STEPS + u) + 3)
                            e.tensor_reduce(sums[:, c:c + 1], part[:, c], AX.X, ALU.add).then_inc(sums_ok, 1)
                            e.wait_ge(sums_ok, m * STEPS + u + 1)
                            e.reciprocal(rc[:, c:c + 1], sums[:, c:c + 1]).then_inc(rc_ok, 1)
                        if s == STEPS and not last:
                            queries(m + 1)
                        if s == STEPS + 1 and not last:
                            keys(m + 1)
                        if s % 2 == 0 and s >= 4:
                            gr = s // 2 - 2
                            e.wait_ge(av_mm, m * NT + gr + 1)
                            e.tensor_copy(ot[:, gr % 2, 0:2 * T], O[:, 0, 0:2 * T]).then_inc(ot_ok, 1)
                        if s % 2 == 1 and s >= 5:
                            gr = s // 2 - 2
                            e.wait_ge(f_mm, m * NT + gr + 1)
                            for c in range(2):
                                u = 2 * gr + c
                                e.wait_ge(rc_ok, m * STEPS + u + 1)
                                e.tensor_scalar(g.ao[:, u % NT, bass.ds(m * 128 + u // NT * DH, DH)], O[0:T, 1, c * DH:(c + 1) * DH],
                                                rc[:, u % SLOTS:u % SLOTS + 1], None, ALU.mult).then_inc(ao_ok, 1)


                e.wait_ge(b_in, 32)
                for i, (high, raw, low) in enumerate(((wqh, qw, wql), (wkh, kw, wkl))):
                    e.wait_ge(w0_ok, i + 1)
                    e.tensor_tensor(low[:], raw[:], high[:].bitcast(F32), ALU.subtract).then_inc(ws_ok, 2)
                e.wait_ge(z_ok, 1)
                for x in (ph, pl):
                    for p in range(2):
                        e.tensor_copy(x[:, p, :, 2 * T:PW], zeros[:].unsqueeze(1).to_broadcast([T, NT, PW - 2 * T])).then_inc(pad_ok, 1)
                e.tensor_scalar(qb[:], qb[:], DH ** -0.5, None, ALU.mult).then_inc(qb_ok, 1)
                queries(0)
                keys(0)
                over_pairs(e, pair)


def tail(nc, g):
    def over_tiles(e, pair):
        pair(0)
        with e.Fori(1, NT // 2 - 1) as i:
            pair(i)
        pair(NT // 2 - 1)

    inside = lambda n, least=0: not isinstance(n, int) or least <= n < NT
    with ExitStack() as ctx:
        sb = lambda n, s, d=F32: ctx.enter_context(nc.sbuf_tensor("ta_" + n, s, d))
        ps = lambda n, s: ctx.enter_context(nc.psum_tensor("ta_" + n, s, F32))
        sem = lambda n: g.sem("ta_" + n)
        wo, wu, wd = sb("wo", [128, KT, D]), sb("wu", [128, KT, FF]), sb("wd", [128, FJ, D])
        woh, wol = sb("woh", [128, KT, D], F32R), sb("wol", [128, KT, D], F32R)
        wdh, wdl = sb("wdh", [128, FJ, D], F32R), sb("wdl", [128, FJ, D], F32R)
        x2 = sb("x2", [T, NT, D])
        bo, bd = sb("bo", [T, D]), sb("bd", [T, D])
        gain, shift, bu = sb("gain", [128, KT]), sb("shift", [128, KT]), sb("bu", [128, FJ])
        stats, mv = sb("stats", [T, NT, 12]), sb("mv", [T, NT, 2])
        veps, std, rstd, tmp = (sb(n, [T, NT]) for n in ("veps", "std", "rstd", "tmp"))
        sh, sl = sb("sh", [128, 2, KT, T], F32R), sb("sl", [128, 2, KT, T], F32R)
        stage = sb("stage", [128, 2, KT, T])
        z, xt, res = sb("z", [T, 2, D]), sb("xt", [T, 2, D]), sb("res", [T, 2, D])
        uT = sb("uT", [128, 2, FJ, T])
        uh, ul = sb("uh", [128, 2, FJ, T], F32R), sb("ul", [128, 2, FJ, T], F32R)
        TR, O = ps("TR", [128, 2, 2, 512]), ps("O", [128, 2, 2, 512])
        y_in = [sem("y_in0"), sem("y_in1")]
        wo_in, w_in, b_in = [sem("wo_in0"), sem("wo_in1")], sem("w_in"), sem("b_in")
        in_, sent = [sem("in0"), sem("in1")], [sem("sent0"), sem("sent1")]
        woh_ok, wol_ok, wdh_ok, wdl_ok, uh_ok, ul_ok, lo_ok, stats_ok, started = (
            sem(n) for n in ("woh_ok", "wol_ok", "wdh_ok", "wdl_ok", "uh_ok", "ul_ok", "lo_ok", "stats_ok", "started"))
        tr_mm, st_ok, mm, add_ok, x2_ok, dve, var_ok, std_ok = (
            sem(n) for n in ("tr_mm", "st_ok", "mm", "add_ok", "x2_ok", "dve", "var_ok", "std_ok"))
        z_ok, zt_mm, zs_ok, up_mm, u_ok, dn_mm, xt_ok, res_ok = (
            sem(n) for n in ("z_ok", "zt_mm", "zs_ok", "up_mm", "u_ok", "dn_mm", "xt_ok", "res_ok"))
        split = lambda x: x.rearrange("p (c n) -> p c n", c=2)
        staged = lambda x: x.rearrange("p (c k) t -> p c (k t)", c=2)

        with nc.Block() as block:
            @block.sync
            def _(sp):
                for c in range(2):
                    ks = slice(c * KT // 2, (c + 1) * KT // 2)
                    sp.dma_start(wo[:, ks], weight_view(g.ffn_ao_w)[:, ks]).then_inc(wo_in[c], 16)
                for c in range(2):
                    ts = slice(c * NT // 2, (c + 1) * NT // 2)
                    sp.dma_start(x2[:, ts], node_view(g.y_dram)[:, ts]).then_inc(y_in[c], 16)
                    if c == 0:
                        sp.dma_start(bo[:], g.ffn_ao_b.partition_broadcast(T)).then_inc(b_in, 16)
                sp.dma_start(wd[:], weight_view(g.ffn_down_w)).then_inc(w_in, 16)
                sp.dma_start(wu[:], weight_view(g.ffn_up_w)).then_inc(w_in, 16)
                sp.dma_start(bd[:], g.ffn_down_b.partition_broadcast(T)).then_inc(b_in, 16)
                for dst, v in ((gain, g.ffn_n2_g), (shift, g.ffn_n2_b), (bu, g.ffn_up_b)):
                    sp.dma_start(dst[:], v.rearrange("(k p) -> p k", p=128), allow_slow_non_contiguous=True).then_inc(b_in, 16)
                for p in range(2):
                    sp.dma_start(xt[:, p], g.xj[p * T:(p + 1) * T, :]).then_inc(in_[p], 16)
                with sp.Fori(0, NT // 2 - 1) as i:
                    for p in range(2):
                        n = i * 2 + p
                        sp.wait_ge(res_ok, n + 1)
                        sp.dma_start(g.out[bass.ds(n * T, T), :], res[:, p]).then_inc(sent[p], 16)
                        sp.dma_start(xt[:, p], g.xj[bass.ds((n + 2) * T, T), :]).then_inc(in_[p], 16)
                for n in range(NT - 2, NT):
                    sp.wait_ge(res_ok, n + 1)
                    sp.dma_start(g.out[n * T:(n + 1) * T, :], res[:, n % 2]).then_inc(sent[n % 2], 16)
                for s in sent:
                    sp.wait_ge(s, 16 * NT // 2)

            @block.gpsimd
            def _(e):
                def pair(i):
                    for p in range(2):
                        n = i * 2 + p
                        e.wait_ge(u_ok, n + 1)
                        if inside(n - 2):
                            e.wait_ge(dn_mm, n - 1)
                        e.sem_inc(started, 1)
                        e.tensor_copy(uh[:, p], uT[:, p]).then_inc(uh_ok, 1)
                        e.wait_ge(uh_ok, n + 1)
                        e.sem_inc(started, 1)
                        e.tensor_tensor(ul[:, p], uT[:, p], uh[:, p].bitcast(F32), ALU.subtract).then_inc(ul_ok, 1)

                over_tiles(e, pair)

            @block.tensor
            def _(e):
                for n in range(NT + 1):
                    if n < NT:
                        if n >= 2:
                            e.wait_ge(lo_ok, n - 1)
                        for k in range(KT):
                            ins = e.transpose(TR[:, n % 2, k // 3, k % 3 * T:(k % 3 + 1) * T],
                                              g.ao[:, n, k * 128:(k + 1) * 128], g.ident[0:T, 0:T])
                        ins.then_inc(tr_mm, 1)
                    u = n - 1
                    if u >= 0:
                        e.wait_ge(lo_ok, u + 1)
                        if u >= 2:
                            e.wait_ge(add_ok, u - 1)
                        for k in range(KT):
                            if u == 0:
                                e.wait_ge(wol_ok, k + 1)
                            for c in range(2):
                                for x, w in ((sh, woh), (sh, wol), (sl, woh)):
                                    ins = e.matmul(O[0:T, u % 2, c, 0:HALF], x[:, u % 2, k], w[:, k, c * HALF:(c + 1) * HALF],
                                                   start=(k == 0 and x is sh and w is woh), stop=(k == KT - 1 and x is sl))
                        ins.then_inc(mm, 1)
                e.wait_ge(w_in, 32)
                e.wait_ge(add_ok, NT)
                e.wait_ge(wdl_ok, FJ)

                def turn(n, p):
                    e.wait_ge(z_ok, n + 1)
                    for k in range(KT):
                        ins = e.transpose(TR[:, 0, k // 3, k % 3 * T:(k % 3 + 1) * T], z[:, p, k * 128:(k + 1) * 128],
                                          g.ident[0:T, 0:T])
                    ins.then_inc(zt_mm, 1)

                def down(n, p):
                    e.wait_ge(ul_ok, n + 1)
                    if inside(n - 2):
                        e.wait_ge(res_ok, n - 1)
                    for c in range(2):
                        for j in range(FJ):
                            for x, w in ((uh, wdh), (uh, wdl), (ul, wdh)):
                                ins = e.matmul(O[0:T, p, c, 0:HALF], x[:, p, j], w[:, j, c * HALF:(c + 1) * HALF],
                                               start=(j == 0 and x is uh and w is wdh), stop=(j == FJ - 1 and x is ul))
                    ins.then_inc(dn_mm, 1)

                def pair(i):
                    for p in range(2):
                        n = i * 2 + p
                        e.wait_ge(zs_ok, n + 1)
                        if inside(n + 1):
                            turn(n + 1, 1 - p)
                        if inside(n - 2):
                            e.wait_ge(u_ok, n - 1)
                        for j in range(FJ):
                            for k in range(KT):
                                ins = e.matmul(TR[:, 1, p, j * T:(j + 1) * T], wu[:, k, j * 128:(j + 1) * 128], stage[:, p, k],
                                               start=(k == 0), stop=(k == KT - 1))
                        ins.then_inc(up_mm, 1)
                        if inside(n - 1):
                            down(n - 1, 1 - p)

                turn(0, 0)
                over_tiles(e, pair)
                down(NT - 1, 1)

            @block.scalar
            def _(e):
                def high(n):
                    e.wait_ge(tr_mm, n + 1)
                    if n >= 2:
                        e.wait_ge(mm, n - 1)
                    e.activation(staged(sh[:, n % 2]), TR[:, n % 2, :, 0:3 * T], ACT.Copy).then_inc(st_ok, 1)

                high(0)
                for k in range(KT):
                    e.wait_ge(wo_in[k // 3], 16)
                    e.activation(woh[:, k], wo[:, k], ACT.Copy).then_inc(woh_ok, 1)
                for n in range(1, NT):
                    high(n)
                    if n == 3:
                        e.wait_ge(w_in, 32)
                        e.activation(wdh[:], wd[:], ACT.Copy).then_inc(wdh_ok, 1)
                e.wait_ge(var_ok, 1)
                e.activation(std[:], veps[:], ACT.Sqrt).then_inc(std_ok, 1)
                e.wait_ge(b_in, 80)

                def affine(n, p):
                    e.wait_ge(zt_mm, n + 1)
                    if inside(n - 2):
                        e.wait_ge(up_mm, n - 1)
                    for k in range(KT):
                        ins = e.activation(stage[:, p, k], TR[:, 0, k // 3, k % 3 * T:(k % 3 + 1) * T], ACT.Identity,
                                           bias=shift[:, k:k + 1], scale=gain[:, k:k + 1])
                    ins.then_inc(zs_ok, 1)

                def pair(i):
                    for p in range(2):
                        n = i * 2 + p
                        if inside(n + 1):
                            affine(n + 1, 1 - p)
                        e.wait_ge(up_mm, n + 1)
                        if inside(n - 2):
                            e.wait_ge(ul_ok, n - 1)
                        for j in range(FJ):
                            ins = e.activation(uT[:, p, j], TR[:, 1, p, j * T:(j + 1) * T], ACT.Gelu, bias=bu[:, j:j + 1])
                        ins.then_inc(u_ok, 1)

                affine(0, 0)
                over_tiles(e, pair)

            @block.vector
            def _(e):
                seq = Tally(e, dve)

                def low(n):
                    e.wait_ge(st_ok, n + 1)
                    e.tensor_tensor(staged(sl[:, n % 2]), TR[:, n % 2, :, 0:3 * T], staged(sh[:, n % 2]).bitcast(F32),
                                    ALU.subtract).then_inc(lo_ok, 1)

                low(0)
                for k in range(KT):
                    e.wait_ge(woh_ok, k + 1)
                    e.tensor_tensor(wol[:, k], wo[:, k], woh[:, k].bitcast(F32), ALU.subtract).then_inc(wol_ok, 1)
                low(1)
                e.wait_ge(b_in, 80)
                for n in range(NT):
                    p = n % 2
                    if n + 2 < NT:
                        low(n + 2)
                    if n % 5 == 0:
                        e.wait_ge(y_in[n // 5], 16)
                    e.wait_ge(mm, n + 1)
                    e.tensor_tensor(split(z[:, p]), O[0:T, p, :, 0:HALF], split(bo[:]), ALU.add).then_inc(add_ok, 1)
                    e.wait_ge(add_ok, n + 1)
                    e.tensor_tensor(x2[:, n, :], x2[:, n, :], z[:, p], ALU.add).then_inc(x2_ok, 1)
                    e.wait_ge(x2_ok, n + 1)
                    for c in range(2):
                        e.bn_stats(stats[:, n, 6 * c:6 * c + 6], x2[:, n, c * HALF:(c + 1) * HALF]).then_inc(stats_ok, 1)
                    if n == 4:
                        e.wait_ge(wdh_ok, 1)
                        for j in range(FJ):
                            e.tensor_tensor(wdl[:, j], wd[:, j], wdh[:, j].bitcast(F32), ALU.subtract).then_inc(wdl_ok, 1)
                e.wait_ge(stats_ok, 2 * NT)
                for t in range(NT):
                    seq.mark(e.bn_aggr(mv[:, t, :], stats[:, t, :]))
                seq.settle()
                e.tensor_scalar(veps[:], mv[:, :, 1], LN_EPS, None, ALU.add).then_inc(var_ok, 1)
                e.wait_ge(std_ok, 1)
                newton_rstd(e, seq, rstd[:], std[:], veps[:], tmp[:])

                def centre(n, p):
                    if inside(n - 2):
                        e.wait_ge(zt_mm, n - 1)
                    e.tensor_scalar(z[:, p], x2[:, n, :], mv[:, n, 0:1], rstd[:, bass.ds(n, 1)],
                                    ALU.subtract, ALU.mult).then_inc(z_ok, 1)

                def residual(i, n, p):
                    e.wait_ge(in_[p], i * 16 + 16)
                    e.tensor_tensor(xt[:, p], xt[:, p], x2[:, n, :], ALU.add).then_inc(xt_ok, 1)
                    e.wait_ge(xt_ok, 2 * n + 1)
                    e.tensor_tensor(xt[:, p], xt[:, p], bd[:], ALU.add).then_inc(xt_ok, 1)

                def finish(i, n, p):
                    e.wait_ge(dn_mm, n + 1)
                    e.wait_ge(xt_ok, 2 * n + 2)
                    if inside(n - 2):
                        e.wait_ge(sent[p], i * 16)
                    e.tensor_tensor(split(res[:, p]), O[0:T, p, :, 0:HALF], split(xt[:, p]), ALU.add).then_inc(res_ok, 1)

                def pair(i):
                    for p in range(2):
                        n = i * 2 + p
                        if inside(n + 1):
                            centre(n + 1, 1 - p)
                        residual(i, n, p)
                        if inside(n - 1):
                            finish(i - 1 + p, n - 1, 1 - p)

                centre(0, 0)
                over_tiles(e, pair)
                finish(NT // 2 - 1, NT - 1, 1)


def graph_transformer_layer(
    nc: bass.Bass,
    x: bass.AP,
    src: bass.AP,
    dst: bass.AP,
    gnn_W_ah: bass.AP,
    gnn_b_ah: bass.AP,
    gnn_W0: bass.AP,
    gnn_a_src0: bass.AP,
    gnn_a_dst0: bass.AP,
    gnn_b0: bass.AP,
    gnn_W1: bass.AP,
    gnn_a_src1: bass.AP,
    gnn_a_dst1: bass.AP,
    gnn_b1: bass.AP,
    gnn_W2: bass.AP,
    gnn_a_src2: bass.AP,
    gnn_a_dst2: bass.AP,
    gnn_b2: bass.AP,
    gnn_W_out: bass.AP,
    gnn_b_out: bass.AP,
    mix_Wq: bass.AP,
    mix_Wk: bass.AP,
    mix_Wv: bass.AP,
    mix_Wo: bass.AP,
    mix_proj: bass.AP,
    ffn_q_w: bass.AP,
    ffn_q_b: bass.AP,
    ffn_k_w: bass.AP,
    ffn_k_b: bass.AP,
    ffn_ao_w: bass.AP,
    ffn_ao_b: bass.AP,
    ffn_recipe: bass.AP,
    ffn_ctx_pat: bass.AP,
    ffn_basis_emb: bass.AP,
    ffn_basis_A: bass.AP,
    ffn_vout_w: bass.AP,
    ffn_vout_b: bass.AP,
    ffn_up_w: bass.AP,
    ffn_up_b: bass.AP,
    ffn_down_w: bass.AP,
    ffn_down_b: bass.AP,
    ffn_n1_g: bass.AP,
    ffn_n1_b: bass.AP,
    ffn_n2_g: bass.AP,
    ffn_n2_b: bass.AP,
    out: bass.AP,
):
    g = Env()
    g.x = x
    g.src = src
    g.dst = dst
    g.gnn_W_ah = gnn_W_ah
    g.gnn_b_ah = gnn_b_ah
    g.gnn_W0 = gnn_W0
    g.gnn_a_src0 = gnn_a_src0
    g.gnn_a_dst0 = gnn_a_dst0
    g.gnn_b0 = gnn_b0
    g.gnn_W1 = gnn_W1
    g.gnn_a_src1 = gnn_a_src1
    g.gnn_a_dst1 = gnn_a_dst1
    g.gnn_b1 = gnn_b1
    g.gnn_W2 = gnn_W2
    g.gnn_a_src2 = gnn_a_src2
    g.gnn_a_dst2 = gnn_a_dst2
    g.gnn_b2 = gnn_b2
    g.gnn_W_out = gnn_W_out
    g.gnn_b_out = gnn_b_out
    g.mix_Wq = mix_Wq
    g.mix_Wk = mix_Wk
    g.mix_Wv = mix_Wv
    g.mix_Wo = mix_Wo
    g.mix_proj = mix_proj
    g.ffn_q_w = ffn_q_w
    g.ffn_q_b = ffn_q_b
    g.ffn_k_w = ffn_k_w
    g.ffn_k_b = ffn_k_b
    g.ffn_ao_w = ffn_ao_w
    g.ffn_ao_b = ffn_ao_b
    g.ffn_recipe = ffn_recipe
    g.ffn_ctx_pat = ffn_ctx_pat
    g.ffn_basis_emb = ffn_basis_emb
    g.ffn_basis_A = ffn_basis_A
    g.ffn_vout_w = ffn_vout_w
    g.ffn_vout_b = ffn_vout_b
    g.ffn_up_w = ffn_up_w
    g.ffn_up_b = ffn_up_b
    g.ffn_down_w = ffn_down_w
    g.ffn_down_b = ffn_down_b
    g.ffn_n1_g = ffn_n1_g
    g.ffn_n1_b = ffn_n1_b
    g.ffn_n2_g = ffn_n2_g
    g.ffn_n2_b = ffn_n2_b
    g.out = out
    g.TABLE_ZERO = 16 * (NT // 2 + 1)
    scratch = lambda n, s: nc.dram_tensor(n, s, F32, kind="Internal").ap()
    g.table = scratch("edge_table", (CELLS + T, 1))
    g.mix_out = scratch("mixer_out", (N, D))
    g.rows, g.uv = scratch("score_rows", (2 * GI, N)), scratch("score_uv", (2 * GI, N))
    g.h = scratch("gnn_h", (GI, N, GC))
    g.node = scratch("gnn_nodes", (N, GL * D))
    g.xj, g.y_dram, g.v_dram = (scratch(n, (N, D)) for n in ("residual", "normed_residual", "values"))
    g.sem = lambda n: nc.alloc_semaphore(name=n)
    keep = lambda scope, n, s, d=F32: scope.enter_context(nc.sbuf_tensor(n, s, d))
    with ExitStack() as whole:
        g.ident = keep(whole, "ident", [128, 128])
        with nc.cleanup_on_exit(), ExitStack() as gnn:
            g.table_sem, g.scattered = g.sem("table_zeroed"), g.sem("scattered")
            g.asad, g.as02 = keep(gnn, "asad", [T, NT, 2 * GI]), keep(gnn, "as02", [T, NT, GI])
            with ExitStack() as first:
                g.edge_add, g.edge_cell = keep(first, "edge_add", [T, EB]), keep(first, "edge_cell", [T, EB], I32)
                with ExitStack() as values:
                    g.xnT = keep(values, "xnT", [128, KT, N])
                    g.v = keep(values, "mix_v", [T, NT, MH * (DH + 1)])
                    front(nc, g)
                    mix(nc, g, range(EB))
                lift(nc, g)
            graph(nc, g)
        with nc.cleanup_on_exit(), ExitStack() as ffn:
            g.y = g.ao = keep(ffn, "y", [T, NT, D])
            g.stats = keep(ffn, "stats", [T, NT, 12])
            join(nc, g)
            with ExitStack() as attention:
                g.nTh, g.nTl = keep(attention, "normed_high", [128, KT, N], F32R), keep(attention, "normed_low", [128, KT, N], F32R)
                route(nc, g)
                attend(nc, g)
            tail(nc, g)


_INS = ['x', 'src', 'dst', 'L0_gnn_W_ah', 'L0_gnn_b_ah', 'L0_gnn_W0', 'L0_gnn_a_src0', 'L0_gnn_a_dst0', 'L0_gnn_b0', 'L0_gnn_W1', 'L0_gnn_a_src1', 'L0_gnn_a_dst1', 'L0_gnn_b1', 'L0_gnn_W2', 'L0_gnn_a_src2', 'L0_gnn_a_dst2', 'L0_gnn_b2', 'L0_gnn_W_out', 'L0_gnn_b_out', 'L0_mix_Wq', 'L0_mix_Wk', 'L0_mix_Wv', 'L0_mix_Wo', 'L0_mix_proj', 'L0_ffn_q_w', 'L0_ffn_q_b', 'L0_ffn_k_w', 'L0_ffn_k_b', 'L0_ffn_ao_w', 'L0_ffn_ao_b', 'L0_ffn_recipe', 'L0_ffn_ctx_pat', 'L0_ffn_basis_emb', 'L0_ffn_basis_A', 'L0_ffn_vout_w', 'L0_ffn_vout_b', 'L0_ffn_up_w', 'L0_ffn_up_b', 'L0_ffn_down_w', 'L0_ffn_down_b', 'L0_ffn_n1_g', 'L0_ffn_n1_b', 'L0_ffn_n2_g', 'L0_ffn_n2_b']


def kernel(**inputs):
    import numpy as _np
    import concourse.bacc as _bacc
    from concourse import mybir as _mybir
    from concourse.bass_utils import run_bass_kernel_spmd as _run

    nc = _bacc.Bacc("TRN2", target_bir_lowering=False, num_devices=1)
    arrays, args = {}, []
    for name in _INS:
        a = _np.ascontiguousarray(inputs[name])
        arrays[f"in_{name}_dram"] = a
        args.append(nc.dram_tensor(f"in_{name}_dram", a.shape, _mybir.dt.from_np(a.dtype), kind="ExternalInput").ap())
    args.append(nc.dram_tensor("out_0_dram", (1250, 768), _mybir.dt.float32, kind="ExternalOutput").ap())
    graph_transformer_layer(nc, *args)
    r = _run(nc, [arrays], core_ids=[0])
    return r.results[0]["out_0_dram"]
```
